# Optimizing a Trainium2 kernel written in Bass

```python
import numpy as np
import jax
import jax.numpy as jnp

def _softmax(x, axis=-1):
    return jax.nn.softmax(x, axis=axis)

def _gelu(x):
    return jax.nn.gelu(x, approximate=True)

def _silu(x):
    return jax.nn.silu(x)

def _sigmoid(x):
    return jax.nn.sigmoid(x)

def _layernorm(x, axis=-1, eps=1e-05):
    m = jnp.mean(x, axis=axis, keepdims=True)
    v = jnp.var(x, axis=axis, keepdims=True)
    return (x - m) / jnp.sqrt(v + eps)

def _scatter_add(tgt, idx, src, axis=0):
    return tgt.at[idx].add(src)

def _segment_sum(src, seg, n):
    return jax.ops.segment_sum(src, seg, n)
kernel_name = 'mk_macaron_d1_jaxref_r4_a5d58d'

def setup_inputs(seed: int=0):
    np.random.seed(seed)
    _w = jnp.asarray

    def _L0_attn_setup():
        import jax, jax.numpy as jnp
        import numpy as np
        D_MODEL = 256
        NUM_HEADS = 16
        HEAD_DIM = D_MODEL // NUM_HEADS
        MAX_SEQ_LEN = 512

        def _rope_tables(seq_len, head_dim):
            inv_freq = 1.0 / 10000.0 ** (jnp.arange(0, head_dim, 2, dtype=jnp.float32) / head_dim)
            pos = jnp.arange(seq_len, dtype=jnp.float32)
            freqs = jnp.einsum('i,j->ij', pos, inv_freq)
            return (jnp.cos(freqs), jnp.sin(freqs))

        def _apply_rope(x, cos_half, sin_half):
            x_even = x[..., ::2]
            x_odd = x[..., 1::2]
            rot_even = x_even * cos_half - x_odd * sin_half
            rot_odd = x_even * sin_half + x_odd * cos_half
            return jnp.stack([rot_even, rot_odd], axis=-1).reshape(x.shape)
        key = jax.random.key(seed)
        ks = jax.random.split(key, 9)
        B, S = (2, 512)
        glorot = lambda k: jax.random.normal(k, (D_MODEL, D_MODEL), dtype=jnp.float32) * (1.0 / np.sqrt(D_MODEL))
        return {'x': jax.random.normal(ks[0], (B, S, D_MODEL), dtype=jnp.float32), 'wq': glorot(ks[1]), 'bq': jnp.zeros((D_MODEL,), jnp.float32), 'wk': glorot(ks[2]), 'bk': jnp.zeros((D_MODEL,), jnp.float32), 'wv': glorot(ks[3]), 'bv': jnp.zeros((D_MODEL,), jnp.float32), 'wo': glorot(ks[4]), 'bo': jnp.zeros((D_MODEL,), jnp.float32)}
    _L0_attn_in = _L0_attn_setup()

    def _L0_ffn_setup():
        import jax, jax.numpy as jnp
        import numpy as np
        NUM_EXPERTS = 8
        TOP_K = 2
        CAPACITY_FACTOR = 1.0

        def _dispatch_compute(xf, top_expert, w1, w2, capacity):
            tokens, hs = xf.shape
            tpe = jnp.bincount(top_expert, length=NUM_EXPERTS)
            indices = jnp.argsort(top_expert)
            offsets = jnp.concatenate([jnp.zeros((1,), tpe.dtype), jnp.cumsum(tpe)[:-1]])
            slot = jnp.arange(capacity)
            pos = offsets[:, None] + slot[None, :]
            valid = slot[None, :] < tpe[:, None]
            tok_idx = indices[jnp.minimum(pos, tokens - 1)]
            xe = jnp.where(valid[..., None], xf[tok_idx], 0.0)
            h = jax.nn.gelu(jnp.einsum('ech,ehf->ecf', xe, w1), approximate=True)
            ye = jnp.einsum('ecf,efh->ech', h, w2)
            tok_safe = jnp.where(valid, tok_idx, tokens)
            out = jnp.zeros((tokens + 1, hs), xf.dtype).at[tok_safe.reshape(-1)].add(ye.reshape(-1, hs))
            return out[:tokens]
        key = jax.random.key(seed)
        k1, k2, k3, k4 = jax.random.split(key, 4)
        hs, ffn = (256, 1024)
        x = jax.random.normal(k1, (512, 2, hs), dtype=jnp.float32)
        router_w = jax.random.normal(k2, (hs, NUM_EXPERTS), dtype=jnp.float32) * hs ** (-0.5)
        w1 = jax.random.normal(k3, (NUM_EXPERTS, hs, ffn), dtype=jnp.float32) * 0.02
        w2 = jax.random.normal(k4, (NUM_EXPERTS, ffn, hs), dtype=jnp.float32) * 0.02
        bias = jnp.zeros((1, 1, hs), dtype=jnp.float32)
        return {'x': x, 'router_w': router_w, 'w1': w1, 'w2': w2, 'bias': bias}
    _L0_ffn_in = _L0_ffn_setup()
    _d = {'L0_attn_x': _L0_attn_in['x'], 'L0_attn_wq': _L0_attn_in['wq'], 'L0_attn_bq': _L0_attn_in['bq'], 'L0_attn_wk': _L0_attn_in['wk'], 'L0_attn_bk': _L0_attn_in['bk'], 'L0_attn_wv': _L0_attn_in['wv'], 'L0_attn_bv': _L0_attn_in['bv'], 'L0_attn_wo': _L0_attn_in['wo'], 'L0_attn_bo': _L0_attn_in['bo'], 'L0_ffn_router_w': _L0_ffn_in['router_w'], 'L0_ffn_w1': _L0_ffn_in['w1'], 'L0_ffn_w2': _L0_ffn_in['w2'], 'L0_ffn_bias': _L0_ffn_in['bias']}
    _x0 = _d['L0_attn_x']
    _d['L0_attn_x'] = jax.random.normal(jax.random.fold_in(jax.random.key(seed), 1), (4, 1024, 256), dtype=_x0.dtype)
    del _x0
    return _d

def reference(L0_attn_x, L0_attn_wq, L0_attn_bq, L0_attn_wk, L0_attn_bk, L0_attn_wv, L0_attn_bv, L0_attn_wo, L0_attn_bo, L0_ffn_router_w, L0_ffn_w1, L0_ffn_w2, L0_ffn_bias):

    def _L0_attn_ref(x, wq, bq, wk, bk, wv, bv, wo, bo):
        import jax, jax.numpy as jnp
        import numpy as np
        D_MODEL = 256
        NUM_HEADS = 16
        HEAD_DIM = D_MODEL // NUM_HEADS
        MAX_SEQ_LEN = 512

        def _rope_tables(seq_len, head_dim):
            inv_freq = 1.0 / 10000.0 ** (jnp.arange(0, head_dim, 2, dtype=jnp.float32) / head_dim)
            pos = jnp.arange(seq_len, dtype=jnp.float32)
            freqs = jnp.einsum('i,j->ij', pos, inv_freq)
            return (jnp.cos(freqs), jnp.sin(freqs))

        def _apply_rope(x, cos_half, sin_half):
            x_even = x[..., ::2]
            x_odd = x[..., 1::2]
            rot_even = x_even * cos_half - x_odd * sin_half
            rot_odd = x_even * sin_half + x_odd * cos_half
            return jnp.stack([rot_even, rot_odd], axis=-1).reshape(x.shape)
        B, S, _ = x.shape
        q = (x @ wq + bq).reshape(B, S, NUM_HEADS, HEAD_DIM)
        k = (x @ wk + bk).reshape(B, S, NUM_HEADS, HEAD_DIM)
        v = (x @ wv + bv).reshape(B, S, NUM_HEADS, HEAD_DIM)
        cos, sin = _rope_tables(S, HEAD_DIM)
        cos = cos[None, :, None, :]
        sin = sin[None, :, None, :]
        q = _apply_rope(q, cos, sin)
        k = _apply_rope(k, cos, sin)
        q = q.transpose(0, 2, 1, 3)
        k = k.transpose(0, 2, 1, 3)
        v = v.transpose(0, 2, 1, 3)
        scores = jnp.einsum('bhqd,bhkd->bhqk', q, k) / jnp.sqrt(jnp.float32(HEAD_DIM))
        causal = jnp.where(jnp.tril(jnp.ones((S, S), jnp.float32)) == 0, -1000000000.0, 0.0)
        scores = scores + causal
        attn = jax.nn.softmax(scores, axis=-1)
        out = jnp.einsum('bhqk,bhkd->bhqd', attn, v)
        out = out.transpose(0, 2, 1, 3).reshape(B, S, D_MODEL)
        return out @ wo + bo

    def _L0_ffn_ref(x, router_w, w1, w2, bias):
        import jax, jax.numpy as jnp
        import numpy as np
        NUM_EXPERTS = 8
        TOP_K = 2
        CAPACITY_FACTOR = 1.0

        def _dispatch_compute(xf, top_expert, w1, w2, capacity):
            tokens, hs = xf.shape
            tpe = jnp.bincount(top_expert, length=NUM_EXPERTS)
            indices = jnp.argsort(top_expert)
            offsets = jnp.concatenate([jnp.zeros((1,), tpe.dtype), jnp.cumsum(tpe)[:-1]])
            slot = jnp.arange(capacity)
            pos = offsets[:, None] + slot[None, :]
            valid = slot[None, :] < tpe[:, None]
            tok_idx = indices[jnp.minimum(pos, tokens - 1)]
            xe = jnp.where(valid[..., None], xf[tok_idx], 0.0)
            h = jax.nn.gelu(jnp.einsum('ech,ehf->ecf', xe, w1), approximate=True)
            ye = jnp.einsum('ecf,efh->ech', h, w2)
            tok_safe = jnp.where(valid, tok_idx, tokens)
            out = jnp.zeros((tokens + 1, hs), xf.dtype).at[tok_safe.reshape(-1)].add(ye.reshape(-1, hs))
            return out[:tokens]
        sl, bs, hs = x.shape
        tokens = sl * bs
        capacity = int(CAPACITY_FACTOR * tokens / NUM_EXPERTS)
        xf = x.reshape(tokens, hs)
        scores = jax.nn.softmax(xf @ router_w, axis=-1)
        expert_weights, top_experts = jax.lax.top_k(scores, TOP_K)
        out = jnp.zeros_like(xf)
        for k in range(TOP_K):
            y = _dispatch_compute(xf, top_experts[:, k].astype(jnp.int32), w1, w2, capacity)
            out = out + y * expert_weights[:, k][:, None]
        return out.reshape(sl, bs, hs) + bias
    x = L0_attn_x
    x = x + 0.5 * _L0_ffn_ref(_layernorm(x, axis=-1), L0_ffn_router_w, L0_ffn_w1, L0_ffn_w2, L0_ffn_bias)
    x = x + _L0_attn_ref(_layernorm(x, axis=-1), L0_attn_wq, L0_attn_bq, L0_attn_wk, L0_attn_bk, L0_attn_wv, L0_attn_bv, L0_attn_wo, L0_attn_bo)
    x = x + 0.5 * _L0_ffn_ref(_layernorm(x, axis=-1), L0_ffn_router_w, L0_ffn_w1, L0_ffn_w2, L0_ffn_bias)
    return x

_drawn_inputs = setup_inputs


def setup_inputs(seed=0):
    import zlib

    import numpy as np

    out = dict(_drawn_inputs(seed))
    spreads = {'L0_attn_bq': (0.0, 0.733),
     'L0_attn_bk': (0.0, 0.8),
     'L0_attn_bv': (0.0, 0.1),
     'L0_attn_bo': (0.0, 0.1),
     'L0_ffn_bias': (0.0, 0.1)}
    factors = {}
    for name, (base, spread) in spreads.items():
        noise = np.random.default_rng([zlib.crc32(name.encode()), seed]).standard_normal(out[name].shape)
        drawn = base * np.exp(spread * noise) if base else spread * noise
        out[name] = jnp.asarray(drawn.astype(out[name].dtype))
    for name, factor in factors.items():
        out[name] = (out[name] * factor).astype(out[name].dtype)
    return out
```

```python
from contextlib import ExitStack

import numpy as np
import concourse.bass as bass
from concourse import mybir

F32 = mybir.dt.float32
F32R = mybir.dt.float32r
BF16 = mybir.dt.bfloat16
U32 = mybir.dt.uint32
ALU = mybir.AluOpType
ACT = mybir.ActivationFunctionType
AX = mybir.AxisListType

P = 128
D = 256
DH = D // P
SEQ = 1024
NB = 4
TOK = NB * SEQ
TPB = SEQ // P
HEADS = 16
HD = D // HEADS
GH = 4
NG = HEADS // GH
NE = 8
TOPK = 2
CAP = TOK // NE
FFN = 1024
NF = FFN // P
NS = CAP // P
SLOTS = TOPK * TOK
C = 512
SCORE_SCALE = float(HD) ** -0.5
EPS = 1e-5
NEG = -1e30

Q_PARTS = (0, 0, 0, 1, 1, 2)
K_PARTS = (0, 1, 2, 0, 1, 0)
STACK = HD * len(Q_PARTS)
ROWS = STACK + 3

PIECES = [(c, j, max(0, P * j - C * c), C - max(0, P * j - C * c)) for c in range(2) for j in range(4 * (c + 1))]
DIAG = [j >= 4 * c for c, j, _, _ in PIECES]
NP_ = len(PIECES)
MAXP = [(q, c, min(C, P * (q + 1) - C * c)) for q in range(TPB) for c in range(q // 4 + 1)]
MAX_STEPS = 8
MAX_PER = GH * len(MAXP) // MAX_STEPS
STEPS = NG * NP_

K_ID, K_LT, K_MASK, K_IOTA, K_OFF, K_END = 0, P, 2 * P, 3 * P, 3 * P + NE, 3 * P + NE + TOPK * TPB


def shape_constants():
    p = np.arange(P)
    k = np.zeros((P, K_END), np.float32)
    k[:, K_ID:K_ID + P] = np.eye(P)
    k[:, K_LT:K_LT + P] = p[:, None] < p[None, :]
    k[:, K_MASK:K_MASK + P] = np.where(p[None, :] > p[:, None], NEG, 0.0)
    k[:, K_IOTA:K_IOTA + NE] = np.arange(NE)
    k[:, K_OFF:K_END] = np.repeat(np.arange(TOPK) * TOK - SLOTS, TPB)
    return k


def rope_tables():
    one = np.float32(1.0)
    inv = one / np.float32(10000.0) ** (np.arange(0, HD, 2, dtype=np.float32) / np.float32(HD))
    angle = inv[:, None] * np.arange(SEQ, dtype=np.float32)[None, :]
    pair = (np.arange(P) % HD) // 2
    sign = np.where(np.arange(P) % 2 == 0, -one, one)[:, None]
    return np.stack([np.cos(angle)[pair], np.sin(angle)[pair] * sign]).astype(np.float32)


class Link:

    def __init__(self, eng, sem, base=0):
        self.eng, self.sem, self.base, self.n = eng, sem, base, 0

    def add(self, ins):
        ins.then_inc(self.sem, 1)
        self.n += 1

    def sync(self):
        self.eng.wait_ge(self.sem, self.base + self.n)


def build(nc, x, wq, bq, wk, bk, wv, bv, wo, bo, router_w, w1, w2, fbias, consts, rope, out):
    ctx = ExitStack()
    with ctx:
        def sb(name, shape, dt, where=ctx):
            return where.enter_context(nc.sbuf_tensor(name, shape, dt))

        def sem(name):
            return ctx.enter_context(nc.semaphore(name))

        def sems(prefix, names):
            return {n: sem(f"{prefix}_{n}") for n in names.split()}

        bank = [ctx.enter_context(nc.psum_tensor(f"bank{i}", [P, C], F32)) for i in range(8)]

        xe = nc.dram_tensor("expert_rows", [SLOTS, D], F32, kind="Internal").ap()
        ye = nc.dram_tensor("expert_out", [SLOTS + 1, D], F32, kind="Internal").ap()
        qkd = nc.dram_tensor("qk_parts", [3, 2, D, SEQ], BF16, kind="Internal").ap()
        md = nc.dram_tensor("max_rows", [3, GH * TPB, P], BF16, kind="Internal").ap()

        X = sb("X", [P, NB * TPB, D], F32)
        XN = sb("XN", [P, TPB, D], F32)
        XTH = sb("XTH", [P, DH, SEQ], F32R)
        XTL = sb("XTL", [P, DH, SEQ], F32R)
        WH = sb("WH", [P, 4, DH, D], F32R)
        WL = sb("WL", [P, 4, DH, D], F32R)
        RW = sb("RW", [P, DH, 2 * NE], F32R)
        KC = sb("KC", [P, K_END], F32)
        ID16 = sb("ID16", [P, P], BF16)
        LT16 = sb("LT16", [P, P], BF16)
        MASK16 = sb("MASK16", [P, P], BF16)
        ONES16 = sb("ONES16", [P, P], BF16)
        BQK = sb("BQK", [P, 2, DH], F32)
        BV = sb("BV", [P, D], F32)
        BO = sb("BO", [P, D], F32)
        FB = sb("FB", [P, D], F32)
        NEGHALF = sb("NEGHALF", [P, TPB], F32)
        BST = sb("BST", [P, TPB, 6], F32)
        MV = sb("MV", [P, TPB, 2], F32)
        VE = sb("VE", [P, TPB], F32)
        RSTD = sb("RSTD", [P, TPB], F32)
        LA = sb("LA", [P, TPB, NE], F32)
        LG = sb("LG", [P, TPB, NE], F32)
        TOP = sb("TOP", [P, TPB, 8], F32)
        TIX = sb("TIX", [P, TPB, 8], U32)
        IDXF = sb("IDXF", [P, TOPK, TPB], F32)
        OH = sb("OH", [P, TOPK, TPB, NE], BF16)
        DL = sb("DL", [P, TPB, NE], F32)
        DW = sb("DW", [P, TOPK, TPB], F32)
        EL = sb("EL", [P, TPB, NE], F32)
        EW = sb("EW", [P, TOPK, TPB], F32)
        SUM = sb("SUM", [P, TPB], F32)
        RS = sb("RS", [P, TPB], F32)
        WV_ = sb("WV_", [P, TOPK, TPB], F32)
        TOT = sb("TOT", [P, TOPK, TPB, NE], F32)
        PX = sb("PX", [P, TOPK, TPB, NE], F32)
        CARRY = sb("CARRY", [P, TOPK, NE], F32)
        RANK = sb("RANK", [P, TOPK, TPB, NE], F32)
        SEL = sb("SEL", [P, TOPK, TPB, NE], F32)
        RK = sb("RK", [P, TOPK, TPB], F32)
        OK = sb("OK", [P, TOPK, TPB], F32)
        SL = sb("SL", [P, TOPK, TPB], F32)
        SL2 = sb("SL2", [P, TOPK, TPB], F32)
        SLT = sb("SLT", [P, TOPK * TPB], U32)
        GIX = sb("GIX", [P, TOPK * TPB], U32)
        SLP = sb("SLP", [P, NB + 1, TOPK * TPB], U32)
        WP = sb("WP", [P, NB, TOPK * TPB], F32)

        fctx = ExitStack()
        WRAW1 = sb("WRAW1", [P, DH, FFN], F32, fctx)
        WRAW2 = sb("WRAW2", [P, NF, D], F32, fctx)
        W1H = sb("W1H", [P, DH, FFN], F32R, fctx)
        W1L = sb("W1L", [P, DH, FFN], F32R, fctx)
        W2H = sb("W2H", [P, NF, D], F32R, fctx)
        W2L = sb("W2L", [P, NF, D], F32R, fctx)
        XR = [sb(f"XR{k}", [P, NS, D], F32, fctx) for k in range(TOPK)]
        XEH = [sb(f"XEH{k}", [P, DH, CAP], F32R, fctx) for k in range(TOPK)]
        XEL = [sb(f"XEL{k}", [P, DH, CAP], F32R, fctx) for k in range(TOPK)]
        GE = sb("GE", [P, 2, C], F32, fctx)
        HH = sb("HH", [P, 4, C], F32R, fctx)
        HL = sb("HL", [P, 4, C], F32R, fctx)
        YS = [sb(f"YS{k}", [P, NS, D], F32, fctx) for k in range(TOPK)]
        fctx.close()
        actx = ctx
        G = sb("G", [P, TOPK * TPB, D], F32, actx)
        ROPE = sb("ROPE", [P, 2, SEQ], F32, actx)
        STQ = [sb(f"STQ{i}", [ROWS, GH, SEQ], BF16, actx) for i in range(2)]
        STK = [sb(f"STK{i}", [ROWS, GH, SEQ], BF16, actx) for i in range(2)]
        PR = sb("PR", [P, 2 * GH, C], F32, actx)
        V = sb("V", [P, TPB, HEADS, 32], F32, actx)
        QB = sb("QB", [P, 2, C], F32, actx)
        QS = sb("QS", [P, C], F32, actx)
        QC = sb("QC", [P, 2, C], F32, actx)
        QN = sb("QN", [P, C], F32, actx)
        QR = sb("QR", [P, C], F32, actx)
        QE = sb("QE", [P, C], F32, actx)
        PT = sb("PT", [P, 2, 3, C], BF16, actx)
        MX = sb("MX", [P, 2, P], F32, actx)
        MR = sb("MR", [GH * TPB, P], F32, actx)
        M3 = sb("M3", [GH * TPB, 3, P], BF16, actx)
        OT = sb("OT", [P, 2, C], F32, actx)
        RC = sb("RC", [P, 4, GH], F32, actx)
        A = sb("A", [P, TPB, D], F32, actx)

        ident = KC[:, K_ID:K_ID + P]

        passed = {}

        def gate(eng, name, sem_, value):
            eng.wait_ge(sem_, value)
            eng.sem_inc(passed[name], 1)

        su = sems("setup", "dma split raw_used zeros filled act dve pool")
        x_in, out_done = sem("x_in"), sem("out_done")
        LN_SEMS = "link stats rstd_link rstd xn tp hi lo"
        RT_SEMS = "logits link oh diff exps ranks route scattered"
        ln = {n: sems(f"ln_{n}", LN_SEMS) for n in ("r0", "att", "r1")}
        pj = sems("proj", "tp hi lo out added")
        rt = {n: sems(f"rt{n}", RT_SEMS) for n in range(2)}
        ff = [sems(f"ffn{n}", "w_in xe_in0 xe_in1 w1_hi w2_hi w1_lo w2_lo xe_tp xe_hi xe_lo "
                              "up gelu h_hi h_lo down y_evac y_out0 y_out1") for n in range(2)]
        cb = [sems(f"comb{n}", "index gathered link x") for n in range(2)]
        at = sems("att", "rope_in const qkv qb swap cos sin rot p1 e1 p2 p3 parts_out0 parts_out1 v_ps v stk_in0 stk_in1 "
                         "mx_ps mx_red m_link m_done m3_link m3 m_out m_row st exp sel pv ot b7 b7_free a_link a_done")

        passed.update(dve=sem("dve_passed"), pool=sem("pool_passed"), sp=sem("sp_passed"))

        block = ctx.enter_context(nc.Block())
        batch_tiles = x.rearrange("b (t p) d -> b p t d", p=P)
        out_tiles = out.rearrange("b (t p) d -> b p t d", p=P)

        def xb(b, t=None):
            if t is None:
                return X[:, bass.ds(b * TPB, TPB), :]
            return X[:, bass.ds(b * TPB + t, 1), :].rearrange("p o d -> p (o d)")

        def norm_dve(dve, s, b):
            for t in range(TPB):
                ins = nc.vector.bn_stats(BST[:, t, :], xb(b, t))
            ins.then_inc(s["link"], 1)
            gate(dve, "dve", s["link"], 1 + b)
            for t in range(TPB):
                ins = nc.vector.bn_aggr(MV[:, t, :], BST[:, t, :])
            ins.then_inc(s["stats"], 1)
            dve.wait_ge(s["rstd"], 1 + b)
            for t in range(TPB):
                nc.vector.tensor_scalar(XN[:, t, :], xb(b, t), MV[:, t, 0:1], RSTD[:, t:t + 1],
                                        ALU.subtract, ALU.mult).then_inc(s["xn"], 1)

        def norm_pool(pool, s, b):
            gate(pool, "pool", s["stats"], 1 + b)
            nc.gpsimd.tensor_scalar(VE[:, :], MV[:, :, 1], EPS, None, ALU.add).then_inc(s["rstd_link"], 1)
            pool.wait_ge(s["rstd_link"], 1 + b)
            nc.gpsimd.tensor_tensor(RSTD[:, :], VE[:, :], NEGHALF[:, :], ALU.pow).then_inc(s["rstd"], 1)

        def turn_pe(pe, s, src, b):
            for i in range(4):
                pe.wait_ge(s["lo"], 1 + i + 4 * b)
                if "xn" in s:
                    pe.wait_ge(s["xn"], 2 * i + 2 + TPB * b)
                for d in range(DH):
                    for t in range(2):
                        ins = nc.tensor.transpose(bank[i % 2][:, d * 2 * P + t * P:d * 2 * P + t * P + P],
                                                  src[:, 2 * i + t, d * P:d * P + P], ident)
                ins.then_inc(s["tp"], 1)

        def turn_act(act, s, b):
            for i in range(4):
                act.wait_ge(s["tp"], 1 + i + 4 * b)
                nc.scalar.activation(XTH[:, :, i * 2 * P:(i + 1) * 2 * P],
                                     bank[i % 2][:, :].rearrange("p (d n) -> p d n", d=DH), ACT.Copy).then_inc(s["hi"], 1)

        def turn_dve(dve, s, b):
            for i in range(4):
                dve.wait_ge(s["hi"], 1 + i + 4 * b)
                cols = slice(i * 2 * P, (i + 1) * 2 * P)
                nc.vector.tensor_tensor(XTL[:, :, cols], bank[i % 2][:, :].rearrange("p (d n) -> p d n", d=DH),
                                        XTH[:, :, cols].bitcast(F32), ALU.subtract).then_inc(s["lo"], 1)

        LOGIT, RANKB = bank[6], bank[7]

        def route_pe(pe, l, s, b):
            pe.wait_ge(l["lo"], 6 + 4 * b)
            for t in range(TPB):
                tok = slice(t * P, t * P + P)
                o = LOGIT[:, t * 2 * NE:(t + 1) * 2 * NE]
                for d in range(DH):
                    nc.tensor.matmul(o, XTH[:, d, tok], RW[:, d, :], start=(d == 0), stop=False, skip_group_check=True)
                for d in range(DH):
                    ins = nc.tensor.matmul(o[:, 0:NE], XTL[:, d, tok], RW[:, d, 0:NE], start=False, stop=(d == 1),
                                           skip_group_check=True)
            ins.then_inc(s["logits"], 1)
            pe.wait_ge(s["oh"], 1 + b)
            oh = OH[:, :, :, :].rearrange("p k t e -> p (k t e)")
            n = TOPK * TPB * NE
            nc.tensor.matmul(RANKB[:, 0:n], LT16[:, :], oh, start=True, stop=True)
            nc.tensor.matmul(RANKB[:, n:2 * n], ONES16[:, :], oh, start=True, stop=True).then_inc(s["ranks"], 1)

        def route_act(act, s, b):
            act.wait_ge(s["diff"], 1 + b)
            nc.scalar.activation(EL[:, :, :], DL[:, :, :], ACT.Exp)
            nc.scalar.activation(EW[:, :, :], DW[:, :, :], ACT.Exp).then_inc(s["exps"], 1)

        ROUTE_LINKS = 26

        def route_dve(dve, s, b):
            k = Link(dve, s["link"], b * ROUTE_LINKS)
            dve.wait_ge(s["logits"], 1 + b)
            logit = LOGIT[:, 0:TPB * 2 * NE].rearrange("p (t e) -> p t e", t=TPB)
            k.add(nc.vector.tensor_copy(LA[:, :, :], logit[:, :, NE:]))
            k.sync()
            k.add(nc.vector.tensor_tensor(LG[:, :, :], logit[:, :, 0:NE], LA[:, :, :], ALU.add))
            gate(dve, "dve", s["link"], k.base + k.n)
            for t in range(TPB):
                ins = nc.vector.max(TOP[:, t, :], LG[:, t, :])
            k.add(ins)
            gate(dve, "dve", s["link"], k.base + k.n)
            for t in range(TPB):
                ins = nc.vector.max_index(TIX[:, t, :], TOP[:, t, :], LG[:, t, :])
            k.add(ins)
            k.sync()
            k.add(nc.vector.tensor_copy(IDXF[:, :, :], TIX[:, :, 0:TOPK].rearrange("p t k -> p k t")))
            k.sync()
            iota = KC[:, K_IOTA:K_IOTA + NE].unsqueeze(1).to_broadcast([P, TPB, NE])
            for c in range(TOPK):
                ins = nc.vector.tensor_tensor(OH[:, c, :, :], IDXF[:, c, :].unsqueeze(2).to_broadcast([P, TPB, NE]),
                                              iota, ALU.is_equal)
            ins.then_inc(s["oh"], 1)
            nc.vector.tensor_tensor(DL[:, :, :], LG[:, :, :], TOP[:, :, 0:1].to_broadcast([P, TPB, NE]), ALU.subtract)
            for c in range(TOPK):
                ins = nc.vector.tensor_tensor(DW[:, c, :], TOP[:, :, c], TOP[:, :, 0], ALU.subtract)
            ins.then_inc(s["diff"], 1)
            n = TOPK * TPB * NE
            dve.wait_ge(s["ranks"], 1 + b)
            k.add(nc.vector.tensor_copy(TOT[:, :, :, :].rearrange("p k t e -> p (k t e)"), RANKB[:, n:2 * n]))
            k.add(nc.vector.tensor_copy(PX[:, :, 0, :], CARRY[:, :, :]))
            k.sync()
            for t in range(1, TPB):
                k.add(nc.vector.tensor_tensor(PX[:, :, t, :], PX[:, :, t - 1, :], TOT[:, :, t - 1, :], ALU.add))
                k.sync()
            k.add(nc.vector.tensor_tensor(CARRY[:, :, :], PX[:, :, TPB - 1, :], TOT[:, :, TPB - 1, :], ALU.add))
            k.add(nc.vector.tensor_tensor(RANK[:, :, :, :].rearrange("p k t e -> p (k t e)"), RANKB[:, 0:n],
                                          PX[:, :, :, :].rearrange("p k t e -> p (k t e)"), ALU.add))
            k.sync()
            k.add(nc.vector.tensor_tensor(SEL[:, :, :, :].rearrange("p k t e -> p (k t e)"),
                                          RANK[:, :, :, :].rearrange("p k t e -> p (k t e)"),
                                          OH[:, :, :, :].rearrange("p k t e -> p (k t e)"), ALU.mult))
            k.sync()
            k.add(nc.vector.tensor_reduce(RK[:, :, :], SEL[:, :, :, :], AX.X, ALU.add))
            k.sync()
            k.add(nc.vector.tensor_scalar(OK[:, :, :], RK[:, :, :], float(CAP), None, ALU.is_lt))
            k.add(nc.vector.scalar_tensor_tensor(SL[:, :, :], IDXF[:, :, :], float(CAP), RK[:, :, :], ALU.mult, ALU.add))
            k.sync()
            k.add(nc.vector.tensor_tensor(SL2[:, :, :].rearrange("p k t -> p (k t)"), SL[:, :, :].rearrange("p k t -> p (k t)"),
                                          KC[:, K_OFF:K_END], ALU.add))
            k.sync()
            k.add(nc.vector.tensor_tensor(SL[:, :, :], SL2[:, :, :], OK[:, :, :], ALU.mult))
            k.sync()
            flat = SL[:, :, :].rearrange("p k t -> p (k t)")
            k.add(nc.vector.tensor_scalar(SLP[:, bass.ds(b, 1), :].rearrange("p o n -> p (o n)"), flat, float(SLOTS), None, ALU.add))
            nc.vector.tensor_scalar(SLT[:, :], flat, float(SLOTS), None, ALU.add).then_inc(s["route"], 1)
            dve.wait_ge(s["exps"], 1 + b)
            k.add(nc.vector.tensor_reduce(SUM[:, :], EL[:, :, :], AX.X, ALU.add))
            k.sync()
            k.add(nc.vector.reciprocal(RS[:, :], SUM[:, :]))
            k.sync()
            for c in range(TOPK):
                ins = nc.vector.tensor_tensor(WV_[:, c, :], EW[:, c, :], RS[:, :], ALU.mult)
            k.add(ins)
            k.sync()
            nc.vector.scalar_tensor_tensor(WP[:, bass.ds(b, 1), :].rearrange("p o n -> p (o n)"),
                                           WV_[:, :, :].rearrange("p k t -> p (k t)"), 0.5,
                                           OK[:, :, :].rearrange("p k t -> p (k t)"), ALU.mult, ALU.mult)
            assert k.n == ROUTE_LINKS, k.n

        def route_pool(pool, s, b):
            gate(pool, "pool", s["route"], 1 + b)
            for c in range(TOPK):
                for t in range(TPB):
                    nc.gpsimd.indirect_dma_start(
                        out=xe[:, :], out_offset=bass.IndirectOffsetOnAxis(ap=SLT[:, c * TPB + t:c * TPB + t + 1], axis=0),
                        in_=XN[:, t, :], in_offset=None, bounds_check=SLOTS - 1, oob_is_err=False,
                    ).then_inc(s["scattered"], 16)

        SCATTERED = 16 * TOPK * TPB

        Y, UP, XTP = [bank[0], bank[1]], [bank[2], bank[3], bank[4], bank[5]], [bank[6], bank[7]]

        def ffn_sync(sp, ph):
            s = ff[ph]
            with sp.Fori(0, NE) as e:
                sp.dma_start(WRAW1[:, :, :], w1[bass.ds(e, 1), :, :].rearrange("o (c p) f -> p (o c) f", p=P)).then_inc(s["w_in"], 16)
                sp.dma_start(WRAW2[:, :, :], w2[bass.ds(e, 1), :, :].rearrange("o (c p) f -> p (o c) f", p=P)).then_inc(s["w_in"], 16)
                for k in range(TOPK):
                    rows = xe[bass.ds(e * CAP + k * TOK, CAP), :].rearrange("(s p) d -> p s d", p=P)
                    sp.dma_start(XR[k][:, :, :], rows).then_inc(s[f"xe_in{k}"], 16)
                sp.wait_ge(s["w1_lo"], NF * e + NF)
                sp.wait_ge(s["w2_lo"], NF * e + NF)
                sp.wait_ge(s["w1_hi"], NF * e + NF)
                sp.wait_ge(s["w2_hi"], NF * e + NF)
                gate(sp, "sp", s["xe_tp"], 2 * TOPK * e + 2 * TOPK)

        def xe_pe(pe, s, e, k):
            pe.wait_ge(s[f"xe_in{k}"], 16 * e + 16)
            for d in range(DH):
                pe.wait_ge(s["xe_lo"], 4 * e + 2 * k + d + 1)
                for t in range(NS):
                    ins = nc.tensor.transpose(XTP[d][:, t * P:t * P + P], XR[k][:, t, d * P:d * P + P], ident)
                ins.then_inc(s["xe_tp"], 1)

        def xe_act(act, s, e, k):
            for d in range(DH):
                act.wait_ge(s["xe_tp"], 4 * e + 2 * k + d + 1)
                nc.scalar.activation(XEH[k][:, d, :], XTP[d][:, :], ACT.Copy).then_inc(s["xe_hi"], 1)

        def xe_dve(dve, s, e, k):
            for d in range(DH):
                dve.wait_ge(s["xe_hi"], 4 * e + 2 * k + d + 1)
                nc.vector.tensor_tensor(XEL[k][:, d, :], XTP[d][:, :], XEH[k][:, d, :].bitcast(F32),
                                        ALU.subtract).then_inc(s["xe_lo"], 1)

        def block_pe(pe, s, e, k, last):
            n8 = 2 * NF * e + NF * k
            pe.wait_ge(s["xe_lo"], 4 * e + 2 * k + 4)

            def up(f):
                pe.wait_ge(s["gelu"], n8 + f + 1)
                pe.wait_ge(s["w1_hi"], NF * e + f + 1)
                pe.wait_ge(s["w1_lo"], NF * e + f + 1)
                cols = slice(f * P, f * P + P)
                ops = [(w, a, d) for w, a in ((W1H, XEH), (W1H, XEL), (W1L, XEH)) for d in range(DH)]
                for i, (w, a, d) in enumerate(ops):
                    ins = nc.tensor.matmul(UP[f % 4][:, :], w[:, d, cols], a[k][:, d, :], start=(i == 0), stop=(i == len(ops) - 1))
                ins.then_inc(s["up"], 1)

            def down(f):
                pe.wait_ge(s["h_lo"], 2 + n8 + f + 1)
                pe.wait_ge(s["w2_hi"], NF * e + f + 1)
                pe.wait_ge(s["w2_lo"], NF * e + f + 1)
                for t in range(NS):
                    if f == 0 and t % 2 == 0:
                        pe.wait_ge(s["y_evac"], 4 * e + 2 * k + t // 2 + 1)
                    o = Y[t // 2][:, (t % 2) * D:(t % 2 + 1) * D]
                    rows = slice(t * P, t * P + P)
                    for i, (h, w) in enumerate(((HH, W2H), (HL, W2H), (HH, W2L))):
                        ins = nc.tensor.matmul(o, h[:, f % 4, rows], w[:, f, :], start=(f == 0 and t % 2 == 0 and i == 0),
                                               stop=(f == NF - 1 and i == 2), skip_group_check=True)
                ins.then_inc(s["down"], 1)

            for f in range(NF + 2):
                if f < NF:
                    up(f)
                if f >= 2:
                    down(f - 2)
                if f == 3:
                    if k == 0:
                        xe_pe(pe, s, e, 1)
                    elif not last:
                        xe_pe(pe, s, e + 1, 0)

        def w1_hi(s, f):
            cols = slice(f * P, f * P + P)
            nc.scalar.activation(W1H[:, :, cols], WRAW1[:, :, cols], ACT.Copy).then_inc(s["w1_hi"], 1)

        def w2_hi(s, f):
            nc.scalar.activation(W2H[:, f, :], WRAW2[:, f, :], ACT.Copy).then_inc(s["w2_hi"], 1)

        def block_act(act, s, e, k, last):
            n8 = 2 * NF * e + NF * k
            split_next = k == TOPK - 1 and not last
            if split_next:
                act.wait_ge(s["w_in"], 32 * e + 64)
            for f in range(NF + 3):
                if f < NF:
                    act.wait_ge(s["up"], n8 + f + 1)
                    act.wait_ge(s["h_lo"], n8 + f + 1)
                    nc.scalar.activation(GE[:, f % 2, :], UP[f % 4][:, :], ACT.Gelu_apprx_tanh).then_inc(s["gelu"], 1)
                    if split_next:
                        w1_hi(s, f)
                if f >= 3 and split_next:
                    act.wait_ge(s["down"], 4 + n8 + f - 2)
                    w2_hi(s, f - 3)
                if f == 3:
                    if k == 0:
                        xe_act(act, s, e, 1)
                    elif not last:
                        xe_act(act, s, e + 1, 0)
            act.wait_ge(s["down"], 4 + n8 + NF)
            act.wait_ge(s[f"y_out{k}"], 16 * e + 16)
            for i in range(2):
                nc.scalar.activation(YS[k][:, 2 * i:2 * i + 2, :], Y[i][:, :].rearrange("p (t n) -> p t n", t=2),
                                     ACT.Copy).then_inc(s["y_evac"], 1)
            act.wait_ge(s["y_evac"], 4 + 4 * e + 2 * k)
            act.dma_start(ye[bass.ds(e * CAP + k * TOK, CAP), :].rearrange("(s p) d -> p s d", p=P),
                          YS[k][:, :, :]).then_inc(s[f"y_out{k}"], 16)

        def block_dve(dve, s, e, k, last):
            n8 = 2 * NF * e + NF * k
            for f in range(NF):
                dve.wait_ge(s["gelu"], 4 + n8 + f + 1)
                dve.wait_ge(s["down"], n8 + f + 1)
                nc.vector.tensor_copy(HH[:, f % 4, :], GE[:, f % 2, :]).then_inc(s["h_hi"], 1)
                dve.wait_ge(s["h_hi"], n8 + f + 1)
                nc.vector.tensor_tensor(HL[:, f % 4, :], GE[:, f % 2, :], HH[:, f % 4, :].bitcast(F32),
                                        ALU.subtract).then_inc(s["h_lo"], 1)
                if f == 3:
                    if k == 0:
                        xe_dve(dve, s, e, 1)
                    elif not last:
                        xe_dve(dve, s, e + 1, 0)

        def split_pool(pool, s, e):
            for f in range(NF):
                cols = slice(f * P, f * P + P)
                pool.wait_ge(s["w1_hi"], NF * e + f + 1)
                nc.gpsimd.tensor_tensor(W1L[:, :, cols], WRAW1[:, :, cols], W1H[:, :, cols].bitcast(F32),
                                        ALU.subtract).then_inc(s["w1_lo"], 1)
                pool.wait_ge(s["w2_hi"], NF * e + f + 1)
                nc.gpsimd.tensor_tensor(W2L[:, f, :], WRAW2[:, f, :], W2H[:, f, :].bitcast(F32),
                                        ALU.subtract).then_inc(s["w2_lo"], 1)

        def ffn_pe(pe, ph):
            s = ff[ph]
            xe_pe(pe, s, 0, 0)
            with pe.Fori(0, NE - 1) as e:
                for k in range(TOPK):
                    block_pe(pe, s, e, k, False)
            for k in range(TOPK):
                block_pe(pe, s, NE - 1, k, True)

        def ffn_act(act, ph):
            s = ff[ph]
            act.wait_ge(s["w_in"], 32)
            for f in range(NF):
                w1_hi(s, f)
                w2_hi(s, f)
            xe_act(act, s, 0, 0)
            with act.Fori(0, NE - 1) as e:
                for k in range(TOPK):
                    block_act(act, s, e, k, False)
            for k in range(TOPK):
                block_act(act, s, NE - 1, k, True)

        def ffn_dve(dve, ph):
            s = ff[ph]
            xe_dve(dve, s, 0, 0)
            with dve.Fori(0, NE - 1) as e:
                for k in range(TOPK):
                    block_dve(dve, s, e, k, False)
            for k in range(TOPK):
                block_dve(dve, s, NE - 1, k, True)

        def ffn_pool(pool, ph):
            with pool.Fori(0, NE) as e:
                split_pool(pool, ff[ph], e)

        FFN_OUT = 16 + 16 * NE

        def index_dve(dve, s, b):
            nc.vector.tensor_copy(GIX[:, :], SLP[:, bass.ds(b, 1), :].rearrange("p o n -> p (o n)")).then_inc(s["index"], 1)

        def gather_pool(pool, s, b):
            gate(pool, "pool", s["index"], 1 + b)
            for n in range(TOPK * TPB):
                nc.gpsimd.indirect_dma_start(
                    out=G[:, n, :], out_offset=None, in_=ye[:, :],
                    in_offset=bass.IndirectOffsetOnAxis(ap=GIX[:, n:n + 1], axis=0),
                ).then_inc(s["gathered"], 16)

        GATHERED = 16 * TOPK * TPB

        def combine_dve(dve, s, b):
            dve.wait_ge(s["gathered"], GATHERED * b + GATHERED)
            for c in range(TOPK):
                for t in range(TPB):
                    n = c * TPB + t
                    ins = nc.vector.scalar_tensor_tensor(
                        xb(b, t), G[:, n, :], WP[:, bass.ds(b, 1), n:n + 1].rearrange("p o n -> p (o n)"),
                        xb(b, t), ALU.mult, ALU.add)
                ins.then_inc(s["link"], 1)
                dve.wait_ge(s["link"], 2 * b + c + 1)
            nc.vector.scalar_tensor_tensor(xb(b), FB[:, :].unsqueeze(1).to_broadcast([P, TPB, D]), 0.5,
                                           xb(b), ALU.mult, ALU.add).then_inc(s["x"], 1)
            gate(dve, "dve", s["x"], 1 + b)

        MAXB, STB, PVB, B7 = [bank[0], bank[1]], [bank[2], bank[3], bank[4]], [bank[5], bank[6]], bank[7]
        QKB, VB_, OPB = [bank[2], bank[3]], [bank[4], bank[5]], [bank[4], bank[5]]
        QK = [(m, h, c) for m in range(2) for h in range(DH) for c in range(2)]
        PAIR_SWAP = [i ^ 1 for i in range(32)]

        def project(o, lhs, rhs):
            ops = [(a, c, d) for a, c in ((0, 0), (1, 0), (0, 1)) for d in range(DH)]
            for i, (a, c, d) in enumerate(ops):
                ins = nc.tensor.matmul(o, lhs(a, d), rhs(c, d), start=(i == 0), stop=(i == len(ops) - 1))
            return ins

        XT = (XTH, XTL)
        W = (WH, WL)

        def qkv_pe(pe, b):
            l = ln["att"]
            pe.wait_ge(l["lo"], 6 + 4 * b)
            for i, (m, h, c) in enumerate(QK):
                pe.wait_ge(at["qb"], 8 * b + i + 1)
                project(QKB[i % 2][:, :], lambda a, d: W[a][:, m, d, h * P:h * P + P],
                        lambda a, d: XT[a][:, d, c * C:c * C + C]).then_inc(at["qkv"], 1)
            for t in range(TPB):
                pe.wait_ge(at["v"], 8 * b + t + 1)
                project(VB_[t % 2][:, 0:D], lambda a, d: XT[a][:, d, t * P:t * P + P],
                        lambda a, d: W[a][:, 2, d, :]).then_inc(at["v_ps"], 1)

        def qk_act(act, b):
            def p1(i):
                act.wait_ge(at["rot"], 8 * b + i + 1)
                act.wait_ge(at[f"parts_out{i % 2}"], 16 * (4 * b + i // 2 + 1))
                nc.scalar.activation(PT[:, i % 2, 0, :], QN[:, :], ACT.Copy).then_inc(at["p1"], 1)
                act.wait_ge(at["e1"], 8 * b + i + 1)
                nc.scalar.activation(PT[:, i % 2, 1, :], QR[:, :], ACT.Copy).then_inc(at["p2"], 1)

            for i, (m, h, c) in enumerate(QK):
                act.wait_ge(at["qkv"], 8 * b + i + 1)
                act.wait_ge(at["cos"], 8 * b + i + 1)
                nc.scalar.activation(QB[:, i % 2, :], QKB[i % 2][:, :], ACT.Identity, bias=BQK[:, m, h:h + 1]).then_inc(at["qb"], 1)
                if i >= 1:
                    p1(i - 1)
            p1(7)

        def qk_pool(pool, b):
            for i, (m, h, c) in enumerate(QK):
                pool.wait_ge(at["qb"], 2 + 8 * b + i + 1)
                nc.gpsimd.tensor_tensor(QC[:, i % 2, :], QB[:, i % 2, :], ROPE[:, 0, c * C:c * C + C], ALU.mult).then_inc(at["cos"], 1)
                pool.wait_ge(at["e1"], 8 * b + i + 1)
                pool.wait_ge(at["p2"], 8 * b + i + 1)
                nc.gpsimd.tensor_tensor(PT[:, i % 2, 2, :], QR[:, :], PT[:, i % 2, 1, :], ALU.subtract).then_inc(at["p3"], 1)

        def qkv_dve(dve, b):
            for i, (m, h, c) in enumerate(QK):
                gate(dve, "dve", at["qb"], 2 + 8 * b + i + 1)
                nc.vector.stream_shuffle(QS[:, :], QB[:, i % 2, :], PAIR_SWAP).then_inc(at["swap"], 1)
                dve.wait_ge(at["swap"], 8 * b + i + 1)
                nc.vector.tensor_tensor(QE[:, :], QS[:, :], ROPE[:, 1, c * C:c * C + C], ALU.mult).then_inc(at["sin"], 1)
                dve.wait_ge(at["sin"], 8 * b + i + 1)
                dve.wait_ge(at["cos"], 2 + 8 * b + i + 1)
                nc.vector.tensor_tensor(QN[:, :], QC[:, i % 2, :], QE[:, :], ALU.add).then_inc(at["rot"], 1)
                dve.wait_ge(at["p1"], 8 * b + i + 1)
                dve.wait_ge(at["p3"], 8 * b + i + 1)
                nc.vector.tensor_tensor(QR[:, :], QN[:, :], PT[:, i % 2, 0, :], ALU.subtract).then_inc(at["e1"], 1)
            for t in range(TPB):
                dve.wait_ge(at["v_ps"], 8 * b + t + 1)
                nc.vector.tensor_tensor(V[:, t, :, 0:HD], VB_[t % 2][:, 0:D].rearrange("p (h d) -> p h d", h=HEADS),
                                        BV[:, :].rearrange("p (h d) -> p h d", h=HEADS), ALU.add).then_inc(at["v"], 1)

        def parts_sync(sp, b):
            for i, (m, h, c) in enumerate(QK):
                sp.wait_ge(at["p3"], 1 + 8 * b + i + 1)
                sp.dma_start(qkd[:, m, h * P:h * P + P, c * C:c * C + C].rearrange("a p n -> p a n"),
                             PT[:, i % 2, :, :]).then_inc(at[f"parts_out{i % 2}"], 16)
            for i in range(2):
                sp.wait_ge(at[f"parts_out{i}"], 16 + 64 * b + 64)

        STACKED = 16 * 2 * len(Q_PARTS)

        def stack_sync(sp, g):
            for m, buf, parts in ((0, STQ, Q_PARTS), (1, STK, K_PARTS)):
                for r, part in enumerate(parts):
                    sp.dma_start(buf[g % 2][HD * r:HD * r + HD, :, :],
                                 qkd[part, m, g * GH * HD:(g + 1) * GH * HD, :].rearrange("(h r) n -> r h n", h=GH),
                                 ).then_inc(at[f"stk_in{g % 2}"], 16)

        def maxrow_sync(sp, b, g):
            u = 4 * b + g
            sp.wait_ge(at["m3"], u + 1)
            sp.dma_start(md.rearrange("a p n -> p a n"), M3[:, :, :]).then_inc(at["m_out"], 16)
            sp.wait_ge(at["m_out"], 16 * u + 16)
            sp.dma_start(STQ[g % 2][STACK:ROWS, :, :], md.rearrange("a (h q) n -> a h (q n)", h=GH)).then_inc(at["m_row"], 16)

        def att_sync(sp, b):
            parts_sync(sp, b)
            stack_sync(sp, 0)
            stack_sync(sp, 1)
            maxrow_sync(sp, b, 0)
            maxrow_sync(sp, b, 1)
            for g in range(2, NG):
                sp.wait_ge(at["st"], (4 * b + g - 1) * GH * NP_)
                stack_sync(sp, g)
                maxrow_sync(sp, b, g)

        def max_pieces(step):
            g, p = divmod(step, NP_)
            if g + 1 >= NG or p >= MAX_STEPS:
                return []
            return [(g + 1, n) for n in range(p * MAX_PER, (p + 1) * MAX_PER)]

        def max_pe(pe, b, g, n):
            h, (q, c, cols) = n // len(MAXP), MAXP[n % len(MAXP)]
            i = (4 * b + g) * GH * len(MAXP) + n
            if n == 0:
                pe.wait_ge(at[f"stk_in{g % 2}"], (2 * b + g // 2 + 1) * STACKED)
            pe.wait_ge(at["mx_red"], i + 1)
            o = MAXB[n % 2]
            diag = q // 4 == c
            ins = nc.tensor.matmul(o[:, 0:cols], STQ[g % 2][0:STACK, h, q * P:q * P + P], STK[g % 2][0:STACK, h, c * C:c * C + cols],
                                   start=True, stop=not diag)
            if diag:
                ins = nc.tensor.matmul(o[:, cols - P:cols], ID16[:, :], MASK16[:, :], start=False, stop=True)
            ins.then_inc(at["mx_ps"], 1)

        def max_dve(dve, b, g, n):
            h, (q, c, cols) = n // len(MAXP), MAXP[n % len(MAXP)]
            i = (4 * b + g) * GH * len(MAXP) + n
            dve.wait_ge(at["mx_ps"], i + 1)
            if n == 0:
                dve.wait_ge(at["m_done"], 4 * b + g + 1)
            nc.vector.tensor_reduce(MX[:, c, h * TPB + q:h * TPB + q + 1], MAXB[n % 2][:, 0:cols], AX.X, ALU.max).then_inc(at["mx_red"], 1)

        def max_join_dve(dve, b, g):
            u = 4 * b + g
            dve.wait_ge(at["mx_red"], 2 + (u + 1) * GH * len(MAXP))
            a, c = (MX[:, i, 0:GH * TPB].rearrange("p (h q) -> p h q", h=GH)[:, :, 4:8] for i in range(2))
            nc.vector.tensor_tensor(a, a, c, ALU.max).then_inc(at["m_link"], 1)

        def b7_use(b, g, what):
            order = [("m", 0)]
            for n in range(NG):
                order += [(0, n)] + ([("m", n + 1)] if n + 1 < NG else []) + [(1, n)]
            return 12 * b + order.index((what, g))

        def max_turn_pe(pe, b, g):
            pe.wait_ge(at["m_link"], 4 * b + g + 1)
            pe.wait_ge(at["b7_free"], b7_use(b, g, "m") + 1)
            nc.tensor.transpose(B7[:, 0:P], MX[:, 0, :], ident).then_inc(at["m_done"], 1)

        def max_split_dve(dve, b, g):
            u = 4 * b + g
            dve.wait_ge(at["m_done"], 1 + u + 1)
            if g:
                dve.wait_ge(at["m_row"], 16 * u)
            src = B7[0:GH * TPB, 0:P]
            nc.vector.tensor_scalar(M3[:, 0, :], src, -1.0, None, ALU.mult).then_inc(at["m3_link"], 1)
            dve.wait_ge(at["m3_link"], 3 * u + 1)
            nc.vector.scalar_tensor_tensor(MR[:, :], src, -1.0, M3[:, 0, :], ALU.mult, ALU.subtract).then_inc(at["b7_free"], 1)
            dve.wait_ge(at["b7_free"], 1 + b7_use(b, g, "m") + 1)
            nc.vector.tensor_copy(M3[:, 1, :], MR[:, :]).then_inc(at["m3_link"], 1)
            dve.wait_ge(at["m3_link"], 3 * u + 2)
            nc.vector.tensor_tensor(MR[:, :], MR[:, :], M3[:, 1, :], ALU.subtract).then_inc(at["m3_link"], 1)
            dve.wait_ge(at["m3_link"], 3 * u + 3)
            nc.vector.tensor_copy(M3[:, 2, :], MR[:, :]).then_inc(at["m3"], 1)

        def score_pe(pe, b, step):
            g, p = divmod(step, NP_)
            c, j, off, cols = PIECES[p]
            if p == 0:
                pe.wait_ge(at["m_row"], 16 * (4 * b + g + 1))
            for h in range(GH):
                n = step * GH + h
                pe.wait_ge(at["exp"], STEPS * GH * b + n + 1)
                q0 = c * C + off
                nc.tensor.matmul(STB[n % 3][:, 0:cols], STK[g % 2][0:ROWS, h, j * P:j * P + P],
                                 STQ[g % 2][0:ROWS, h, q0:q0 + cols], start=True, stop=True).then_inc(at["st"], 1)

        def exp_act(act, b, step):
            g, p = divmod(step, NP_)
            cols = PIECES[p][3]
            act.wait_ge(at["pv"], STEPS * b + step + 1)
            for h in range(GH):
                n = step * GH + h
                act.wait_ge(at["st"], STEPS * GH * b + n + 1)
                nc.scalar.activation(PR[:, n % (2 * GH), 0:cols], STB[n % 3][:, 0:cols], ACT.Exp,
                                     scale=SCORE_SCALE).then_inc(at["exp"], 1)

        DIAGS = sum(DIAG)

        def mask_pool(pool, b, step):
            g, p = divmod(step, NP_)
            if not DIAG[p]:
                return
            for h in range(GH):
                n = step * GH + h
                gate(pool, "pool", at["exp"], 3 + STEPS * GH * b + n + 1)
                blk = PR[:, n % (2 * GH), 0:P]
                nc.gpsimd.affine_select(out=blk, in_=blk, compare_op=ALU.is_ge, fill=0.0, base=0,
                                        pattern=[[1, P]], channel_multiplier=-1).then_inc(at["sel"], 1)

        def value_pe(pe, b, step):
            g, p = divmod(step, NP_)
            c, j, off, cols = PIECES[p]
            pe.wait_ge(at["exp"], 3 + STEPS * GH * b + (step + 1) * GH)
            if DIAG[p]:
                pe.wait_ge(at["sel"], (DIAGS * (NG * b + g) + sum(DIAG[:p + 1])) * GH)
            if j == 0:
                pe.wait_ge(at["ot"], 8 * b + 2 * g + c + 1)
            for h in range(GH):
                ins = nc.tensor.matmul(PVB[c][32 * h:32 * h + 32, off:C], V[:, j, g * GH + h, :],
                                       PR[:, (step * GH + h) % (2 * GH), 0:cols],
                                       start=(j == 0), stop=(j == 4 * c + 3), skip_group_check=True)
            ins.then_inc(at["pv"], 1)

        def outputs(step, lag):
            g, p = divmod(step - lag, NP_)
            return [(g, 0)] if p == 3 and g < NG else [(g, 1)] if p == NP_ - 1 and 0 <= g < NG else []

        def out_act(act, b, g, c):
            u = 8 * b + 2 * g + c
            act.wait_ge(at["pv"], 2 + STEPS * b + NP_ * g + (4 if c == 0 else NP_))
            act.wait_ge(at["b7"], u + 1)
            nc.scalar.activation(OT[:, c, :], PVB[c][:, :], ACT.Copy).then_inc(at["ot"], 1)

        def out_pe(pe, b, g, c):
            pe.wait_ge(at["ot"], 2 + 8 * b + 2 * g + c + 1)
            pe.wait_ge(at["b7_free"], b7_use(b, g, c) + 1)
            for t in range(4):
                ins = nc.tensor.transpose(B7[:, t * P:t * P + P], OT[:, c, t * P:t * P + P], ident)
            ins.then_inc(at["b7"], 1)

        def out_dve(dve, b, g, c):
            u = 8 * b + 2 * g + c
            dve.wait_ge(at["b7"], 2 + u + 1)
            o = B7[:, :].rearrange("p (t h d) -> p t h d", t=4, h=GH)
            nc.vector.reciprocal(RC[:, :, :], o[:, :, :, HD]).then_inc(at["a_link"], 1)
            dve.wait_ge(at["a_link"], u + 1)
            dst = A[:, 4 * c:4 * c + 4, g * GH * HD:(g + 1) * GH * HD].rearrange("p t (h d) -> p t h d", h=GH)
            nc.vector.tensor_tensor(dst, o[:, :, :, 0:HD], RC[:, :, :].unsqueeze(3).to_broadcast([P, 4, GH, HD]),
                                    ALU.mult).then_inc(at["b7_free"], 1)

        TAIL = 6
        ACT_LAG, PE_LAG, DVE_LAG = 2, 3, 4

        def groups_pe(pe, b):
            pe.wait_ge(at["qb"], 2 + 8 * b + 8)
            pe.wait_ge(at["v"], 2 + 8 * b + 8)
            for n in range(GH * len(MAXP)):
                max_pe(pe, b, 0, n)
            max_turn_pe(pe, b, 0)
            for step in range(STEPS + TAIL):
                if step < STEPS:
                    score_pe(pe, b, step)
                if 1 <= step <= STEPS:
                    value_pe(pe, b, step - 1)
                for g, n in max_pieces(step):
                    max_pe(pe, b, g, n)
                if step < STEPS - NP_ and step % NP_ == MAX_STEPS + 1:
                    max_turn_pe(pe, b, step // NP_ + 1)
                for g, c in outputs(step, PE_LAG):
                    out_pe(pe, b, g, c)

        def groups_act(act, b):
            for step in range(STEPS + TAIL):
                if step < STEPS:
                    exp_act(act, b, step)
                for g, c in outputs(step, ACT_LAG):
                    out_act(act, b, g, c)

        def groups_dve(dve, b):
            for n in range(GH * len(MAXP)):
                max_dve(dve, b, 0, n)
            max_join_dve(dve, b, 0)
            max_split_dve(dve, b, 0)
            for step in range(STEPS + TAIL):
                for g, n in max_pieces(step):
                    max_dve(dve, b, g, n)
                if step < STEPS - NP_ and step % NP_ == MAX_STEPS:
                    max_join_dve(dve, b, step // NP_ + 1)
                if step < STEPS - NP_ and step % NP_ == MAX_STEPS + 1:
                    max_split_dve(dve, b, step // NP_ + 1)
                for g, c in outputs(step, DVE_LAG):
                    out_dve(dve, b, g, c)

        def proj_pe(pe, b):
            pe.wait_ge(at["b7_free"], 1 + 12 * b + 12)
            pe.wait_ge(at["mx_red"], 2 + GH * len(MAXP) * (NG * b + NG))
            pe.wait_ge(at["exp"], 3 + STEPS * GH * (b + 1))
            pe.wait_ge(at["ot"], 2 + 8 * b + 8)
            turn_pe(pe, pj, A, b)
            pe.wait_ge(pj["lo"], 6 + 4 * b)
            for t in range(TPB):
                pe.wait_ge(pj["added"], 8 * b + t + 1)
                project(OPB[t % 2][:, 0:D], lambda a, d: XT[a][:, d, t * P:t * P + P],
                        lambda a, d: W[a][:, 3, d, :]).then_inc(pj["out"], 1)

        def proj_dve(dve, b):
            turn_dve(dve, pj, b)
            for t in range(TPB):
                dve.wait_ge(pj["out"], 8 * b + t + 1)
                nc.vector.tensor_tensor(xb(b, t), OPB[t % 2][:, 0:D], xb(b, t), ALU.add).then_inc(pj["added"], 1)
            dve.wait_ge(pj["added"], 2 + 8 * b + 8)
            nc.vector.tensor_tensor(xb(b), xb(b), BO[:, :].unsqueeze(1).to_broadcast([P, TPB, D]), ALU.add).then_inc(at["a_done"], 1)
            gate(dve, "dve", at["a_done"], 1 + b)

        FILLED = 16 * (SLOTS // CAP + 1)
        SETUP_DMAS = 16 * 11

        @block.sync
        def _(sp):
            for i, wt in enumerate((wq, wk, wv, wo)):
                sp.dma_start(A[:, 2 * i:2 * i + 2, :], wt.rearrange("(c p) n -> p c n", p=P)).then_inc(su["dma"], 16)
            sp.dma_start(XN[:, 0, 0:DH * NE].rearrange("p (c n) -> p c n", c=DH), router_w.rearrange("(c p) n -> p c n", p=P)).then_inc(su["dma"], 16)
            sp.dma_start(KC[:, :], consts).then_inc(su["dma"], 16)
            for m, v in enumerate((bq, bk)):
                sp.dma_start(BQK[:, m, :], v.rearrange("(c p) -> p c", p=P), allow_slow_non_contiguous=True).then_inc(su["dma"], 16)
            for buf, v in ((BV, bv), (BO, bo), (FB, fbias.rearrange("a b d -> (a b d)"))):
                sp.dma_start(buf[:, :], v.partition_broadcast(P)).then_inc(su["dma"], 16)
            with sp.Fori(0, NB) as b:
                sp.dma_start(xb(b), batch_tiles[bass.ds(b, 1), :, :, :].rearrange("o p t d -> p (o t) d")).then_inc(x_in, 16)
                gate(sp, "sp", x_in, 16 * b + 16)
            sp.wait_ge(su["zeros"], 1)
            for i in range(SLOTS // CAP):
                sp.dma_start(xe[i * CAP:(i + 1) * CAP, :].rearrange("(p r) d -> p r d", p=P), G[:, 0:NS, :]).then_inc(su["filled"], 16)
            sp.dma_start(ye[SLOTS:SLOTS + 1, :], G[0:1, 0, :]).then_inc(su["filled"], 16)
            sp.wait_ge(su["filled"], FILLED)
            sp.wait_ge(rt[0]["scattered"], SCATTERED * NB)
            ffn_sync(sp, 0)
            for k in range(TOPK):
                sp.wait_ge(ff[0][f"y_out{k}"], FFN_OUT)
            sp.dma_start(ROPE[:, :, :], rope.rearrange("a p n -> p a n")).then_inc(at["rope_in"], 16)
            with sp.Fori(0, NB) as b:
                att_sync(sp, b)
            sp.wait_ge(rt[1]["scattered"], SCATTERED * NB)
            ffn_sync(sp, 1)
            with sp.Fori(0, NB) as b:
                sp.wait_ge(cb[1]["x"], 1 + b)
                sp.dma_start(out_tiles[bass.ds(b, 1), :, :, :].rearrange("o p t d -> p (o t) d"), xb(b)).then_inc(out_done, 16)
            sp.wait_ge(out_done, 16 * NB)

        @block.tensor
        def _(pe):
            pe.wait_ge(su["split"], 6)
            with pe.Fori(0, NB) as b:
                turn_pe(pe, ln["r0"], XN, b)
                route_pe(pe, ln["r0"], rt[0], b)
            pe.wait_ge(rt[0]["route"], NB)
            ffn_pe(pe, 0)
            pe.wait_ge(at["const"], 1)
            with pe.Fori(0, NB) as b:
                turn_pe(pe, ln["att"], XN, b)
                qkv_pe(pe, b)
                groups_pe(pe, b)
                proj_pe(pe, b)
                turn_pe(pe, ln["r1"], XN, b)
                route_pe(pe, ln["r1"], rt[1], b)
            pe.wait_ge(rt[1]["route"], NB)
            ffn_pe(pe, 1)

        @block.scalar
        def _(act):
            for s, n in ((ff[0], 4), (ff[1], 4)):
                act.sem_inc(s["gelu"], n)
                act.sem_inc(s["y_evac"], 2)
                act.sem_inc(s["y_out0"], 16)
                act.sem_inc(s["y_out1"], 16)
            act.sem_inc(at["qb"], 2)
            act.sem_inc(at["exp"], 3)
            act.sem_inc(at["ot"], 2)
            act.wait_ge(su["dma"], SETUP_DMAS)
            nc.scalar.activation(WH[:, :, :, :].rearrange("p m d n -> p (m d) n"), A[:, :, :], ACT.Copy)
            nc.scalar.activation(RW[:, :, 0:NE], XN[:, 0, 0:DH * NE].rearrange("p (c n) -> p c n", c=DH), ACT.Copy).then_inc(su["act"], 1)
            with act.Fori(0, NB) as b:
                turn_act(act, ln["r0"], b)
                route_act(act, rt[0], b)
            ffn_act(act, 0)
            with act.Fori(0, NB) as b:
                turn_act(act, ln["att"], b)
                qk_act(act, b)
                groups_act(act, b)
                turn_act(act, pj, b)
                turn_act(act, ln["r1"], b)
                route_act(act, rt[1], b)
            ffn_act(act, 1)

        @block.vector
        def _(dve):
            for l in (*ln.values(), pj):
                dve.sem_inc(l["lo"], 2)
            for s in ff:
                dve.sem_inc(s["xe_lo"], 2)
                dve.sem_inc(s["h_lo"], 2)
            dve.sem_inc(at["v"], 2)
            dve.sem_inc(at["mx_red"], 2)
            dve.sem_inc(at["b7_free"], 1)
            dve.sem_inc(pj["added"], 2)
            nc.vector.memset(G[:, 0:NS, :], 0.0).then_inc(su["zeros"], 1)
            nc.vector.memset(ONES16[:, :], 1.0)
            nc.vector.memset(NEGHALF[:, :], -0.5)
            nc.vector.memset(CARRY[:, :, :], 0.0)
            nc.vector.memset(SLP[:, NB, :], 0.0)
            dve.wait_ge(su["act"], 1)
            for i, (dst, col) in enumerate(((ID16, K_ID), (LT16, K_LT), (MASK16, K_MASK))):
                nc.vector.tensor_copy(dst[:, :], KC[:, col:col + P]).then_inc(su["split"], 1)
            nc.vector.tensor_tensor(WL[:, :, :, :].rearrange("p m d n -> p (m d) n"), A[:, :, :],
                                    WH[:, :, :, :].rearrange("p m d n -> p (m d) n").bitcast(F32), ALU.subtract).then_inc(su["split"], 1)
            nc.vector.tensor_tensor(RW[:, :, NE:2 * NE], XN[:, 0, 0:DH * NE].rearrange("p (c n) -> p c n", c=DH),
                                    RW[:, :, 0:NE].bitcast(F32), ALU.subtract).then_inc(su["split"], 2)
            dve.wait_ge(su["split"], 6)
            with dve.Fori(0, NB) as b:
                gate(dve, "dve", x_in, 16 * b + 16)
                norm_dve(dve, ln["r0"], b)
                turn_dve(dve, ln["r0"], b)
                route_dve(dve, rt[0], b)
                dve.wait_ge(rt[0]["scattered"], SCATTERED * b + SCATTERED)
            ffn_dve(dve, 0)
            for k in range(TOPK):
                dve.wait_ge(ff[0][f"y_out{k}"], FFN_OUT)
            nc.vector.memset(CARRY[:, :, :], 0.0)
            nc.vector.memset(V[:, :, :, :], 0.0)
            nc.vector.memset(MX[:, :, :], 0.0).then_inc(at["const"], 1)
            dve.wait_ge(at["const"], 1)
            nc.vector.memset(V[:, :, :, HD:HD + 1], 1.0)
            for i in range(2):
                ins = nc.vector.memset(STK[i][STACK:ROWS, :, :], 1.0)
            ins.then_inc(at["const"], 1)
            dve.wait_ge(at["const"], 2)
            dve.wait_ge(at["rope_in"], 16)
            index_dve(dve, cb[0], 0)
            with dve.Fori(0, NB) as b:
                combine_dve(dve, cb[0], b)
                index_dve(dve, cb[0], b + 1)
                norm_dve(dve, ln["att"], b)
                turn_dve(dve, ln["att"], b)
                qkv_dve(dve, b)
                groups_dve(dve, b)
                proj_dve(dve, b)
                norm_dve(dve, ln["r1"], b)
                turn_dve(dve, ln["r1"], b)
                route_dve(dve, rt[1], b)
                dve.wait_ge(rt[1]["scattered"], SCATTERED * b + SCATTERED)
            ffn_dve(dve, 1)
            index_dve(dve, cb[1], 0)
            with dve.Fori(0, NB) as b:
                combine_dve(dve, cb[1], b)
                index_dve(dve, cb[1], b + 1)

        @block.gpsimd
        def _(pool):
            pool.sem_inc(at["cos"], 2)
            pool.sem_inc(at["p3"], 1)
            pool.sem_inc(at["parts_out0"], 16)
            pool.sem_inc(at["parts_out1"], 16)
            pool.sem_inc(at["pv"], 2)
            pool.sem_inc(at["m_done"], 1)
            pool.sem_inc(at["b7"], 2)
            for s in ff:
                pool.sem_inc(s["down"], 4)
            pool.wait_ge(su["split"], 6)
            with pool.Fori(0, NB) as b:
                norm_pool(pool, ln["r0"], b)
                pool.wait_ge(su["filled"], FILLED)
                route_pool(pool, rt[0], b)
            ffn_pool(pool, 0)
            for k in range(TOPK):
                pool.wait_ge(ff[0][f"y_out{k}"], FFN_OUT)
            gather_pool(pool, cb[0], 0)
            with pool.Fori(0, NB) as b:
                gather_pool(pool, cb[0], b + 1)
                norm_pool(pool, ln["att"], b)
                qk_pool(pool, b)
                for step in range(STEPS):
                    mask_pool(pool, b, step)
                norm_pool(pool, ln["r1"], b)
                route_pool(pool, rt[1], b)
            pool.wait_ge(cb[0]["gathered"], GATHERED * (NB + 1))
            ffn_pool(pool, 1)
            for k in range(TOPK):
                pool.wait_ge(ff[1][f"y_out{k}"], FFN_OUT)
            gather_pool(pool, cb[1], 0)
            with pool.Fori(0, NB) as b:
                gather_pool(pool, cb[1], b + 1)
            pool.wait_ge(cb[1]["gathered"], GATHERED * (NB + 1))


_INS = ["L0_attn_x", "L0_attn_wq", "L0_attn_bq", "L0_attn_wk", "L0_attn_bk", "L0_attn_wv", "L0_attn_bv",
        "L0_attn_wo", "L0_attn_bo", "L0_ffn_router_w", "L0_ffn_w1", "L0_ffn_w2", "L0_ffn_bias"]


def kernel(**inputs):
    import numpy as _np
    import concourse.bacc as _bacc
    from concourse import mybir as _mybir
    from concourse.bass_utils import run_bass_kernel_spmd as _run

    nc = _bacc.Bacc("TRN2", target_bir_lowering=False, num_devices=1)
    arrays, args = {}, []
    given = {name: _np.ascontiguousarray(inputs[name]) for name in _INS}
    given["shape_constants"] = shape_constants()
    given["rope_tables"] = rope_tables()
    for name, a in given.items():
        arrays[f"in_{name}_dram"] = a
        args.append(nc.dram_tensor(f"in_{name}_dram", a.shape, _mybir.dt.from_np(a.dtype), kind="ExternalInput").ap())
    args.append(nc.dram_tensor("out_0_dram", (NB, SEQ, D), _mybir.dt.float32, kind="ExternalOutput").ap())
    build(nc, *args)
    r = _run(nc, [arrays], core_ids=[0])
    return r.results[0]["out_0_dram"]
```

```python
from contextlib import ExitStack

import numpy as np
import concourse.bass as bass
from concourse import mybir

F32 = mybir.dt.float32
F32R = mybir.dt.float32r
BF16 = mybir.dt.bfloat16
U32 = mybir.dt.uint32
ALU = mybir.AluOpType
ACT = mybir.ActivationFunctionType
AX = mybir.AxisListType

P = 128
D = 256
DH = D // P
SEQ = 1024
NB = 4
TOK = NB * SEQ
TPB = SEQ // P
HEADS = 16
HD = D // HEADS
GH = 4
NG = HEADS // GH
NE = 8
TOPK = 2
CAP = TOK // NE
FFN = 1024
NF = FFN // P
NS = CAP // P
SLOTS = TOPK * TOK
C = 512
SCORE_SCALE = float(HD) ** -0.5
EPS = 1e-5
NEG = -1e30

Q_PARTS = (0, 0, 0, 1, 1, 2)
K_PARTS = (0, 1, 2, 0, 1, 0)
STACK = HD * len(Q_PARTS)
ROWS = STACK + 3

PIECES = [(c, j, max(0, P * j - C * c), C - max(0, P * j - C * c)) for c in range(2) for j in range(4 * (c + 1))]
DIAG = [j >= 4 * c for c, j, _, _ in PIECES]
NP_ = len(PIECES)
MAXP = [(h, q, c, min(C, P * (q + 1) - C * c)) for tiles in (range(4), range(4, TPB))
        for h in range(GH) for q in tiles for c in range(q // 4 + 1)]
MAX_N = len(MAXP)
MAX_EARLY = 4 * GH
MAX_FIRST, MAX_LAST = -2, 8
MAX_UPTO = {p: MAX_EARLY * (p + 3) // 4 if p < 2 else MAX_EARLY + (MAX_N - MAX_EARLY) * (p - 1) // (MAX_LAST - 1)
            for p in range(MAX_FIRST - 1, MAX_LAST + 1)}
STEPS = NG * NP_
VW = HD + 1
VPAD = 32 - VW

K_ID, K_LT, K_MASK, K_IOTA, K_OFF, K_END = 0, P, 2 * P, 3 * P, 3 * P + NE, 3 * P + NE + TOPK * TPB


def shape_constants():
    p = np.arange(P)
    k = np.zeros((P, K_END), np.float32)
    k[:, K_ID:K_ID + P] = np.eye(P)
    k[:, K_LT:K_LT + P] = p[:, None] < p[None, :]
    k[:, K_MASK:K_MASK + P] = np.where(p[None, :] > p[:, None], NEG, 0.0)
    k[:, K_IOTA:K_IOTA + NE] = np.arange(NE)
    k[:, K_OFF:K_END] = np.repeat(np.arange(TOPK) * TOK - SLOTS, TPB)
    return k


def rope_tables():
    one = np.float32(1.0)
    inv = one / np.float32(10000.0) ** (np.arange(0, HD, 2, dtype=np.float32) / np.float32(HD))
    angle = inv[:, None] * np.arange(SEQ, dtype=np.float32)[None, :]
    pair = (np.arange(P) % HD) // 2
    sign = np.where(np.arange(P) % 2 == 0, -one, one)[:, None]
    return np.stack([np.cos(angle)[pair], np.sin(angle)[pair] * sign]).astype(np.float32)


class Link:

    def __init__(self, eng, sem, base=0):
        self.eng, self.sem, self.base, self.n = eng, sem, base, 0

    def add(self, ins):
        ins.then_inc(self.sem, 1)
        self.n += 1

    def sync(self):
        self.eng.wait_ge(self.sem, self.base + self.n)


def build(nc, x, wq, bq, wk, bk, wv, bv, wo, bo, router_w, w1, w2, fbias, consts, rope, out):
    ctx = ExitStack()
    with ctx:
        def sb(name, shape, dt, where=ctx):
            return where.enter_context(nc.sbuf_tensor(name, shape, dt))

        def sem(name):
            return ctx.enter_context(nc.semaphore(name))

        def sems(prefix, names):
            return {n: sem(f"{prefix}_{n}") for n in names.split()}

        bank = [ctx.enter_context(nc.psum_tensor(f"bank{i}", [P, C], F32)) for i in range(8)]

        xe = nc.dram_tensor("expert_rows", [SLOTS, D], F32, kind="Internal").ap()
        ye = nc.dram_tensor("expert_out", [SLOTS + 1, D], F32, kind="Internal").ap()
        qkd = nc.dram_tensor("qk_parts", [NB, 3, 2, D, SEQ], BF16, kind="Internal").ap()
        md = nc.dram_tensor("max_rows", [3, GH * TPB, P], BF16, kind="Internal").ap()

        X = sb("X", [P, NB * TPB, D], F32)
        XN = sb("XN", [P, TPB, D], F32)
        XTH = sb("XTH", [P, DH, SEQ], F32R)
        XTL = sb("XTL", [P, DH, SEQ], F32R)
        WH = sb("WH", [P, 4, DH, D], F32R)
        WL = sb("WL", [P, 4, DH, D], F32R)
        RW = sb("RW", [P, DH, 2 * NE], F32R)
        KC = sb("KC", [P, K_END], F32)
        ID16 = sb("ID16", [P, P], BF16)
        LT16 = sb("LT16", [P, P], BF16)
        MASK16 = sb("MASK16", [P, P], BF16)
        ONES16 = sb("ONES16", [P, P], BF16)
        BQK = sb("BQK", [P, 2, DH], F32)
        BV = sb("BV", [P, D], F32)
        BO = sb("BO", [P, D], F32)
        FB = sb("FB", [P, D], F32)
        NEGHALF = sb("NEGHALF", [P, TPB], F32)
        BST = sb("BST", [P, TPB, 6], F32)
        MV = sb("MV", [P, TPB, 2], F32)
        VE = sb("VE", [P, TPB], F32)
        RSTD = sb("RSTD", [P, TPB], F32)
        LA = sb("LA", [P, TPB, NE], F32)
        LG = sb("LG", [P, TPB, NE], F32)
        TOP = sb("TOP", [P, TPB, 8], F32)
        TIX = sb("TIX", [P, TPB, 8], U32)
        IDXF = sb("IDXF", [P, TOPK, TPB], F32)
        OH = sb("OH", [P, TOPK, TPB, NE], BF16)
        DL = sb("DL", [P, TPB, NE], F32)
        DW = sb("DW", [P, TOPK, TPB], F32)
        EL = sb("EL", [P, TPB, NE], F32)
        EW = sb("EW", [P, TOPK, TPB], F32)
        SUM = sb("SUM", [P, TPB], F32)
        RS = sb("RS", [P, TPB], F32)
        WV_ = sb("WV_", [P, TOPK, TPB], F32)
        TOT = sb("TOT", [P, TOPK, TPB, NE], F32)
        PX = sb("PX", [P, TOPK, TPB, NE], F32)
        CARRY = sb("CARRY", [P, TOPK, NE], F32)
        RANK = sb("RANK", [P, TOPK, TPB, NE], F32)
        SEL = sb("SEL", [P, TOPK, TPB, NE], F32)
        RK = sb("RK", [P, TOPK, TPB], F32)
        OK = sb("OK", [P, TOPK, TPB], F32)
        SL = sb("SL", [P, TOPK, TPB], F32)
        SL2 = sb("SL2", [P, TOPK, TPB], F32)
        SLT = sb("SLT", [P, TOPK * TPB], U32)
        GIX = sb("GIX", [P, TOPK * TPB], U32)
        GIXF = [sb(f"GIXF{i}", [P, TOPK * TPB], U32) for i in range(2)]
        SLP = sb("SLP", [P, NB + 2, TOPK * TPB], U32)
        WP = sb("WP", [P, NB, TOPK * TPB], F32)

        fctx = ExitStack()
        WRAW1 = sb("WRAW1", [P, DH, FFN], F32, fctx)
        WRAW2 = sb("WRAW2", [P, NF, D], F32, fctx)
        W1H = sb("W1H", [P, DH, FFN], F32R, fctx)
        W1L = sb("W1L", [P, DH, FFN], F32R, fctx)
        W2H = sb("W2H", [P, NF, D], F32R, fctx)
        W2L = sb("W2L", [P, NF, D], F32R, fctx)
        XR = [sb(f"XR{k}", [P, NS, D], F32, fctx) for k in range(TOPK)]
        XEH = [sb(f"XEH{k}", [P, DH, CAP], F32R, fctx) for k in range(TOPK)]
        XEL = [sb(f"XEL{k}", [P, DH, CAP], F32R, fctx) for k in range(TOPK)]
        GE = sb("GE", [P, 2, C], F32, fctx)
        HH = sb("HH", [P, 4, C], F32R, fctx)
        HL = sb("HL", [P, 4, C], F32R, fctx)
        YS = [sb(f"YS{k}", [P, NS, D], F32, fctx) for k in range(TOPK)]
        fctx.close()
        gctx = ExitStack()
        GF = [[sb(f"GF{i}{c}", [P, TPB, D], F32, gctx) for c in range(TOPK)] for i in range(2)]
        gctx.close()
        actx = ctx
        G = sb("G", [P, TPB, D], F32, actx)
        ROPE = sb("ROPE", [P, 2, SEQ], F32, actx)
        STQ = [sb(f"STQ{i}", [ROWS, GH, SEQ], BF16, actx) for i in range(2)]
        STK = [sb(f"STK{i}", [ROWS, GH, SEQ], BF16, actx) for i in range(2)]
        PR = sb("PR", [P, 2 * GH, C], F32, actx)
        V = sb("V", [P, TPB, HEADS * VW + VPAD], F32, actx)
        VN = sb("VN", [P, TPB, HEADS * VW + VPAD], F32, actx)
        QB = sb("QB", [P, 2, C], F32, actx)
        QS = sb("QS", [P, 3, C], F32, actx)
        QC = sb("QC", [P, 2, C], F32, actx)
        PT = sb("PT", [P, 3, 3, C], BF16, actx)
        MX = sb("MX", [P, 2, P], F32, actx)
        MR = sb("MR", [GH * TPB, P], F32, actx)
        M3 = sb("M3", [GH * TPB, 3, P], BF16, actx)
        OT = sb("OT", [P, 2, C], F32, actx)
        RC = sb("RC", [P, 4, GH], F32, actx)
        A = sb("A", [P, TPB, D], F32, actx)

        XNS, SLTS = (XN, A), (SLT, GIX)
        ident = KC[:, K_ID:K_ID + P]

        passed = {}

        def gate(eng, name, sem_, value):
            eng.wait_ge(sem_, value)
            eng.sem_inc(passed[name], 1)

        su = sems("setup", "dma split raw_used zeros filled act dve pool")
        x_in, out_done = sem("x_in"), sem("out_done")
        LN_SEMS = "link stats rstd_link rstd xn tp hi lo"
        RT_SEMS = "logits lg rank link oh diff exps ranks route scattered sent"
        ln = {n: sems(f"ln_{n}", LN_SEMS) for n in ("r0", "att", "r1")}
        pj = sems("proj", "tp hi lo out added")
        rt = {n: sems(f"rt{n}", RT_SEMS) for n in range(2)}
        ff = [sems(f"ffn{n}", "w_in xe_in0 xe_in1 w1_hi w2_hi w1_lo w2_lo xe_tp xe_hi xe_lo "
                              "up gelu h_hi h_lo down y_evac y_out0 y_out1") for n in range(2)]
        cb = [sems(f"comb{n}", "index0 index1 index gathered gathered0 gathered1 link x") for n in range(2)]
        at = sems("att", "rope_in const qkv qb swap cos sin rot p1 low p2 p3 parts_out0 parts_out1 parts_out2 v_ps vn v stk_in00 stk_in01 stk_in10 stk_in11 "
                         "mx_ps mx_red m_link m_done m3_link m3 m_out m_row st exp sel pv ot b7 b7_free a_link a_done")

        passed.update(dve=sem("dve_passed"), pool=sem("pool_passed"), sp=sem("sp_passed"))

        block = ctx.enter_context(nc.Block())
        batch_tiles = x.rearrange("b (t p) d -> b p t d", p=P)
        out_tiles = out.rearrange("b (t p) d -> b p t d", p=P)

        def xb(b, t=None):
            if t is None:
                return X[:, bass.ds(b * TPB, TPB), :]
            return X[:, bass.ds(b * TPB + t, 1), :].rearrange("p o d -> p (o d)")

        def stats_dve(dve, s, b):
            for t in range(TPB):
                ins = nc.vector.bn_stats(BST[:, t, :], xb(b, t))
            ins.then_inc(s["link"], 1)
            gate(dve, "dve", s["link"], 1 + b)
            for t in range(TPB):
                ins = nc.vector.bn_aggr(MV[:, t, :], BST[:, t, :])
            ins.then_inc(s["stats"], 1)

        def norm_dve(dve, s, b, xn=XN):
            dve.wait_ge(s["rstd"], 1 + b)
            for t in range(TPB):
                nc.vector.tensor_scalar(xn[:, t, :], xb(b, t), MV[:, t, 0:1], RSTD[:, t:t + 1],
                                        ALU.subtract, ALU.mult).then_inc(s["xn"], 1)

        def norm_pool(pool, s, b):
            gate(pool, "pool", s["stats"], 1 + b)
            nc.gpsimd.tensor_scalar(VE[:, :], MV[:, :, 1], EPS, None, ALU.add).then_inc(s["rstd_link"], 1)
            pool.wait_ge(s["rstd_link"], 1 + b)
            nc.gpsimd.tensor_tensor(RSTD[:, :], VE[:, :], NEGHALF[:, :], ALU.pow).then_inc(s["rstd"], 1)

        def turn_pe(s, src, i, bk):
            for d in range(DH):
                for t in range(2):
                    ins = nc.tensor.transpose(bk[:, d * 2 * P + t * P:d * 2 * P + t * P + P],
                                              src[:, 2 * i + t, d * P:d * P + P], ident)
            ins.then_inc(s["tp"], 1)

        def turn_act(act, s, b, i, bk):
            act.wait_ge(s["tp"], 1 + i + 4 * b)
            nc.scalar.activation(XTH[:, :, i * 2 * P:(i + 1) * 2 * P],
                                 bk[:, :].rearrange("p (d n) -> p d n", d=DH), ACT.Copy).then_inc(s["hi"], 1)

        def turn_dve(dve, s, b, i, bk):
            dve.wait_ge(s["hi"], 1 + i + 4 * b)
            cols = slice(i * 2 * P, (i + 1) * 2 * P)
            nc.vector.tensor_tensor(XTL[:, :, cols], bk[:, :].rearrange("p (d n) -> p d n", d=DH),
                                    XTH[:, :, cols].bitcast(F32), ALU.subtract).then_inc(s["lo"], 1)

        def logit_pe(s, bk):
            for t in range(TPB):
                tok = slice(t * P, t * P + P)
                o = bk[:, t * 2 * NE:(t + 1) * 2 * NE]
                for d in range(DH):
                    nc.tensor.matmul(o, XTH[:, d, tok], RW[:, d, :], start=(d == 0), stop=False, skip_group_check=True)
                for d in range(DH):
                    ins = nc.tensor.matmul(o[:, 0:NE], XTL[:, d, tok], RW[:, d, 0:NE], start=False, stop=(d == 1),
                                           skip_group_check=True)
            ins.then_inc(s["logits"], 1)

        def rank_pe(pe, s, b, bk):
            pe.wait_ge(s["oh"], 1 + b)
            oh = OH[:, :, :, :].rearrange("p k t e -> p (k t e)")
            n = TOPK * TPB * NE
            nc.tensor.matmul(bk[:, 0:n], LT16[:, :], oh, start=True, stop=True)
            nc.tensor.matmul(bk[:, n:2 * n], ONES16[:, :], oh, start=True, stop=True).then_inc(s["ranks"], 1)

        def route_act(act, s, b):
            act.wait_ge(s["diff"], 1 + b)
            nc.scalar.activation(EL[:, :, :], DL[:, :, :], ACT.Exp)
            nc.scalar.activation(EW[:, :, :], DW[:, :, :], ACT.Exp).then_inc(s["exps"], 1)

        CHOICE_LINKS, SLOT_LINKS = 4, 20

        def choice_dve(dve, s, b, bk):
            k = Link(dve, s["link"], b * (CHOICE_LINKS + SLOT_LINKS))
            dve.wait_ge(s["logits"], 1 + b)
            logit = bk[:, 0:TPB * 2 * NE].rearrange("p (t e) -> p t e", t=TPB)
            k.add(nc.vector.tensor_copy(LA[:, :, :], logit[:, :, NE:]))
            k.sync()
            nc.vector.tensor_tensor(LG[:, :, :], logit[:, :, 0:NE], LA[:, :, :], ALU.add).then_inc(s["lg"], 1)
            gate(dve, "dve", s["lg"], 1 + b)
            for t in range(TPB):
                ins = nc.vector.max(TOP[:, t, :], LG[:, t, :])
            k.add(ins)
            gate(dve, "dve", s["link"], k.base + k.n)
            for t in range(TPB):
                ins = nc.vector.max_index(TIX[:, t, :], TOP[:, t, :], LG[:, t, :])
            k.add(ins)
            k.sync()
            k.add(nc.vector.tensor_copy(IDXF[:, :, :], TIX[:, :, 0:TOPK].rearrange("p t k -> p k t")))
            k.sync()
            iota = KC[:, K_IOTA:K_IOTA + NE].unsqueeze(1).to_broadcast([P, TPB, NE])
            for c in range(TOPK):
                ins = nc.vector.tensor_tensor(OH[:, c, :, :], IDXF[:, c, :].unsqueeze(2).to_broadcast([P, TPB, NE]),
                                              iota, ALU.is_equal)
            ins.then_inc(s["oh"], 1)
            nc.vector.tensor_tensor(DL[:, :, :], LG[:, :, :], TOP[:, :, 0:1].to_broadcast([P, TPB, NE]), ALU.subtract)
            for c in range(TOPK):
                ins = nc.vector.tensor_tensor(DW[:, c, :], TOP[:, :, c], TOP[:, :, 0], ALU.subtract)
            ins.then_inc(s["diff"], 1)
            assert k.n == CHOICE_LINKS, k.n

        def slot_dve(dve, s, b, bk, slt=SLT):
            k = Link(dve, s["link"], b * (CHOICE_LINKS + SLOT_LINKS) + CHOICE_LINKS)
            n = TOPK * TPB * NE
            dve.wait_ge(s["ranks"], 1 + b)
            k.add(nc.vector.tensor_copy(TOT[:, :, :, :].rearrange("p k t e -> p (k t e)"), bk[:, n:2 * n]))
            k.add(nc.vector.tensor_copy(PX[:, :, 0, :], CARRY[:, :, :]))
            k.sync()
            for t in range(1, TPB):
                k.add(nc.vector.tensor_tensor(PX[:, :, t, :], PX[:, :, t - 1, :], TOT[:, :, t - 1, :], ALU.add))
                k.sync()
            k.add(nc.vector.tensor_tensor(CARRY[:, :, :], PX[:, :, TPB - 1, :], TOT[:, :, TPB - 1, :], ALU.add))
            nc.vector.tensor_tensor(RANK[:, :, :, :].rearrange("p k t e -> p (k t e)"), bk[:, 0:n],
                                    PX[:, :, :, :].rearrange("p k t e -> p (k t e)"), ALU.add).then_inc(s["rank"], 1)
            dve.wait_ge(s["rank"], 1 + b)
            k.add(nc.vector.tensor_tensor(SEL[:, :, :, :].rearrange("p k t e -> p (k t e)"),
                                          RANK[:, :, :, :].rearrange("p k t e -> p (k t e)"),
                                          OH[:, :, :, :].rearrange("p k t e -> p (k t e)"), ALU.mult))
            k.sync()
            k.add(nc.vector.tensor_reduce(RK[:, :, :], SEL[:, :, :, :], AX.X, ALU.add))
            k.sync()
            k.add(nc.vector.tensor_scalar(OK[:, :, :], RK[:, :, :], float(CAP), None, ALU.is_lt))
            k.add(nc.vector.scalar_tensor_tensor(SL[:, :, :], IDXF[:, :, :], float(CAP), RK[:, :, :], ALU.mult, ALU.add))
            k.sync()
            k.add(nc.vector.tensor_tensor(SL2[:, :, :].rearrange("p k t -> p (k t)"), SL[:, :, :].rearrange("p k t -> p (k t)"),
                                          KC[:, K_OFF:K_END], ALU.add))
            k.sync()
            k.add(nc.vector.tensor_tensor(SL[:, :, :], SL2[:, :, :], OK[:, :, :], ALU.mult))
            k.sync()
            flat = SL[:, :, :].rearrange("p k t -> p (k t)")
            k.add(nc.vector.tensor_scalar(SLP[:, bass.ds(b, 1), :].rearrange("p o n -> p (o n)"), flat, float(SLOTS), None, ALU.add))
            nc.vector.tensor_scalar(slt[:, :], flat, float(SLOTS), None, ALU.add).then_inc(s["route"], 1)
            dve.wait_ge(s["exps"], 1 + b)
            k.add(nc.vector.tensor_reduce(SUM[:, :], EL[:, :, :], AX.X, ALU.add))
            k.sync()
            k.add(nc.vector.reciprocal(RS[:, :], SUM[:, :]))
            k.sync()
            for c in range(TOPK):
                ins = nc.vector.tensor_tensor(WV_[:, c, :], EW[:, c, :], RS[:, :], ALU.mult)
            k.add(ins)
            k.sync()
            nc.vector.scalar_tensor_tensor(WP[:, bass.ds(b, 1), :].rearrange("p o n -> p (o n)"),
                                           WV_[:, :, :].rearrange("p k t -> p (k t)"), 0.5,
                                           OK[:, :, :].rearrange("p k t -> p (k t)"), ALU.mult, ALU.mult)
            assert k.n == SLOT_LINKS, k.n

        def route_pool(pool, s, b, xn=XN, slt=SLT):
            gate(pool, "pool", s["route"], 1 + b)
            for c in range(TOPK):
                for t in range(TPB):
                    nc.gpsimd.indirect_dma_start(
                        out=xe[:, :], out_offset=bass.IndirectOffsetOnAxis(ap=slt[:, c * TPB + t:c * TPB + t + 1], axis=0),
                        in_=xn[:, t, :], in_offset=None, bounds_check=SLOTS - 1, oob_is_err=False,
                    ).then_inc(s["scattered"], 16)

        SCATTERED = 16 * TOPK * TPB

        Y, UP, XTP = [bank[0], bank[1]], [bank[2], bank[3], bank[4], bank[5]], [bank[6], bank[7]]

        def ffn_sync(sp, ph):
            s = ff[ph]
            with sp.Fori(0, NE) as e:
                sp.dma_start(WRAW1[:, :, :], w1[bass.ds(e, 1), :, :].rearrange("o (c p) f -> p (o c) f", p=P)).then_inc(s["w_in"], 16)
                sp.dma_start(WRAW2[:, :, :], w2[bass.ds(e, 1), :, :].rearrange("o (c p) f -> p (o c) f", p=P)).then_inc(s["w_in"], 16)
                for k in range(TOPK):
                    rows = xe[bass.ds(e * CAP + k * TOK, CAP), :].rearrange("(s p) d -> p s d", p=P)
                    sp.dma_start(XR[k][:, :, :], rows).then_inc(s[f"xe_in{k}"], 16)
                sp.wait_ge(s["w1_lo"], NF * e + NF)
                sp.wait_ge(s["w2_lo"], NF * e + NF)
                sp.wait_ge(s["w1_hi"], NF * e + NF)
                sp.wait_ge(s["w2_hi"], NF * e + NF)
                gate(sp, "sp", s["xe_tp"], 2 * TOPK * e + 2 * TOPK)

        def xe_pe(pe, s, e, k):
            pe.wait_ge(s[f"xe_in{k}"], 16 * e + 16)
            for d in range(DH):
                pe.wait_ge(s["xe_lo"], 4 * e + 2 * k + d + 1)
                for t in range(NS):
                    ins = nc.tensor.transpose(XTP[d][:, t * P:t * P + P], XR[k][:, t, d * P:d * P + P], ident)
                ins.then_inc(s["xe_tp"], 1)

        def xe_act(act, s, e, k):
            for d in range(DH):
                act.wait_ge(s["xe_tp"], 4 * e + 2 * k + d + 1)
                nc.scalar.activation(XEH[k][:, d, :], XTP[d][:, :], ACT.Copy).then_inc(s["xe_hi"], 1)

        def xe_dve(dve, s, e, k):
            for d in range(DH):
                dve.wait_ge(s["xe_hi"], 4 * e + 2 * k + d + 1)
                nc.vector.tensor_tensor(XEL[k][:, d, :], XTP[d][:, :], XEH[k][:, d, :].bitcast(F32),
                                        ALU.subtract).then_inc(s["xe_lo"], 1)

        def block_pe(pe, s, e, k, last):
            n8 = 2 * NF * e + NF * k
            pe.wait_ge(s["xe_lo"], 4 * e + 2 * k + 4)

            def up(f):
                pe.wait_ge(s["gelu"], n8 + f + 1)
                pe.wait_ge(s["w1_hi"], NF * e + f + 1)
                pe.wait_ge(s["w1_lo"], NF * e + f + 1)
                cols = slice(f * P, f * P + P)
                ops = [(w, a, d) for w, a in ((W1H, XEH), (W1H, XEL), (W1L, XEH)) for d in range(DH)]
                for i, (w, a, d) in enumerate(ops):
                    ins = nc.tensor.matmul(UP[f % 4][:, :], w[:, d, cols], a[k][:, d, :], start=(i == 0), stop=(i == len(ops) - 1))
                ins.then_inc(s["up"], 1)

            def down(f):
                pe.wait_ge(s["h_lo"], 2 + n8 + f + 1)
                pe.wait_ge(s["w2_hi"], NF * e + f + 1)
                pe.wait_ge(s["w2_lo"], NF * e + f + 1)
                for t in range(NS):
                    if f == 0 and t % 2 == 0:
                        pe.wait_ge(s["y_evac"], 4 * e + 2 * k + t // 2 + 1)
                    o = Y[t // 2][:, (t % 2) * D:(t % 2 + 1) * D]
                    rows = slice(t * P, t * P + P)
                    for i, (h, w) in enumerate(((HH, W2H), (HL, W2H), (HH, W2L))):
                        ins = nc.tensor.matmul(o, h[:, f % 4, rows], w[:, f, :], start=(f == 0 and t % 2 == 0 and i == 0),
                                               stop=(f == NF - 1 and i == 2), skip_group_check=True)
                ins.then_inc(s["down"], 1)

            for f in range(NF + 2):
                if f < NF:
                    up(f)
                if f >= 2:
                    down(f - 2)
                if f == 3:
                    if k == 0:
                        xe_pe(pe, s, e, 1)
                    elif not last:
                        xe_pe(pe, s, e + 1, 0)

        def w1_hi(s, f):
            cols = slice(f * P, f * P + P)
            nc.scalar.activation(W1H[:, :, cols], WRAW1[:, :, cols], ACT.Copy).then_inc(s["w1_hi"], 1)

        def w2_hi(s, f):
            nc.scalar.activation(W2H[:, f, :], WRAW2[:, f, :], ACT.Copy).then_inc(s["w2_hi"], 1)

        def block_act(act, s, e, k, last):
            n8 = 2 * NF * e + NF * k
            split_next = k == TOPK - 1 and not last
            if split_next:
                act.wait_ge(s["w_in"], 32 * e + 64)
            for f in range(NF + 3):
                if f < NF:
                    act.wait_ge(s["up"], n8 + f + 1)
                    act.wait_ge(s["h_lo"], n8 + f + 1)
                    nc.scalar.activation(GE[:, f % 2, :], UP[f % 4][:, :], ACT.Gelu_apprx_tanh).then_inc(s["gelu"], 1)
                    if split_next:
                        w1_hi(s, f)
                if f >= 3 and split_next:
                    act.wait_ge(s["down"], 4 + n8 + f - 2)
                    w2_hi(s, f - 3)
                if f == 3:
                    if k == 0:
                        xe_act(act, s, e, 1)
                    elif not last:
                        xe_act(act, s, e + 1, 0)
            act.wait_ge(s["down"], 4 + n8 + NF)
            act.wait_ge(s[f"y_out{k}"], 16 * e + 16)
            for i in range(2):
                nc.scalar.activation(YS[k][:, 2 * i:2 * i + 2, :], Y[i][:, :].rearrange("p (t n) -> p t n", t=2),
                                     ACT.Copy).then_inc(s["y_evac"], 1)
            act.wait_ge(s["y_evac"], 4 + 4 * e + 2 * k)
            act.dma_start(ye[bass.ds(e * CAP + k * TOK, CAP), :].rearrange("(s p) d -> p s d", p=P),
                          YS[k][:, :, :]).then_inc(s[f"y_out{k}"], 16)

        def block_dve(dve, s, e, k, last):
            n8 = 2 * NF * e + NF * k
            for f in range(NF):
                dve.wait_ge(s["gelu"], 4 + n8 + f + 1)
                dve.wait_ge(s["down"], n8 + f + 1)
                nc.vector.tensor_copy(HH[:, f % 4, :], GE[:, f % 2, :]).then_inc(s["h_hi"], 1)
                dve.wait_ge(s["h_hi"], n8 + f + 1)
                nc.vector.tensor_tensor(HL[:, f % 4, :], GE[:, f % 2, :], HH[:, f % 4, :].bitcast(F32),
                                        ALU.subtract).then_inc(s["h_lo"], 1)
                if f == 3:
                    if k == 0:
                        xe_dve(dve, s, e, 1)
                    elif not last:
                        xe_dve(dve, s, e + 1, 0)

        def split_pool(pool, s, e):
            for f in range(NF):
                cols = slice(f * P, f * P + P)
                pool.wait_ge(s["w1_hi"], NF * e + f + 1)
                nc.gpsimd.tensor_tensor(W1L[:, :, cols], WRAW1[:, :, cols], W1H[:, :, cols].bitcast(F32),
                                        ALU.subtract).then_inc(s["w1_lo"], 1)
                pool.wait_ge(s["w2_hi"], NF * e + f + 1)
                nc.gpsimd.tensor_tensor(W2L[:, f, :], WRAW2[:, f, :], W2H[:, f, :].bitcast(F32),
                                        ALU.subtract).then_inc(s["w2_lo"], 1)

        def ffn_pe(pe, ph):
            s = ff[ph]
            xe_pe(pe, s, 0, 0)
            with pe.Fori(0, NE - 1) as e:
                for k in range(TOPK):
                    block_pe(pe, s, e, k, False)
            for k in range(TOPK):
                block_pe(pe, s, NE - 1, k, True)

        def ffn_act(act, ph):
            s = ff[ph]
            act.wait_ge(s["w_in"], 32)
            for f in range(NF):
                w1_hi(s, f)
                w2_hi(s, f)
            xe_act(act, s, 0, 0)
            with act.Fori(0, NE - 1) as e:
                for k in range(TOPK):
                    block_act(act, s, e, k, False)
            for k in range(TOPK):
                block_act(act, s, NE - 1, k, True)

        def ffn_dve(dve, ph):
            s = ff[ph]
            xe_dve(dve, s, 0, 0)
            with dve.Fori(0, NE - 1) as e:
                for k in range(TOPK):
                    block_dve(dve, s, e, k, False)
            for k in range(TOPK):
                block_dve(dve, s, NE - 1, k, True)

        def ffn_pool(pool, ph):
            with pool.Fori(0, NE) as e:
                split_pool(pool, ff[ph], e)

        FFN_OUT = 16 + 16 * NE

        def index_dve(s, index, b):
            nc.vector.tensor_copy(index[:, :], SLP[:, bass.ds(b, 1), :].rearrange("p o n -> p (o n)")).then_inc(s["index"], 1)

        GATHERED = 16 * TPB

        def gather_pool(pool, sem_, dst, index, c):
            for t in range(TPB):
                n = c * TPB + t
                nc.gpsimd.indirect_dma_start(
                    out=dst[:, t, :], out_offset=None, in_=ye[:, :],
                    in_offset=bass.IndirectOffsetOnAxis(ap=index[:, n:n + 1], axis=0),
                ).then_inc(sem_, 16)

        def gather_first_pool(pool, b):
            gate(pool, "pool", cb[0]["index"], 1 + b)
            gather_pool(pool, cb[0]["gathered"], G, GIX, 0)

        def gather_second_pool(pool, b):
            gate(pool, "pool", cb[0]["link"], 2 * b + 1)
            gather_pool(pool, cb[0]["gathered"], G, GIX, 1)

        def add_rows_dve(src, s, b, c, tiles):
            for t in tiles:
                ins = nc.vector.scalar_tensor_tensor(
                    xb(b, t), src[:, t, :], WP[:, bass.ds(b, 1), c * TPB + t:c * TPB + t + 1].rearrange("p o n -> p (o n)"),
                    xb(b, t), ALU.mult, ALU.add)
            if tiles[-1] == TPB - 1:
                ins.then_inc(s["link"], 1)

        def combine_dve(dve, b, part):
            c = part // 2
            if part % 2 == 0:
                dve.wait_ge(cb[0]["gathered"], GATHERED * (2 * b + c + 1))
            if part == 2:
                dve.wait_ge(cb[0]["link"], 2 * b + 1)
            add_rows_dve(G, cb[0], b, c, range(4 * (part % 2), 4 * (part % 2) + 4))

        def combine_pool(pool, s, b):
            pool.wait_ge(s["link"], 2 * b + 2)
            nc.gpsimd.tensor_tensor(xb(b), xb(b), FB[:, :].unsqueeze(1).to_broadcast([P, TPB, D]), ALU.add).then_inc(s["x"], 1)

        MAXB, STB, PVB, AUX, B7 = [bank[0], bank[1], bank[5]], [bank[2], bank[3]], bank[4], bank[6], bank[7]
        QK = [(m, h, c) for h in range(DH) for m in range(2) for c in range(2)]
        PAIR_SWAP = [i ^ 1 for i in range(32)]

        def project(o, lhs, rhs):
            ops = [(a, c, d) for a, c in ((0, 0), (1, 0), (0, 1)) for d in range(DH)]
            for i, (a, c, d) in enumerate(ops):
                ins = nc.tensor.matmul(o, lhs(a, d), rhs(c, d), start=(i == 0), stop=(i == len(ops) - 1))
            return ins

        XT = (XTH, XTL)
        W = (WH, WL)

        def qk_pe(b, i):
            m, h, c = QK[i]
            project(AUX[:, :], lambda a, d: W[a][:, m, d, h * P:h * P + P],
                    lambda a, d: XT[a][:, d, c * C:c * C + C]).then_inc(at["qkv"], 1)

        def qk_act(act, b, i):
            m, h, c = QK[i]
            act.wait_ge(at["qkv"], 8 * b + i + 1)
            act.wait_ge(at["cos"], 8 * b + i + 1)
            nc.scalar.activation(QB[:, i % 2, :], AUX[:, :], ACT.Identity, bias=BQK[:, m, h:h + 1]).then_inc(at["qb"], 1)

        def qk_dve(dve, b, i):
            m, h, c = QK[i]
            r = QS[:, i % 3, :]
            dve.wait_ge(at["p3"], 8 * b + i + 1)
            gate(dve, "dve", at["qb"], 8 * b + i + 1)
            nc.vector.stream_shuffle(r, QB[:, i % 2, :], PAIR_SWAP).then_inc(at["swap"], 1)
            dve.wait_ge(at["swap"], 8 * b + i + 1)
            nc.vector.tensor_tensor(r, r, ROPE[:, 1, c * C:c * C + C], ALU.mult).then_inc(at["sin"], 1)

        def rotate_pool(pool, b, i):
            m, h, c = QK[i]
            q = QC[:, i % 2, :]
            pool.wait_ge(at["swap"], 8 * b + i + 1)
            pool.wait_ge(at["low"], 8 * b + i + 1)
            nc.gpsimd.tensor_tensor(q, QB[:, i % 2, :], ROPE[:, 0, c * C:c * C + C], ALU.mult).then_inc(at["cos"], 1)
            pool.wait_ge(at["cos"], 2 + 8 * b + i + 1)
            pool.wait_ge(at["sin"], 8 * b + i + 1)
            nc.gpsimd.tensor_tensor(q, q, QS[:, i % 3, :], ALU.add).then_inc(at["rot"], 1)

        def part1_act(act, b, i):
            act.wait_ge(at["rot"], 8 * b + i + 1)
            if i < 3:
                if not isinstance(b, int) or b:
                    act.wait_ge(at[f"parts_out{i}"], 16 * len(range(i, 8, 3)) * b)
            else:
                act.wait_ge(at[f"parts_out{i % 3}"], 16 * (len(range(i % 3, 8, 3)) * b + i // 3))
            nc.scalar.activation(PT[:, i % 3, 0, :], QC[:, i % 2, :], ACT.Copy).then_inc(at["p1"], 1)

        def low1_dve(dve, b, i):
            dve.wait_ge(at["p1"], 8 * b + i + 1)
            nc.vector.tensor_tensor(QS[:, i % 3, :], QC[:, i % 2, :], PT[:, i % 3, 0, :], ALU.subtract).then_inc(at["low"], 1)

        def part2_act(act, b, i):
            act.wait_ge(at["low"], 2 + 8 * b + i + 1)
            nc.scalar.activation(PT[:, i % 3, 1, :], QS[:, i % 3, :], ACT.Copy).then_inc(at["p2"], 1)

        def part3_pool(pool, b, i):
            pool.wait_ge(at["p2"], 8 * b + i + 1)
            nc.gpsimd.tensor_tensor(PT[:, i % 3, 2, :], QS[:, i % 3, :], PT[:, i % 3, 1, :], ALU.subtract).then_inc(at["p3"], 1)

        def v_pe(b, i):
            for t in range(2):
                ins = project(AUX[:, t * D:(t + 1) * D], lambda a, d: XT[a][:, d, (2 * i + t) * P:(2 * i + t + 1) * P],
                              lambda a, d: W[a][:, 2, d, :])
            ins.then_inc(at["v_ps"], 1)

        def v_dve(dve, b, i):
            dve.wait_ge(at["v_ps"], 4 * b + i + 1)
            for t in range(2):
                ins = nc.vector.tensor_tensor(
                    VN[:, 2 * i + t, 0:HEADS * VW].rearrange("p (h d) -> p h d", d=VW)[:, :, 0:HD],
                    AUX[:, t * D:(t + 1) * D].rearrange("p (h d) -> p h d", d=HD),
                    BV[:, :].rearrange("p (h d) -> p h d", d=HD), ALU.add)
            ins.then_inc(at["vn"], 1)

        def v_copy_dve(dve, b, prev):
            dve.wait_ge(at["vn"], 4 * b + 4)
            if prev:
                dve.wait_ge(at["pv"], 2 + STEPS * b)
            nc.vector.tensor_copy(V[:, :, :], VN[:, :, :]).then_inc(at["v"], 1)

        def part_sync(sp, b, i):
            m, h, c = QK[i]
            sp.wait_ge(at["p3"], 3 + 8 * b + i + 1)
            sp.dma_start(qkd[bass.ds(b, 1), :, m, h * P:h * P + P, c * C:c * C + C].rearrange("o a p n -> p (o a) n"),
                         PT[:, i % 3, :, :]).then_inc(at[f"parts_out{i % 3}"], 16)

        def parts_sync(sp, b, first, end):
            for i in range(first, end):
                part_sync(sp, b, i)

        STACKED = 16 * 2 * len(Q_PARTS)

        def stack_sync(sp, b, g, half):
            if half == 0 and g in (0, 2):
                for i in range(3):
                    gate(sp, "sp", at[f"parts_out{i}"], 16 * (len(range(i, 8, 3)) * b + len(range(i, 4 if g == 0 else 8, 3))))
            cols = slice(half * C, half * C + C)
            for m, buf, parts in ((0, STQ, Q_PARTS), (1, STK, K_PARTS)):
                for r, part in enumerate(parts):
                    src = qkd[bass.ds(b, 1), part, m, g * GH * HD:(g + 1) * GH * HD, cols]
                    sp.dma_start(buf[g % 2][HD * r:HD * r + HD, :, cols],
                                 src.rearrange("o (h r) n -> r (o h) n", h=GH)).then_inc(at[f"stk_in{g % 2}{half}"], 16)

        def maxrow_sync(sp, b, g):
            u = 4 * b + g
            sp.wait_ge(at["m3"], u + 1)
            sp.dma_start(md.rearrange("a p n -> p a n"), M3[:, :, :]).then_inc(at["m_out"], 16)
            sp.wait_ge(at["m_out"], 16 * u + 16)
            sp.dma_start(STQ[g % 2][STACK:ROWS, :, :], md.rearrange("a (h q) n -> a h (q n)", h=GH)).then_inc(at["m_row"], 16)

        def next_stack_sync(sp, b, g, half, pre):
            if g + 2 >= NG and not pre:
                return
            sp.wait_ge(at["st"], (STEPS * b + NP_ * g + (8 if half == 0 else NP_)) * GH)
            stack_sync(sp, *after(b, g, 2), half)

        def att_sync(sp, b, pre):
            for g in range(NG):
                next_stack_sync(sp, b, g, 0, pre)
                if pre and g == 2:
                    parts_sync(sp, b + 1, 4, 6)
                if g + 1 < NG or pre:
                    maxrow_sync(sp, *after(b, g, 1))
                if pre and g == 1:
                    parts_sync(sp, b + 1, 0, 1)
                if pre and g == 2:
                    parts_sync(sp, b + 1, 6, 7)
                next_stack_sync(sp, b, g, 1, pre)
                if pre and g == 1:
                    parts_sync(sp, b + 1, 1, 4)
                if pre and g == 2:
                    parts_sync(sp, b + 1, 7, 8)

        def after(b, g, n):
            return (b, g + n) if g + n < NG else (b + 1, g + n - NG)

        def max_pieces(b, step, pre):
            g, p = divmod(step, NP_)
            if p > MAX_LAST:
                ahead, p = 2, p - NP_
            else:
                ahead = 1
            if p < MAX_FIRST or g + ahead >= NG and not pre:
                return []
            return [(*after(b, g, ahead), n) for n in range(MAX_UPTO[p - 1], MAX_UPTO[p])]

        def of_head(pieces, h):
            return pieces[len(pieces) * h // GH:len(pieces) * (h + 1) // GH]

        def max_ends(b, step, pre, at_piece):
            g, p = divmod(step, NP_)
            return [after(b, g, 1)] if p == at_piece and (g + 1 < NG or pre) else []

        def max_pe(pe, b, g, n):
            h, q, c, cols = MAXP[n]
            i = (4 * b + g) * MAX_N + n
            if n in (0, MAX_EARLY):
                pe.wait_ge(at[f"stk_in{g % 2}{int(n > 0)}"], (2 * b + g // 2 + 1) * STACKED)
            pe.wait_ge(at["mx_red"], i + 1)
            o = MAXB[n % 3]
            diag = q // 4 == c
            ins = nc.tensor.matmul(o[:, 0:cols], STQ[g % 2][0:STACK, h, q * P:q * P + P], STK[g % 2][0:STACK, h, c * C:c * C + cols],
                                   start=True, stop=not diag)
            if diag:
                ins = nc.tensor.matmul(o[:, cols - P:cols], ID16[:, :], MASK16[:, :], start=False, stop=True)
            ins.then_inc(at["mx_ps"], 1)

        def max_dve(dve, b, g, n):
            h, q, c, cols = MAXP[n]
            i = (4 * b + g) * MAX_N + n
            dve.wait_ge(at["mx_ps"], i + 1)
            if n == 0:
                dve.wait_ge(at["m_done"], 4 * b + g + 1)
            nc.vector.tensor_reduce(MX[:, c, h * TPB + q:h * TPB + q + 1], MAXB[n % 3][:, 0:cols], AX.X, ALU.max).then_inc(at["mx_red"], 1)

        def max_join_dve(dve, b, g):
            u = 4 * b + g
            dve.wait_ge(at["mx_red"], 3 + (u + 1) * MAX_N)
            a, c = (MX[:, i, 0:GH * TPB].rearrange("p (h q) -> p h q", h=GH)[:, :, 4:8] for i in range(2))
            nc.vector.tensor_tensor(a, a, c, ALU.max).then_inc(at["m_link"], 1)

        def b7_use(b, g, what):
            u = NG * b + g
            if what == "m":
                return 0 if isinstance(u, int) and u == 0 else 3 * u - 1
            last = isinstance(u, int) and u == NB * NG - 1
            return 3 * u + 1 + (0 if what == 0 else 1 if last else 2)

        def max_turn_pe(pe, b, g):
            pe.wait_ge(at["m_link"], 4 * b + g + 1)
            pe.wait_ge(at["b7_free"], b7_use(b, g, "m") + 1)
            nc.tensor.transpose(B7[:, 0:P], MX[:, 0, :], ident).then_inc(at["m_done"], 1)

        def max_split_dve(dve, b, g):
            u = 4 * b + g
            dve.wait_ge(at["m_done"], 1 + u + 1)
            if not isinstance(u, int) or u:
                dve.wait_ge(at["m_row"], 16 * u)
            src = B7[0:GH * TPB, 0:P]
            nc.vector.tensor_scalar(M3[:, 0, :], src, -1.0, None, ALU.mult).then_inc(at["m3_link"], 1)
            dve.wait_ge(at["m3_link"], 3 * u + 1)
            nc.vector.scalar_tensor_tensor(MR[:, :], src, -1.0, M3[:, 0, :], ALU.mult, ALU.subtract).then_inc(at["b7_free"], 1)
            dve.wait_ge(at["b7_free"], 1 + b7_use(b, g, "m") + 1)
            nc.vector.tensor_copy(M3[:, 1, :], MR[:, :]).then_inc(at["m3_link"], 1)
            dve.wait_ge(at["m3_link"], 3 * u + 2)
            nc.vector.tensor_tensor(MR[:, :], MR[:, :], M3[:, 1, :], ALU.subtract).then_inc(at["m3_link"], 1)
            dve.wait_ge(at["m3_link"], 3 * u + 3)
            nc.vector.tensor_copy(M3[:, 2, :], MR[:, :]).then_inc(at["m3"], 1)

        def score_pe(pe, b, step, h):
            g, p = divmod(step, NP_)
            c, j, off, cols = PIECES[p]
            if p == 0 and h == 0:
                pe.wait_ge(at["m_row"], 16 * (4 * b + g + 1))
            n = step * GH + h
            pe.wait_ge(at["exp"], STEPS * GH * b + n + 1)
            q0 = c * C + off
            ins = nc.tensor.matmul(STB[n % 2][:, 0:cols], STK[g % 2][0:ROWS, h, j * P:j * P + P],
                                   STQ[g % 2][0:ROWS, h, q0:q0 + cols], start=True, stop=not DIAG[p])
            if DIAG[p]:
                ins = nc.tensor.matmul(STB[n % 2][:, 0:P], MASK16[:, :], ID16[:, :], start=False, stop=True)
            ins.then_inc(at["st"], 1)

        def exp_act(act, b, step, prev):
            g, p = divmod(step, NP_)
            cols = PIECES[p][3]
            act.wait_ge(at["pv"], STEPS * b + step + 1)
            for h in range(GH):
                n = step * GH + h
                act.wait_ge(at["st"], STEPS * GH * b + n + 1)
                nc.scalar.activation(PR[:, n % (2 * GH), 0:cols], STB[n % 2][:, 0:cols], ACT.Exp,
                                     scale=SCORE_SCALE).then_inc(at["exp"], 1)
                if h == 2:
                    for u in outputs(b, step, 1, prev):
                        out_act(act, *u)

        def value_pe(pe, b, step):
            g, p = divmod(step, NP_)
            c, j, off, cols = PIECES[p]
            pe.wait_ge(at["exp"], 2 + STEPS * GH * b + (step + 1) * GH)
            if step == 0:
                pe.wait_ge(at["v"], 1 + b)
            if j == 0:
                pe.wait_ge(at["ot"], 8 * b + 2 * g + c + 2)
            for h in range(GH):
                ins = nc.tensor.matmul(PVB[32 * h:32 * h + 32, off:C], V[:, j, (g * GH + h) * VW:(g * GH + h) * VW + 32],
                                       PR[:, (step * GH + h) % (2 * GH), 0:cols],
                                       start=(j == 0), stop=(j == 4 * c + 3), skip_group_check=True)
            ins.then_inc(at["pv"], 1)

        def outputs(b, step, lag, prev):
            g, p = divmod(step - lag, NP_)
            if g < 0:
                return [(b - 1, NG - 1, 1)] if p == NP_ - 1 and prev else []
            return [(b, g, 0)] if p == 3 and g < NG else [(b, g, 1)] if p == NP_ - 1 and g < NG else []

        def out_act(act, b, g, c):
            u = 8 * b + 2 * g + c
            act.wait_ge(at["pv"], 2 + STEPS * b + NP_ * g + (4 if c == 0 else NP_))
            act.wait_ge(at["b7"], u + 1)
            nc.scalar.activation(OT[:, c, :], PVB[:, :], ACT.Copy).then_inc(at["ot"], 1)

        def out_pe(pe, b, g, c):
            pe.wait_ge(at["ot"], 2 + 8 * b + 2 * g + c + 1)
            pe.wait_ge(at["b7_free"], b7_use(b, g, c) + 1)
            for t in range(4):
                ins = nc.tensor.transpose(B7[:, t * P:t * P + P], OT[:, c, t * P:t * P + P], ident)
            ins.then_inc(at["b7"], 1)

        def out_dve(dve, b, g, c):
            u = 8 * b + 2 * g + c
            dve.wait_ge(at["b7"], 2 + u + 1)
            o = B7[:, :].rearrange("p (t h d) -> p t h d", t=4, h=GH)
            nc.vector.reciprocal(RC[:, :, :], o[:, :, :, HD]).then_inc(at["a_link"], 1)
            dve.wait_ge(at["a_link"], u + 1)
            dst = A[:, 4 * c:4 * c + 4, g * GH * HD:(g + 1) * GH * HD].rearrange("p t (h d) -> p t h d", h=GH)
            nc.vector.tensor_tensor(dst, o[:, :, :, 0:HD], RC[:, :, :].unsqueeze(3).to_broadcast([P, 4, GH, HD]),
                                    ALU.mult).then_inc(at["b7_free"], 1)

        def proj_pe(b, i):
            for t in range(2):
                ins = project(AUX[:, t * D:(t + 1) * D], lambda a, d: XT[a][:, d, (2 * i + t) * P:(2 * i + t + 1) * P],
                              lambda a, d: W[a][:, 3, d, :])
            ins.then_inc(pj["out"], 1)

        def proj_dve(dve, b, i):
            dve.wait_ge(pj["out"], 4 * b + i + 1)
            rows = X[:, bass.ds(b * TPB + 2 * i, 2), :]
            nc.vector.tensor_tensor(rows, AUX[:, :].rearrange("p (t d) -> p t d", t=2), rows, ALU.add).then_inc(pj["added"], 1)

        def bias_pool(pool, b):
            pool.wait_ge(pj["added"], 4 * b + 4)
            nc.gpsimd.tensor_tensor(xb(b), xb(b), BO[:, :].unsqueeze(1).to_broadcast([P, TPB, D]), ALU.add).then_inc(at["a_done"], 1)

        LAST_JOBS = {4 + i: ("turn_out", i) for i in range(4)} | {8 + i: ("proj", i) for i in range(4)} \
            | {33 + i: ("turn_route", i) for i in range(4)} | {37: ("logit", 0), 44: ("rank", 0)}
        NEXT_JOBS = {13 + i: ("turn_qkv", i) for i in range(4)} | {17 + 2 * i: ("qk", i) for i in range(8)} \
            | {18 + 2 * i: ("v", i) for i in range(4)}
        TURNS = {"turn_out": (pj, A), "turn_qkv": (ln["att"], XN), "turn_route": (ln["r1"], XN)}

        def jobs(b, step, prev, pre):
            found = []
            if prev and step in LAST_JOBS:
                found.append((b - 1, *LAST_JOBS[step]))
            if pre and step in NEXT_JOBS:
                found.append((b + 1, *NEXT_JOBS[step]))
            return found

        def released(b, what, i):
            if what in TURNS:
                return TURNS[what][0]["lo"], 2 + 4 * b + i + 1
            return {"proj": (pj["added"], 4 * b + i + 1), "qk": (at["qb"], 8 * b + i + 1), "v": (at["vn"], 4 * b + i + 1),
                    "logit": (rt[1]["lg"], 1 + b), "rank": (rt[1]["rank"], 1 + b)}[what]

        def job_pe(pe, b, what, i, before):
            if before is not None:
                pe.wait_ge(*released(*before))
            if what in TURNS:
                s, src = TURNS[what]
                if "xn" in s:
                    pe.wait_ge(s["xn"], 2 * i + 2 + TPB * b)
                else:
                    pe.wait_ge(at["b7_free"], 1 + 1 + b7_use(b, NG - 1, 1))
                turn_pe(s, src, i, AUX)
            elif what == "proj":
                if i == 0:
                    pe.wait_ge(pj["lo"], 6 + 4 * b)
                proj_pe(b, i)
            elif what == "qk":
                if i == 0:
                    pe.wait_ge(ln["att"]["lo"], 6 + 4 * b)
                qk_pe(b, i)
            elif what == "v":
                v_pe(b, i)
            elif what == "logit":
                pe.wait_ge(ln["r1"]["lo"], 6 + 4 * b)
                logit_pe(rt[1], AUX)
            else:
                rank_pe(pe, rt[1], b, AUX)

        def job_act(act, b, what, i):
            if what in TURNS:
                turn_act(act, TURNS[what][0], b, i, AUX)
            elif what == "qk":
                qk_act(act, b, i)

        def job_dve(dve, b, what, i):
            if what in TURNS:
                turn_dve(dve, TURNS[what][0], b, i, AUX)
            elif what == "proj":
                proj_dve(dve, b, i)
            elif what == "qk":
                qk_dve(dve, b, i)
            elif what == "v":
                v_dve(dve, b, i)
            elif what == "logit":
                choice_dve(dve, rt[1], b, AUX)
            else:
                slot_dve(dve, rt[1], b, AUX)

        def side_dve(dve, b, step, prev, pre):
            if pre and step in (0, 1):
                combine_dve(dve, b + 1, step)
            if pre and step in (9, 10):
                combine_dve(dve, b + 1, step - 7)
            if pre and step == 11:
                index_dve(cb[0], GIX, b + 2)
                gate(dve, "dve", cb[0]["x"], b + 2)
                stats_dve(dve, ln["att"], b + 1)
            if pre and step == 12:
                if prev:
                    dve.wait_ge(rt[1]["sent"], b)
                norm_dve(dve, ln["att"], b + 1)
            if prev and step == 21:
                gate(dve, "dve", at["a_done"], b)
                stats_dve(dve, ln["r1"], b - 1)
            if prev and step == 24:
                norm_dve(dve, ln["r1"], b - 1)
            for n, what, i in jobs(b, step - 4, prev, pre):
                if what == "qk":
                    low1_dve(dve, n, i)

        def groups_pe(pe, b, prev, pre):
            before = None
            for step in range(STEPS):
                pieces = max_pieces(b, step, pre)
                for h in range(GH):
                    score_pe(pe, b, step, h)
                    if h == 0:
                        for u in max_ends(b, step, pre, MAX_LAST + 1):
                            max_turn_pe(pe, *u)
                    if h == 1:
                        if step:
                            value_pe(pe, b, step - 1)
                        elif prev:
                            value_pe(pe, b - 1, STEPS - 1)
                    for piece in of_head(pieces, h):
                        max_pe(pe, *piece)
                for u in outputs(b, step, PE_LAG, prev):
                    out_pe(pe, *u)
                for job in jobs(b, step, prev, pre):
                    job_pe(pe, *job, before)
                    before = job
            if before is not None:
                pe.wait_ge(*released(*before))

        def groups_act(act, b, prev, pre):
            for step in range(STEPS):
                for job in jobs(b, step - 1, prev, pre):
                    job_act(act, *job)
                exp_act(act, b, step, prev)
                for lag, part in ((3, part1_act), (5, part2_act)):
                    for n, what, i in jobs(b, step - lag, prev, pre):
                        if what == "qk":
                            part(act, n, i)
                if prev and step == 39:
                    route_act(act, rt[1], b - 1)

        def groups_dve(dve, b, prev, pre):
            for step in range(STEPS):
                for u in max_ends(b, step, pre, MAX_LAST + 1):
                    max_split_dve(dve, *u)
                pieces = max_pieces(b, step, pre)
                for h in range(GH):
                    for piece in of_head(pieces, h):
                        max_dve(dve, *piece)
                    if h == JOB_AT:
                        for job in jobs(b, step - 1, prev, pre):
                            job_dve(dve, *job)
                    if h == 1 and step == 0:
                        v_copy_dve(dve, b, prev)
                for u in max_ends(b, step, pre, MAX_LAST):
                    max_join_dve(dve, *u)
                for u in outputs(b, step, DVE_LAG, prev):
                    out_dve(dve, *u)
                side_dve(dve, b, step, prev, pre)

        def groups_pool(pool, b, prev, pre):
            for step in range(STEPS):
                for lag, part in ((2, rotate_pool), (6, part3_pool)):
                    for n, what, i in jobs(b, step - lag, prev, pre):
                        if what == "qk":
                            part(pool, n, i)
                if pre and step == 2:
                    gather_second_pool(pool, b + 1)
                if pre and step == 11:
                    combine_pool(pool, cb[0], b + 1)
                if pre and step == 12:
                    norm_pool(pool, ln["att"], b + 1)
                if prev and step == 13:
                    bias_pool(pool, b - 1)
                if pre and step == 14:
                    gather_first_pool(pool, b + 2)
                if prev and step == 22:
                    norm_pool(pool, ln["r1"], b - 1)
                if prev and step == 46:
                    route_pool(pool, rt[1], b - 1)
                if prev and step == STEPS - 1:
                    pool.wait_ge(rt[1]["scattered"], SCATTERED * b)
                    pool.sem_inc(rt[1]["sent"], 1)

        def batches(groups, eng):
            groups(eng, 0, False, True)
            with eng.Fori(1, NB - 1) as b:
                groups(eng, b, True, True)
            groups(eng, NB - 1, True, False)

        PE_LAG, DVE_LAG = 2, 3
        JOB_AT = 0

        def alone(what, n):
            return [(what, i) for i in range(n)]

        BEGIN = alone("turn_qkv", 4), alone("qk", 8), alone("v", 4)
        END = alone("turn_out", 4), alone("proj", 4), alone("turn_route", 4), alone("logit", 1), alone("rank", 1)

        def run_pe(pe, b, stages):
            before = None
            for what, i in sum(stages, []):
                job_pe(pe, b, what, i, before and (b, *before))
                before = what, i
            pe.wait_ge(*released(b, *before))

        FILLED = 16 * (SLOTS // CAP + 1)
        SETUP_DMAS = 16 * 11

        @block.sync
        def _(sp):
            for i, wt in enumerate((wq, wk, wv, wo)):
                sp.dma_start(A[:, 2 * i:2 * i + 2, :], wt.rearrange("(c p) n -> p c n", p=P)).then_inc(su["dma"], 16)
            sp.dma_start(XN[:, 0, 0:DH * NE].rearrange("p (c n) -> p c n", c=DH), router_w.rearrange("(c p) n -> p c n", p=P)).then_inc(su["dma"], 16)
            sp.dma_start(KC[:, :], consts).then_inc(su["dma"], 16)
            for m, v in enumerate((bq, bk)):
                sp.dma_start(BQK[:, m, :], v.rearrange("(c p) -> p c", p=P), allow_slow_non_contiguous=True).then_inc(su["dma"], 16)
            for buf, v in ((BV, bv), (BO, bo), (FB, fbias.rearrange("a b d -> (a b d)"))):
                sp.dma_start(buf[:, :], v.partition_broadcast(P)).then_inc(su["dma"], 16)
            with sp.Fori(0, NB) as b:
                sp.dma_start(xb(b), batch_tiles[bass.ds(b, 1), :, :, :].rearrange("o p t d -> p (o t) d")).then_inc(x_in, 16)
                gate(sp, "sp", x_in, 16 * b + 16)
            sp.wait_ge(su["zeros"], 1)
            for i in range(SLOTS // CAP):
                sp.dma_start(xe[i * CAP:(i + 1) * CAP, :].rearrange("(p r) d -> p r d", p=P), G[:, 0:NS, :]).then_inc(su["filled"], 16)
            sp.dma_start(ye[SLOTS:SLOTS + 1, :], G[0:1, 0, :]).then_inc(su["filled"], 16)
            sp.wait_ge(su["filled"], FILLED)
            sp.wait_ge(rt[0]["scattered"], SCATTERED * NB)
            ffn_sync(sp, 0)
            for k in range(TOPK):
                sp.wait_ge(ff[0][f"y_out{k}"], FFN_OUT)
            sp.dma_start(ROPE[:, :, :], rope.rearrange("a p n -> p a n")).then_inc(at["rope_in"], 16)
            parts_sync(sp, 0, 0, 8)
            for g in range(2):
                for half in range(2):
                    stack_sync(sp, 0, g, half)
            maxrow_sync(sp, 0, 0)
            att_sync(sp, 0, True)
            with sp.Fori(1, NB - 1) as b:
                att_sync(sp, b, True)
            att_sync(sp, NB - 1, False)
            sp.wait_ge(rt[1]["scattered"], SCATTERED * NB)
            ffn_sync(sp, 1)
            with sp.Fori(0, NB) as b:
                sp.wait_ge(cb[1]["x"], 1 + b)
                sp.dma_start(out_tiles[bass.ds(b, 1), :, :, :].rearrange("o p t d -> p (o t) d"), xb(b)).then_inc(out_done, 16)
            sp.wait_ge(out_done, 16 * NB)

        @block.tensor
        def _(pe):
            pe.wait_ge(su["split"], 6)
            with pe.Fori(0, NB // 2) as pair:
                for n in range(2):
                    b, l = 2 * pair + n, ln["r0"]
                    for i in range(4):
                        pe.wait_ge(l["lo"], 1 + i + 4 * b)
                        pe.wait_ge(l["xn"], 2 * i + 2 + TPB * b)
                        turn_pe(l, XNS[n], i, bank[i % 2])
                    pe.wait_ge(l["lo"], 6 + 4 * b)
                    logit_pe(rt[0], bank[6])
                    rank_pe(pe, rt[0], b, bank[7])
            pe.wait_ge(rt[0]["route"], NB)
            ffn_pe(pe, 0)
            pe.wait_ge(at["const"], 1)
            run_pe(pe, 0, BEGIN)
            for n in range(MAX_N):
                max_pe(pe, 0, 0, n)
            max_turn_pe(pe, 0, 0)
            for n in range(MAX_UPTO[-1]):
                max_pe(pe, 0, 1, n)
            batches(groups_pe, pe)
            value_pe(pe, NB - 1, STEPS - 1)
            out_pe(pe, NB - 1, NG - 1, 1)
            run_pe(pe, NB - 1, END)
            pe.wait_ge(rt[1]["route"], NB)
            ffn_pe(pe, 1)

        @block.scalar
        def _(act):
            for s, n in ((ff[0], 4), (ff[1], 4)):
                act.sem_inc(s["gelu"], n)
                act.sem_inc(s["y_evac"], 2)
                act.sem_inc(s["y_out0"], 16)
                act.sem_inc(s["y_out1"], 16)
            act.sem_inc(at["exp"], 2)
            act.sem_inc(at["ot"], 2)
            act.wait_ge(su["dma"], SETUP_DMAS)
            nc.scalar.activation(WH[:, :, :, :].rearrange("p m d n -> p (m d) n"), A[:, :, :], ACT.Copy)
            nc.scalar.activation(RW[:, :, 0:NE], XN[:, 0, 0:DH * NE].rearrange("p (c n) -> p c n", c=DH), ACT.Copy).then_inc(su["act"], 1)
            with act.Fori(0, NB) as b:
                for i in range(4):
                    turn_act(act, ln["r0"], b, i, bank[i % 2])
                route_act(act, rt[0], b)
            ffn_act(act, 0)
            for what, i in sum(BEGIN, []):
                job_act(act, 0, what, i)
                if what == "qk":
                    part1_act(act, 0, i)
                    part2_act(act, 0, i)
            batches(groups_act, act)
            out_act(act, NB - 1, NG - 1, 1)
            for what, i in sum(END, []):
                job_act(act, NB - 1, what, i)
            route_act(act, rt[1], NB - 1)
            ffn_act(act, 1)

        @block.vector
        def _(dve):
            for l in (*ln.values(), pj):
                dve.sem_inc(l["lo"], 2)
            for s in ff:
                dve.sem_inc(s["xe_lo"], 2)
                dve.sem_inc(s["h_lo"], 2)
            dve.sem_inc(at["mx_red"], 3)
            dve.sem_inc(at["low"], 2)
            dve.sem_inc(at["b7_free"], 1)
            nc.vector.memset(G[:, 0:NS, :], 0.0).then_inc(su["zeros"], 1)
            nc.vector.memset(ONES16[:, :], 1.0)
            dve.wait_ge(su["dma"], SETUP_DMAS)
            nc.vector.tensor_scalar(FB[:, :], FB[:, :], 0.5, None, ALU.mult)
            nc.vector.memset(NEGHALF[:, :], -0.5)
            nc.vector.memset(CARRY[:, :, :], 0.0)
            nc.vector.memset(SLP[:, NB:, :], 0.0)
            dve.wait_ge(su["act"], 1)
            for i, (dst, col) in enumerate(((ID16, K_ID), (LT16, K_LT), (MASK16, K_MASK))):
                nc.vector.tensor_copy(dst[:, :], KC[:, col:col + P]).then_inc(su["split"], 1)
            nc.vector.tensor_tensor(WL[:, :, :, :].rearrange("p m d n -> p (m d) n"), A[:, :, :],
                                    WH[:, :, :, :].rearrange("p m d n -> p (m d) n").bitcast(F32), ALU.subtract).then_inc(su["split"], 1)
            nc.vector.tensor_tensor(RW[:, :, NE:2 * NE], XN[:, 0, 0:DH * NE].rearrange("p (c n) -> p c n", c=DH),
                                    RW[:, :, 0:NE].bitcast(F32), ALU.subtract).then_inc(su["split"], 2)
            dve.wait_ge(su["split"], 6)
            with dve.Fori(0, NB // 2) as pair:
                for n in range(2):
                    b = 2 * pair + n
                    gate(dve, "dve", x_in, 16 * b + 16)
                    stats_dve(dve, ln["r0"], b)
                    dve.wait_ge(rt[0]["sent"], b + 1)
                    norm_dve(dve, ln["r0"], b, XNS[n])
                    for i in range(4):
                        turn_dve(dve, ln["r0"], b, i, bank[i % 2])
                    choice_dve(dve, rt[0], b, bank[6])
                    slot_dve(dve, rt[0], b, bank[7], SLTS[n])
            ffn_dve(dve, 0)
            for k in range(TOPK):
                dve.wait_ge(ff[0][f"y_out{k}"], FFN_OUT)
            nc.vector.memset(CARRY[:, :, :], 0.0)
            nc.vector.memset(VN[:, :, :], 0.0)
            nc.vector.memset(MX[:, :, :], 0.0).then_inc(at["const"], 1)
            dve.wait_ge(at["const"], 1)
            nc.vector.memset(VN[:, :, 0:HEADS * VW].rearrange("p t (h d) -> p t h d", d=VW)[:, :, :, HD:VW], 1.0)
            for i in range(2):
                ins = nc.vector.memset(STK[i][STACK:ROWS, :, :], 1.0)
            ins.then_inc(at["const"], 1)
            dve.wait_ge(at["const"], 2)
            dve.wait_ge(at["rope_in"], 16)
            index_dve(cb[0], GIX, 0)
            for part in range(4):
                combine_dve(dve, 0, part)
            index_dve(cb[0], GIX, 1)
            dve.wait_ge(cb[0]["x"], 1)
            stats_dve(dve, ln["att"], 0)
            norm_dve(dve, ln["att"], 0)
            for what, i in sum(BEGIN, []):
                job_dve(dve, 0, what, i)
                if what == "qk":
                    low1_dve(dve, 0, i)
            for n in range(MAX_N):
                max_dve(dve, 0, 0, n)
            max_join_dve(dve, 0, 0)
            max_split_dve(dve, 0, 0)
            for n in range(MAX_UPTO[-1]):
                max_dve(dve, 0, 1, n)
            batches(groups_dve, dve)
            out_dve(dve, NB - 1, NG - 1, 1)
            turns, projs, turns2, logit, rank = END
            for what, i in turns + projs:
                job_dve(dve, NB - 1, what, i)
            dve.wait_ge(at["a_done"], NB)
            stats_dve(dve, ln["r1"], NB - 1)
            dve.wait_ge(rt[1]["sent"], NB)
            norm_dve(dve, ln["r1"], NB - 1)
            for what, i in turns2 + logit + rank:
                job_dve(dve, NB - 1, what, i)
            ffn_dve(dve, 1)
            for i in range(2):
                index_dve(dict(index=cb[1][f"index{i}"]), GIXF[i], i)
            with dve.Fori(0, NB // 2) as pair:
                for i in range(2):
                    b = 2 * pair + i
                    for c in range(TOPK):
                        dve.wait_ge(cb[1][f"gathered{i}"], TOPK * GATHERED * (pair + 1))
                        if c:
                            dve.wait_ge(cb[1]["link"], 2 * b + 1)
                        add_rows_dve(GF[i][c], cb[1], b, c, range(TPB))
                    dve.wait_ge(cb[1]["link"], 2 * b + 2)
                    nc.vector.tensor_tensor(xb(b), xb(b), FB[:, :].unsqueeze(1).to_broadcast([P, TPB, D]), ALU.add).then_inc(cb[1]["x"], 1)
                    index_dve(dict(index=cb[1][f"index{i}"]), GIXF[i], b + 2)

        @block.gpsimd
        def _(pool):
            pool.sem_inc(at["cos"], 2)
            pool.sem_inc(at["p3"], 3)
            pool.sem_inc(rt[1]["sent"], 1)
            pool.sem_inc(at["pv"], 2)
            pool.sem_inc(at["m_done"], 1)
            pool.sem_inc(at["b7"], 2)
            for s in ff:
                pool.sem_inc(s["down"], 4)
            pool.wait_ge(su["split"], 6)
            pool.sem_inc(rt[0]["sent"], 2)
            with pool.Fori(0, NB // 2) as pair:
                for n in range(2):
                    b = 2 * pair + n
                    norm_pool(pool, ln["r0"], b)
                    pool.wait_ge(su["filled"], FILLED)
                    route_pool(pool, rt[0], b, XNS[n], SLTS[n])
                    pool.wait_ge(rt[0]["scattered"], SCATTERED * (b + 1))
                    pool.sem_inc(rt[0]["sent"], 1)
            ffn_pool(pool, 0)
            for k in range(TOPK):
                pool.wait_ge(ff[0][f"y_out{k}"], FFN_OUT)
            gather_first_pool(pool, 0)
            gather_second_pool(pool, 0)
            combine_pool(pool, cb[0], 0)
            norm_pool(pool, ln["att"], 0)
            gather_first_pool(pool, 1)
            for i in range(8):
                rotate_pool(pool, 0, i)
                part3_pool(pool, 0, i)
            batches(groups_pool, pool)
            bias_pool(pool, NB - 1)
            norm_pool(pool, ln["r1"], NB - 1)
            route_pool(pool, rt[1], NB - 1)
            pool.wait_ge(cb[0]["gathered"], GATHERED * (2 * NB + 1))
            ffn_pool(pool, 1)
            for k in range(TOPK):
                pool.wait_ge(ff[1][f"y_out{k}"], FFN_OUT)
            with pool.Fori(0, NB // 2) as pair:
                for i in range(2):
                    gate(pool, "pool", cb[1][f"index{i}"], pair + 1)
                    for c in range(TOPK):
                        gather_pool(pool, cb[1][f"gathered{i}"], GF[i][c], GIXF[i], c)
            for i in range(2):
                pool.wait_ge(cb[1][f"gathered{i}"], TOPK * GATHERED * NB // 2)


_INS = ["L0_attn_x", "L0_attn_wq", "L0_attn_bq", "L0_attn_wk", "L0_attn_bk", "L0_attn_wv", "L0_attn_bv",
        "L0_attn_wo", "L0_attn_bo", "L0_ffn_router_w", "L0_ffn_w1", "L0_ffn_w2", "L0_ffn_bias"]


def kernel(**inputs):
    import numpy as _np
    import concourse.bacc as _bacc
    from concourse import mybir as _mybir
    from concourse.bass_utils import run_bass_kernel_spmd as _run

    nc = _bacc.Bacc("TRN2", target_bir_lowering=False, num_devices=1)
    arrays, args = {}, []
    given = {name: _np.ascontiguousarray(inputs[name]) for name in _INS}
    given["shape_constants"] = shape_constants()
    given["rope_tables"] = rope_tables()
    for name, a in given.items():
        arrays[f"in_{name}_dram"] = a
        args.append(nc.dram_tensor(f"in_{name}_dram", a.shape, _mybir.dt.from_np(a.dtype), kind="ExternalInput").ap())
    args.append(nc.dram_tensor("out_0_dram", (NB, SEQ, D), _mybir.dt.float32, kind="ExternalOutput").ap())
    build(nc, *args)
    r = _run(nc, [arrays], core_ids=[0])
    return r.results[0]["out_0_dram"]
```

```python
from contextlib import ExitStack

import numpy as np
import concourse.bass as bass
from concourse import mybir

F32 = mybir.dt.float32
F32R = mybir.dt.float32r
BF16 = mybir.dt.bfloat16
U32 = mybir.dt.uint32
ALU = mybir.AluOpType
ACT = mybir.ActivationFunctionType
AX = mybir.AxisListType

P = 128
D = 256
DH = D // P
SEQ = 1024
NB = 4
TOK = NB * SEQ
TPB = SEQ // P
HEADS = 16
HD = D // HEADS
GH = 4
NG = HEADS // GH
NE = 8
TOPK = 2
CAP = TOK // NE
FFN = 1024
NF = FFN // P
NS = CAP // P
SLOTS = TOPK * TOK
C = 512
SCORE_SCALE = float(HD) ** -0.5
EPS = 1e-5
NEG = -1e30

Q_PARTS = (0, 0, 0, 1, 1, 2)
K_PARTS = (0, 1, 2, 0, 1, 0)
STACK = HD * len(Q_PARTS)
ROWS = STACK + 3

PIECES = [(c, j, max(0, P * j - C * c), C - max(0, P * j - C * c)) for c in range(2) for j in range(4 * (c + 1))]
DIAG = [j >= 4 * c for c, j, _, _ in PIECES]
NP_ = len(PIECES)
MAXP = [(h, q, c, min(C, P * (q + 1) - C * c)) for tiles in (range(4), range(4, TPB))
        for h in range(GH) for q in tiles for c in range(q // 4 + 1)]
MAX_N = len(MAXP)
MAX_EARLY = 4 * GH
MAX_FIRST, MAX_LAST = -2, 8
MAX_UPTO = {p: MAX_EARLY * (p + 3) // 4 if p < 2 else MAX_EARLY + (MAX_N - MAX_EARLY) * (p - 1) // (MAX_LAST - 1)
            for p in range(MAX_FIRST - 1, MAX_LAST + 1)}
STEPS = NG * NP_
VW = HD + 1
VPAD = 32 - VW

K_ID, K_LT, K_MASK, K_IOTA, K_OFF = 0, P, 2 * P, 3 * P, 3 * P + NE
K_ROW = K_OFF + TOPK * TPB
K_END = K_ROW + NB * TPB

NOWHERE = 4.0 * SLOTS


def shape_constants():
    p = np.arange(P)
    k = np.zeros((P, K_END), np.float32)
    k[:, K_ID:K_ID + P] = np.eye(P)
    k[:, K_LT:K_LT + P] = p[:, None] < p[None, :]
    k[:, K_MASK:K_MASK + P] = np.where(p[None, :] > p[:, None], NEG, 0.0)
    k[:, K_IOTA:K_IOTA + NE] = np.arange(NE)
    k[:, K_OFF:K_ROW] = np.repeat(np.arange(TOPK) * TOK - SLOTS, TPB)
    k[:, K_ROW:K_END] = p[:, None] + P * np.arange(NB * TPB)[None, :]
    return k


def rope_tables():
    one = np.float32(1.0)
    inv = one / np.float32(10000.0) ** (np.arange(0, HD, 2, dtype=np.float32) / np.float32(HD))
    angle = inv[:, None] * np.arange(SEQ, dtype=np.float32)[None, :]
    pair = (np.arange(P) % HD) // 2
    sign = np.where(np.arange(P) % 2 == 0, -one, one)[:, None]
    return np.stack([np.cos(angle)[pair], np.sin(angle)[pair] * sign]).astype(np.float32)


class Link:

    def __init__(self, eng, sem, base=0):
        self.eng, self.sem, self.base, self.n = eng, sem, base, 0

    def add(self, ins):
        ins.then_inc(self.sem, 1)
        self.n += 1

    def sync(self):
        self.eng.wait_ge(self.sem, self.base + self.n)


def build(nc, x, wq, bq, wk, bk, wv, bv, wo, bo, router_w, w1, w2, fbias, consts, rope, out):
    ctx = ExitStack()
    with ctx:
        def sb(name, shape, dt, where=ctx):
            return where.enter_context(nc.sbuf_tensor(name, shape, dt))

        def sem(name):
            return ctx.enter_context(nc.semaphore(name))

        def sems(prefix, names):
            return {n: sem(f"{prefix}_{n}") for n in names.split()}

        bank = [ctx.enter_context(nc.psum_tensor(f"bank{i}", [P, C], F32)) for i in range(8)]

        xe = nc.dram_tensor("expert_rows", [SLOTS, D + 1], F32, kind="Internal").ap()
        yt = nc.dram_tensor("token_out", [TOPK * TOK, D], F32, kind="Internal").ap()
        qkd = nc.dram_tensor("qk_parts", [NB, 3, 2, D, SEQ], BF16, kind="Internal").ap()
        md = nc.dram_tensor("max_rows", [3, GH * TPB, P], BF16, kind="Internal").ap()

        X = sb("X", [P, NB * TPB, D], F32)
        XN = sb("XN", [P, TPB, D + 1], F32)
        XTH = sb("XTH", [P, DH, SEQ], F32R)
        XTL = sb("XTL", [P, DH, SEQ], F32R)
        WH = sb("WH", [P, 4, DH, D], F32R)
        WL = sb("WL", [P, 4, DH, D], F32R)
        RW = sb("RW", [P, DH, 2 * NE], F32R)
        KC = sb("KC", [P, K_END], F32)
        ID16 = sb("ID16", [P, P], BF16)
        LT16 = sb("LT16", [P, P], BF16)
        MASK16 = sb("MASK16", [P, P], BF16)
        ONES16 = sb("ONES16", [P, P], BF16)
        BQK = sb("BQK", [P, 2, DH], F32)
        BV = sb("BV", [P, D], F32)
        BO = sb("BO", [P, D], F32)
        FB = sb("FB", [P, D], F32)
        NEGHALF = sb("NEGHALF", [P, TPB], F32)
        BST = sb("BST", [P, TPB, 6], F32)
        MV = sb("MV", [P, NB * TPB, 2], F32)
        VE = sb("VE", [P, TPB], F32)
        RSTD = sb("RSTD", [P, NB * TPB], F32)
        LA = sb("LA", [P, TPB, NE], F32)
        LG = sb("LG", [P, TPB, NE], F32)
        TOP = sb("TOP", [P, TPB, 8], F32)
        TIX = sb("TIX", [P, TPB, 8], U32)
        IDXF = sb("IDXF", [P, TOPK, TPB], F32)
        OH = sb("OH", [P, TOPK, TPB, NE], BF16)
        DL = sb("DL", [P, TPB, NE], F32)
        DW = sb("DW", [P, TOPK, TPB], F32)
        EL = sb("EL", [P, TPB, NE], F32)
        EW = sb("EW", [P, TOPK, TPB], F32)
        SUM = sb("SUM", [P, TPB], F32)
        RS = sb("RS", [P, TPB], F32)
        WV_ = sb("WV_", [P, TOPK, TPB], F32)
        TOT = sb("TOT", [P, TOPK, TPB, NE], F32)
        PX = sb("PX", [P, TOPK, TPB, NE], F32)
        CARRY = sb("CARRY", [P, TOPK, NE], F32)
        RANK = sb("RANK", [P, TOPK, TPB, NE], F32)
        SEL = sb("SEL", [P, TOPK, TPB, NE], F32)
        RK = sb("RK", [P, TOPK, TPB], F32)
        OK = sb("OK", [P, TOPK, TPB], F32)
        SL = sb("SL", [P, TOPK, TPB], F32)
        SL2 = sb("SL2", [P, TOPK, TPB], F32)
        SLT = sb("SLT", [P, TOPK * TPB], U32)
        SLT2 = sb("SLT2", [P, TOPK * TPB], U32)
        WP = sb("WP", [P, NB, TOPK * TPB], F32)

        fctx = ExitStack()
        WRAW1 = sb("WRAW1", [P, DH, FFN], F32, fctx)
        WRAW2 = sb("WRAW2", [P, NF, D], F32, fctx)
        W1H = sb("W1H", [P, DH, FFN], F32R, fctx)
        W1L = sb("W1L", [P, DH, FFN], F32R, fctx)
        W2H = sb("W2H", [P, NF, D], F32R, fctx)
        W2L = sb("W2L", [P, NF, D], F32R, fctx)
        XR = [sb(f"XR{k}", [P, NS, D + 1], F32, fctx) for k in range(TOPK)]
        XEH = [sb(f"XEH{k}", [P, DH, CAP], F32R, fctx) for k in range(TOPK)]
        XEL = [sb(f"XEL{k}", [P, DH, CAP], F32R, fctx) for k in range(TOPK)]
        GE = sb("GE", [P, 2, C], F32, fctx)
        HH = sb("HH", [P, 4, C], F32R, fctx)
        HL = sb("HL", [P, 4, C], F32R, fctx)
        YS = [sb(f"YS{k}", [P, NS, D], F32, fctx) for k in range(TOPK)]
        VALID = sb("VALID", [P, NS], F32, fctx)
        ROWM = sb("ROWM", [P, TOPK, NS], F32, fctx)
        GOAL = sb("GOAL", [P, TOPK, NS], U32, fctx)
        GLATE = [sb(f"GF0{b}", [P, TPB, D], F32, fctx) for b in range(2, NB)]
        fctx.close()
        gctx = ExitStack()
        GF0 = [sb(f"GF0{b}", [P, TPB, D], F32, gctx) for b in range(2)] + GLATE
        GF1 = [sb(f"GF1{b}", [P, TPB, D], F32, gctx) for b in range(NB)]
        gctx.close()
        actx = ctx
        G = sb("G", [P, TPB, D], F32, actx)
        ROPE = sb("ROPE", [P, 2, SEQ], F32, actx)
        STQ = [sb(f"STQ{i}", [ROWS, GH, SEQ], BF16, actx) for i in range(2)]
        STK = [sb(f"STK{i}", [ROWS, GH, SEQ], BF16, actx) for i in range(2)]
        PR = sb("PR", [P, 2 * GH, C], F32, actx)
        V = sb("V", [P, TPB, HEADS * VW + VPAD], F32, actx)
        VN = sb("VN", [P, TPB, HEADS * VW + VPAD], F32, actx)
        QB = sb("QB", [P, 2, C], F32, actx)
        QS = sb("QS", [P, 3, C], F32, actx)
        QC = sb("QC", [P, 2, C], F32, actx)
        PT = sb("PT", [P, 3, 3, C], BF16, actx)
        MX = sb("MX", [P, 2, P], F32, actx)
        MR = sb("MR", [GH * TPB, P], F32, actx)
        M3 = sb("M3", [GH * TPB, 3, P], BF16, actx)
        OT = sb("OT", [P, 2, C], F32, actx)
        RC = sb("RC", [P, 4, GH], F32, actx)
        A = sb("A", [P, TPB, D + 1], F32, actx)

        XNS, SLTS = (XN, A), (SLT, SLT2)
        ident = KC[:, K_ID:K_ID + P]

        passed = {}

        def gate(eng, name, sem_, value):
            eng.wait_ge(sem_, value)
            eng.sem_inc(passed[name], 1)

        su = sems("setup", "dma split zeros filled y_filled act")
        x_in, out_done = [sem(f"x_in{b}") for b in range(NB)], sem("out_done")
        LN_SEMS = "link stats rstd_link rstd xn tp hi lo"
        RT_SEMS = "logits lg rank link oh diff exps ranks route scattered sent"
        ln = {n: sems(f"ln_{n}", LN_SEMS) for n in ("r0", "att", "r1")}
        pj = sems("proj", "tp hi lo out added")
        rt = {n: sems(f"rt{n}", RT_SEMS) for n in range(2)}
        ff = [sems(f"ffn{n}", "w_in xe_in0 xe_in1 w1_hi w2_hi w1_lo w2_lo xe_tp xe_hi xe_lo "
                              "up gelu h_hi h_lo down y_evac y_out0 y_out1 y_free0 y_free1 goal_link goal biased") for n in range(2)]
        cb = [sems("comb0", "in0 in1 link"), sems("comb1", "in0 in1 in2 in3 link")]
        at = sems("att", "rope_in const qkv qb swap cos sin rot p1 low p2 p3 parts_out0 parts_out1 parts_out2 v_ps vn v stk_in00 stk_in01 stk_in10 stk_in11 "
                         "mx_ps mx_red m_link m_done m3_link m3 m_out m_row st exp pv ot b7 b7_free a_link biased")

        passed.update(dve=sem("dve_passed"), pool=sem("pool_passed"), sp=sem("sp_passed"))

        block = ctx.enter_context(nc.Block())
        batch_tiles = x.rearrange("b (t p) d -> b p t d", p=P)
        out_tiles = out.rearrange("b (t p) d -> b p t d", p=P)

        def xb(b, t=None):
            if t is None:
                return X[:, bass.ds(b * TPB, TPB), :]
            return X[:, bass.ds(b * TPB + t, 1), :].rearrange("p o d -> p (o d)")

        def mv(m, t, i):
            return MV[:, bass.ds(m * TPB + t, 1), i:i + 1].rearrange("p o n -> p (o n)")

        def stats_dve(dve, s, b, m=0):
            for t in range(TPB):
                ins = nc.vector.bn_stats(BST[:, t, :], xb(b, t))
            ins.then_inc(s["link"], 1)
            gate(dve, "dve", s["link"], 1 + b)
            for t in range(TPB):
                ins = nc.vector.bn_aggr(MV[:, m * TPB + t, :], BST[:, t, :])
            ins.then_inc(s["stats"], 1)

        def norm_dve(dve, s, b, xn=XN, numbered=False, m=0):
            dve.wait_ge(s["rstd"], 1 + b)
            if numbered:
                nc.vector.tensor_copy(xn[:, :, D], KC[:, bass.ds(K_ROW + b * TPB, TPB)])
            for t in range(TPB):
                nc.vector.tensor_scalar(xn[:, t, 0:D], xb(b, t), mv(m, t, 0), RSTD[:, bass.ds(m * TPB + t, 1)],
                                        ALU.subtract, ALU.mult).then_inc(s["xn"], 1)

        def norm_pool(pool, s, b, m=0):
            gate(pool, "pool", s["stats"], 1 + b)
            tiles = slice(m * TPB, m * TPB + TPB)
            nc.gpsimd.tensor_scalar(VE[:, :], MV[:, tiles, 1], EPS, None, ALU.add).then_inc(s["rstd_link"], 1)
            pool.wait_ge(s["rstd_link"], 1 + b)
            nc.gpsimd.tensor_tensor(RSTD[:, tiles], VE[:, :], NEGHALF[:, :], ALU.pow).then_inc(s["rstd"], 1)

        def turn_pe(s, src, i, bk):
            for d in range(DH):
                for t in range(2):
                    ins = nc.tensor.transpose(bk[:, d * 2 * P + t * P:d * 2 * P + t * P + P],
                                              src[:, 2 * i + t, d * P:d * P + P], ident)
            ins.then_inc(s["tp"], 1)

        def turn_act(act, s, b, i, bk):
            act.wait_ge(s["tp"], 1 + i + 4 * b)
            nc.scalar.activation(XTH[:, :, i * 2 * P:(i + 1) * 2 * P],
                                 bk[:, :].rearrange("p (d n) -> p d n", d=DH), ACT.Copy).then_inc(s["hi"], 1)

        def turn_dve(dve, s, b, i, bk):
            dve.wait_ge(s["hi"], 1 + i + 4 * b)
            cols = slice(i * 2 * P, (i + 1) * 2 * P)
            nc.vector.tensor_tensor(XTL[:, :, cols], bk[:, :].rearrange("p (d n) -> p d n", d=DH),
                                    XTH[:, :, cols].bitcast(F32), ALU.subtract).then_inc(s["lo"], 1)

        def logit_pe(s, bk):
            for t in range(TPB):
                tok = slice(t * P, t * P + P)
                o = bk[:, t * 2 * NE:(t + 1) * 2 * NE]
                for d in range(DH):
                    nc.tensor.matmul(o, XTH[:, d, tok], RW[:, d, :], start=(d == 0), stop=False, skip_group_check=True)
                for d in range(DH):
                    ins = nc.tensor.matmul(o[:, 0:NE], XTL[:, d, tok], RW[:, d, 0:NE], start=False, stop=(d == 1),
                                           skip_group_check=True)
            ins.then_inc(s["logits"], 1)

        def rank_pe(pe, s, b, bk):
            pe.wait_ge(s["oh"], 1 + b)
            oh = OH[:, :, :, :].rearrange("p k t e -> p (k t e)")
            n = TOPK * TPB * NE
            nc.tensor.matmul(bk[:, 0:n], LT16[:, :], oh, start=True, stop=True)
            nc.tensor.matmul(bk[:, n:2 * n], ONES16[:, :], oh, start=True, stop=True).then_inc(s["ranks"], 1)

        def route_act(act, s, b):
            act.wait_ge(s["diff"], 1 + b)
            nc.scalar.activation(EL[:, :, :], DL[:, :, :], ACT.Exp)
            nc.scalar.activation(EW[:, :, :], DW[:, :, :], ACT.Exp).then_inc(s["exps"], 1)

        CHOICE_LINKS, SLOT_LINKS = 4, 19

        def choice_dve(dve, s, b, bk):
            k = Link(dve, s["link"], b * (CHOICE_LINKS + SLOT_LINKS))
            dve.wait_ge(s["logits"], 1 + b)
            logit = bk[:, 0:TPB * 2 * NE].rearrange("p (t e) -> p t e", t=TPB)
            k.add(nc.vector.tensor_copy(LA[:, :, :], logit[:, :, NE:]))
            k.sync()
            nc.vector.tensor_tensor(LG[:, :, :], logit[:, :, 0:NE], LA[:, :, :], ALU.add).then_inc(s["lg"], 1)
            gate(dve, "dve", s["lg"], 1 + b)
            for t in range(TPB):
                ins = nc.vector.max(TOP[:, t, :], LG[:, t, :])
            k.add(ins)
            gate(dve, "dve", s["link"], k.base + k.n)
            for t in range(TPB):
                ins = nc.vector.max_index(TIX[:, t, :], TOP[:, t, :], LG[:, t, :])
            k.add(ins)
            k.sync()
            k.add(nc.vector.tensor_copy(IDXF[:, :, :], TIX[:, :, 0:TOPK].rearrange("p t k -> p k t")))
            k.sync()
            iota = KC[:, K_IOTA:K_IOTA + NE].unsqueeze(1).to_broadcast([P, TPB, NE])
            for c in range(TOPK):
                ins = nc.vector.tensor_tensor(OH[:, c, :, :], IDXF[:, c, :].unsqueeze(2).to_broadcast([P, TPB, NE]),
                                              iota, ALU.is_equal)
            ins.then_inc(s["oh"], 1)
            nc.vector.tensor_tensor(DL[:, :, :], LG[:, :, :], TOP[:, :, 0:1].to_broadcast([P, TPB, NE]), ALU.subtract)
            for c in range(TOPK):
                ins = nc.vector.tensor_tensor(DW[:, c, :], TOP[:, :, c], TOP[:, :, 0], ALU.subtract)
            ins.then_inc(s["diff"], 1)
            assert k.n == CHOICE_LINKS, k.n

        def slot_dve(dve, s, b, bk, slt=SLT):
            k = Link(dve, s["link"], b * (CHOICE_LINKS + SLOT_LINKS) + CHOICE_LINKS)
            n = TOPK * TPB * NE
            dve.wait_ge(s["ranks"], 1 + b)
            k.add(nc.vector.tensor_copy(TOT[:, :, :, :].rearrange("p k t e -> p (k t e)"), bk[:, n:2 * n]))
            k.add(nc.vector.tensor_copy(PX[:, :, 0, :], CARRY[:, :, :]))
            k.sync()
            for t in range(1, TPB):
                k.add(nc.vector.tensor_tensor(PX[:, :, t, :], PX[:, :, t - 1, :], TOT[:, :, t - 1, :], ALU.add))
                k.sync()
            k.add(nc.vector.tensor_tensor(CARRY[:, :, :], PX[:, :, TPB - 1, :], TOT[:, :, TPB - 1, :], ALU.add))
            nc.vector.tensor_tensor(RANK[:, :, :, :].rearrange("p k t e -> p (k t e)"), bk[:, 0:n],
                                    PX[:, :, :, :].rearrange("p k t e -> p (k t e)"), ALU.add).then_inc(s["rank"], 1)
            dve.wait_ge(s["rank"], 1 + b)
            k.add(nc.vector.tensor_tensor(SEL[:, :, :, :].rearrange("p k t e -> p (k t e)"),
                                          RANK[:, :, :, :].rearrange("p k t e -> p (k t e)"),
                                          OH[:, :, :, :].rearrange("p k t e -> p (k t e)"), ALU.mult))
            k.sync()
            k.add(nc.vector.tensor_reduce(RK[:, :, :], SEL[:, :, :, :], AX.X, ALU.add))
            k.sync()
            k.add(nc.vector.tensor_scalar(OK[:, :, :], RK[:, :, :], float(CAP), None, ALU.is_lt))
            k.add(nc.vector.scalar_tensor_tensor(SL[:, :, :], IDXF[:, :, :], float(CAP), RK[:, :, :], ALU.mult, ALU.add))
            k.sync()
            k.add(nc.vector.tensor_tensor(SL2[:, :, :].rearrange("p k t -> p (k t)"), SL[:, :, :].rearrange("p k t -> p (k t)"),
                                          KC[:, K_OFF:K_ROW], ALU.add))
            k.sync()
            k.add(nc.vector.tensor_tensor(SL[:, :, :], SL2[:, :, :], OK[:, :, :], ALU.mult))
            k.sync()
            flat = SL[:, :, :].rearrange("p k t -> p (k t)")
            nc.vector.tensor_scalar(slt[:, :], flat, float(SLOTS), None, ALU.add).then_inc(s["route"], 1)
            dve.wait_ge(s["exps"], 1 + b)
            k.add(nc.vector.tensor_reduce(SUM[:, :], EL[:, :, :], AX.X, ALU.add))
            k.sync()
            k.add(nc.vector.reciprocal(RS[:, :], SUM[:, :]))
            k.sync()
            for c in range(TOPK):
                ins = nc.vector.tensor_tensor(WV_[:, c, :], EW[:, c, :], RS[:, :], ALU.mult)
            k.add(ins)
            k.sync()
            nc.vector.scalar_tensor_tensor(WP[:, bass.ds(b, 1), :].rearrange("p o n -> p (o n)"),
                                           WV_[:, :, :].rearrange("p k t -> p (k t)"), 0.5,
                                           OK[:, :, :].rearrange("p k t -> p (k t)"), ALU.mult, ALU.mult)
            assert k.n == SLOT_LINKS, k.n

        def route_pool(pool, s, b, xn=XN, slt=SLT):
            gate(pool, "pool", s["route"], 1 + b)
            for c in range(TOPK):
                for t in range(TPB):
                    nc.gpsimd.indirect_dma_start(
                        out=xe[:, :], out_offset=bass.IndirectOffsetOnAxis(ap=slt[:, c * TPB + t:c * TPB + t + 1], axis=0),
                        in_=xn[:, t, :], in_offset=None, bounds_check=SLOTS - 1, oob_is_err=False,
                    ).then_inc(s["scattered"], 16)

        SCATTERED = 16 * TOPK * TPB

        Y, UP, XTP = [bank[0], bank[1]], [bank[2], bank[3], bank[4], bank[5]], [bank[6], bank[7]]

        def weights_sync(sp, s, e):
            sp.dma_start(WRAW1[:, :, :], w1[bass.ds(e, 1), :, :].rearrange("o (c p) f -> p (o c) f", p=P)).then_inc(s["w_in"], 16)
            sp.dma_start(WRAW2[:, :, :], w2[bass.ds(e, 1), :, :].rearrange("o (c p) f -> p (o c) f", p=P)).then_inc(s["w_in"], 16)

        def rows_sync(sp, s, e):
            for k in range(TOPK):
                rows = xe[bass.ds(e * CAP + k * TOK, CAP), :].rearrange("(s p) d -> p s d", p=P)
                sp.dma_start(XR[k][:, :, :], rows).then_inc(s[f"xe_in{k}"], 16)

        def ffn_sync(sp, ph):
            s = ff[ph]
            rows_sync(sp, s, 0)
            with sp.Fori(0, NE - 1) as e:
                for part in ("w1_hi", "w2_hi", "w1_lo", "w2_lo"):
                    sp.wait_ge(s[part], NF * e + NF)
                weights_sync(sp, s, e + 1)
                gate(sp, "sp", s["goal_link"], 4 * e + 4)
                gate(sp, "sp", s["xe_tp"], 2 * TOPK * e + 2 * TOPK)
                rows_sync(sp, s, e + 1)

        def xe_pe(pe, s, e, k):
            pe.wait_ge(s[f"xe_in{k}"], 16 * e + 16)
            for d in range(DH):
                pe.wait_ge(s["xe_lo"], 4 * e + 2 * k + d + 1)
                for t in range(NS):
                    ins = nc.tensor.transpose(XTP[d][:, t * P:t * P + P], XR[k][:, t, d * P:d * P + P], ident)
                ins.then_inc(s["xe_tp"], 1)

        def xe_act(act, s, e, k):
            for d in range(DH):
                act.wait_ge(s["xe_tp"], 4 * e + 2 * k + d + 1)
                nc.scalar.activation(XEH[k][:, d, :], XTP[d][:, :], ACT.Copy).then_inc(s["xe_hi"], 1)

        def xe_dve(dve, s, e, k):
            for d in range(DH):
                dve.wait_ge(s["xe_hi"], 4 * e + 2 * k + d + 1)
                nc.vector.tensor_tensor(XEL[k][:, d, :], XTP[d][:, :], XEH[k][:, d, :].bitcast(F32),
                                        ALU.subtract).then_inc(s["xe_lo"], 1)

        def block_pe(pe, s, e, k, last):
            n8 = 2 * NF * e + NF * k
            pe.wait_ge(s["xe_lo"], 4 * e + 2 * k + 4)

            def up(f):
                pe.wait_ge(s["gelu"], n8 + f + 1)
                pe.wait_ge(s["w1_hi"], NF * e + f + 1)
                pe.wait_ge(s["w1_lo"], NF * e + f + 1)
                cols = slice(f * P, f * P + P)
                ops = [(w, a, d) for w, a in ((W1H, XEH), (W1H, XEL), (W1L, XEH)) for d in range(DH)]
                for i, (w, a, d) in enumerate(ops):
                    ins = nc.tensor.matmul(UP[f % 4][:, :], w[:, d, cols], a[k][:, d, :], start=(i == 0), stop=(i == len(ops) - 1))
                ins.then_inc(s["up"], 1)

            def down(f):
                pe.wait_ge(s["h_lo"], 2 + n8 + f + 1)
                pe.wait_ge(s["w2_hi"], NF * e + f + 1)
                pe.wait_ge(s["w2_lo"], NF * e + f + 1)
                for t in range(NS):
                    if f == 0 and t % 2 == 0:
                        pe.wait_ge(s["y_evac"], 4 * e + 2 * k + t // 2 + 1)
                    o = Y[t // 2][:, (t % 2) * D:(t % 2 + 1) * D]
                    rows = slice(t * P, t * P + P)
                    for i, (h, w) in enumerate(((HH, W2H), (HL, W2H), (HH, W2L))):
                        ins = nc.tensor.matmul(o, h[:, f % 4, rows], w[:, f, :], start=(f == 0 and t % 2 == 0 and i == 0),
                                               stop=(f == NF - 1 and i == 2), skip_group_check=True)
                ins.then_inc(s["down"], 1)

            for f in range(NF + 2):
                if f < NF:
                    up(f)
                if f >= 2:
                    down(f - 2)
                if f == 3:
                    if k == 0:
                        xe_pe(pe, s, e, 1)
                    elif not last:
                        xe_pe(pe, s, e + 1, 0)

        def w1_hi(s, f):
            cols = slice(f * P, f * P + P)
            nc.scalar.activation(W1H[:, :, cols], WRAW1[:, :, cols], ACT.Copy).then_inc(s["w1_hi"], 1)

        def w2_hi(s, f):
            nc.scalar.activation(W2H[:, f, :], WRAW2[:, f, :], ACT.Copy).then_inc(s["w2_hi"], 1)

        def block_act(act, s, e, k, last):
            n8 = 2 * NF * e + NF * k
            split_next = k == TOPK - 1 and not last
            if split_next:
                act.wait_ge(s["w_in"], 32 * e + 64)
            for f in range(NF + 3):
                if f < NF:
                    act.wait_ge(s["up"], n8 + f + 1)
                    act.wait_ge(s["h_lo"], n8 + f + 1)
                    nc.scalar.activation(GE[:, f % 2, :], UP[f % 4][:, :], ACT.Gelu_apprx_tanh).then_inc(s["gelu"], 1)
                    if split_next:
                        w1_hi(s, f)
                if f >= 3 and split_next:
                    act.wait_ge(s["down"], 4 + n8 + f - 2)
                    w2_hi(s, f - 3)
                if f == 3:
                    if k == 0:
                        xe_act(act, s, e, 1)
                    elif not last:
                        xe_act(act, s, e + 1, 0)
            act.wait_ge(s["down"], 4 + n8 + NF)
            act.wait_ge(s[f"y_free{k}"], e + 1)
            for i in range(2):
                nc.scalar.activation(YS[k][:, 2 * i:2 * i + 2, :], Y[i][:, :].rearrange("p (t n) -> p t n", t=2),
                                     ACT.Copy).then_inc(s["y_evac"], 1)

        def numbers_dve(dve, s, e, k):
            n = 2 * e + k
            nc.vector.tensor_scalar(VALID[:, :], KC[:, K_ROW:K_ROW + NS], CARRY[:, k, bass.ds(e, 1)], None,
                                    ALU.is_lt).then_inc(s["goal_link"], 1)
            dve.wait_ge(s["goal_link"], 2 * n + 1)
            nc.vector.scalar_tensor_tensor(ROWM[:, k, :], XR[k][:, :, D], -NOWHERE, VALID[:, :], ALU.add,
                                           ALU.mult).then_inc(s["goal_link"], 1)

        def goal_dve(dve, s, e, k):
            dve.wait_ge(s["goal_link"], 2 * (2 * e + k) + 2)
            dve.wait_ge(s[f"y_free{k}"], e + 1)
            nc.vector.tensor_scalar(GOAL[:, k, :], ROWM[:, k, :], NOWHERE + k * TOK, None, ALU.add).then_inc(s["goal"], 1)

        def block_dve(dve, s, e, k, last, beside=None):
            n8 = 2 * NF * e + NF * k
            for f in range(NF):
                dve.wait_ge(s["gelu"], 4 + n8 + f + 1)
                dve.wait_ge(s["down"], n8 + f + 1)
                nc.vector.tensor_copy(HH[:, f % 4, :], GE[:, f % 2, :]).then_inc(s["h_hi"], 1)
                dve.wait_ge(s["h_hi"], n8 + f + 1)
                nc.vector.tensor_tensor(HL[:, f % 4, :], GE[:, f % 2, :], HH[:, f % 4, :].bitcast(F32),
                                        ALU.subtract).then_inc(s["h_lo"], 1)
                if f == 3:
                    if k == 0:
                        xe_dve(dve, s, e, 1)
                        numbers_dve(dve, s, e, 1)
                    elif not last:
                        xe_dve(dve, s, e + 1, 0)
                        numbers_dve(dve, s, e + 1, 0)
                if f == 5:
                    goal_dve(dve, s, e, k)
                if beside:
                    beside(f)

        def split_low(eng, ops, s, e):
            for f in range(NF):
                cols = slice(f * P, f * P + P)
                eng.wait_ge(s["w1_hi"], NF * e + f + 1)
                ops.tensor_tensor(W1L[:, :, cols], WRAW1[:, :, cols], W1H[:, :, cols].bitcast(F32),
                                        ALU.subtract).then_inc(s["w1_lo"], 1)
                eng.wait_ge(s["w2_hi"], NF * e + f + 1)
                ops.tensor_tensor(W2L[:, f, :], WRAW2[:, f, :], W2H[:, f, :].bitcast(F32),
                                        ALU.subtract).then_inc(s["w2_lo"], 1)

        def ffn_pe(pe, ph):
            s = ff[ph]
            xe_pe(pe, s, 0, 0)
            with pe.Fori(0, NE - 1) as e:
                for k in range(TOPK):
                    block_pe(pe, s, e, k, False)
            for k in range(TOPK):
                block_pe(pe, s, NE - 1, k, True)

        def ffn_act(act, ph):
            s = ff[ph]
            act.wait_ge(s["w_in"], 32)
            for f in range(NF):
                w1_hi(s, f)
                w2_hi(s, f)
            xe_act(act, s, 0, 0)
            with act.Fori(0, NE - 1) as e:
                for k in range(TOPK):
                    block_act(act, s, e, k, False)
            for k in range(TOPK):
                block_act(act, s, NE - 1, k, True)

        def ffn_dve(dve, ph):
            s = ff[ph]
            split_low(dve, nc.vector, s, 0)
            xe_dve(dve, s, 0, 0)
            numbers_dve(dve, s, 0, 0)
            with dve.Fori(0, NE - 1) as e:
                for k in range(TOPK):
                    block_dve(dve, s, e, k, False)
            block_dve(dve, s, NE - 1, 0, True)
            block_dve(dve, s, NE - 1, 1, True, beside=(lambda f: first_rows_dve(dve, f)) if ph else None)

        def first_rows_dve(dve, f):
            part = f - 3
            if part < 0:
                return
            b, half = divmod(part, 2)
            if part == 0:
                dve.wait_ge(ff[1]["biased"], NE)
            if half == 0:
                dve.wait_ge(x_in[b], 32)
            add_rows_dve(GF0[b], cb[1], b, 0, range(4 * half, 4 * half + 4))

        def scatter_pool(pool, s, e, k):
            gate(pool, "pool", s["goal"], 2 * e + k + 1)
            gate(pool, "pool", s["y_evac"], 4 + 4 * e + 2 * k)
            for t in range(NS):
                nc.gpsimd.indirect_dma_start(
                    out=yt[:, :], out_offset=bass.IndirectOffsetOnAxis(ap=GOAL[:, k, t:t + 1], axis=0),
                    in_=YS[k][:, t, :], in_offset=None, bounds_check=SLOTS - 1, oob_is_err=False,
                ).then_inc(s[f"y_out{k}"], 16)

        def stored_pool(pool, s, e, k):
            pool.wait_ge(s[f"y_out{k}"], 16 * NS * (e + 1))
            pool.sem_inc(s[f"y_free{k}"], 1)

        def ffn_bias_pool(s, e):
            n = NB * TPB // NE
            rows = X[:, bass.ds(n * e, n), :]
            nc.gpsimd.tensor_tensor(rows, rows, FB[:, :].unsqueeze(1).to_broadcast([P, n, D]), ALU.add).then_inc(s["biased"], 1)

        def ffn_pool(pool, ph):
            s = ff[ph]
            if ph == 0:
                pool.wait_ge(su["y_filled"], Y_FILLED)
            with pool.Fori(0, NE - 1) as e:
                scatter_pool(pool, s, e, 0)
                split_low(pool, nc.gpsimd, s, e + 1)
                stored_pool(pool, s, e, 0)
                scatter_pool(pool, s, e, 1)
                ffn_bias_pool(s, e)
                stored_pool(pool, s, e, 1)
            ffn_bias_pool(s, NE - 1)
            for k in range(TOPK):
                scatter_pool(pool, s, NE - 1, k)

        Y_OUT = 16 * NS * NE

        def y_rows(b, c):
            return yt[bass.ds(c * TOK + b * SEQ, SEQ), :].rearrange("(t p) d -> p t d", p=P)

        def y_sync(sp, b, c):
            if c:
                sp.wait_ge(cb[0]["link"], 2 * b + 1)
            elif not isinstance(b, int) or b:
                sp.wait_ge(cb[0]["link"], 2 * b)
            sp.dma_start(G[:, :, :], y_rows(b, c)).then_inc(cb[0][f"in{c}"], 16)

        def add_rows_dve(src, s, b, c, tiles):
            for t in tiles:
                ins = nc.vector.scalar_tensor_tensor(
                    xb(b, t), src[:, t, 0:D], WP[:, bass.ds(b, 1), c * TPB + t:c * TPB + t + 1].rearrange("p o n -> p (o n)"),
                    xb(b, t), ALU.mult, ALU.add)
            if tiles[-1] == TPB - 1:
                ins.then_inc(s["link"], 1)

        def combine_dve(dve, b, part, second=G):
            c = part // 2
            if part % 2 == 0:
                dve.wait_ge(cb[0][f"in{c}"], 16 * (b + 1))
            if part == 2:
                dve.wait_ge(cb[0]["link"], 2 * b + 1)
            add_rows_dve(second if c else G, cb[0], b, c, range(4 * (part % 2), 4 * (part % 2) + 4))

        MAXB, STB, PVB, AUX, B7 = [bank[0], bank[1], bank[5]], [bank[2], bank[3]], bank[4], bank[6], bank[7]
        QK = [(m, h, c) for h in range(DH) for m in range(2) for c in range(2)]
        PAIR_SWAP = [i ^ 1 for i in range(32)]

        def project(o, lhs, rhs):
            ops = [(a, c, d) for a, c in ((0, 0), (1, 0), (0, 1)) for d in range(DH)]
            for i, (a, c, d) in enumerate(ops):
                ins = nc.tensor.matmul(o, lhs(a, d), rhs(c, d), start=(i == 0), stop=(i == len(ops) - 1))
            return ins

        XT = (XTH, XTL)
        W = (WH, WL)

        def qk_pe(b, i, bk):
            m, h, c = QK[i]
            project(bk[:, :], lambda a, d: W[a][:, m, d, h * P:h * P + P],
                    lambda a, d: XT[a][:, d, c * C:c * C + C]).then_inc(at["qkv"], 1)

        def qk_act(act, b, i, bk):
            m, h, c = QK[i]
            act.wait_ge(at["qkv"], 8 * b + i + 1)
            act.wait_ge(at["cos"], 8 * b + i + 1)
            nc.scalar.activation(QB[:, i % 2, :], bk[:, :], ACT.Identity, bias=BQK[:, m, h:h + 1]).then_inc(at["qb"], 1)

        def qk_dve(dve, b, i):
            m, h, c = QK[i]
            r = QS[:, i % 3, :]
            dve.wait_ge(at["p3"], 8 * b + i + 1)
            gate(dve, "dve", at["qb"], 8 * b + i + 1)
            nc.vector.stream_shuffle(r, QB[:, i % 2, :], PAIR_SWAP).then_inc(at["swap"], 1)
            dve.wait_ge(at["swap"], 8 * b + i + 1)
            nc.vector.tensor_tensor(r, r, ROPE[:, 1, c * C:c * C + C], ALU.mult).then_inc(at["sin"], 1)

        def cos_dve(dve, b, i):
            m, h, c = QK[i]
            dve.wait_ge(at["low"], 8 * b + i + 1)
            nc.vector.tensor_tensor(QC[:, i % 2, :], QB[:, i % 2, :], ROPE[:, 0, c * C:c * C + C], ALU.mult).then_inc(at["cos"], 1)

        def rotate_pool(pool, b, i, cos=True):
            m, h, c = QK[i]
            q = QC[:, i % 2, :]
            if cos:
                pool.wait_ge(at["swap"], 8 * b + i + 1)
                pool.wait_ge(at["low"], 8 * b + i + 1)
                nc.gpsimd.tensor_tensor(q, QB[:, i % 2, :], ROPE[:, 0, c * C:c * C + C], ALU.mult).then_inc(at["cos"], 1)
            pool.wait_ge(at["cos"], 2 + 8 * b + i + 1)
            pool.wait_ge(at["sin"], 8 * b + i + 1)
            nc.gpsimd.tensor_tensor(q, q, QS[:, i % 3, :], ALU.add).then_inc(at["rot"], 1)

        def part1_act(act, b, i):
            act.wait_ge(at["rot"], 8 * b + i + 1)
            if i < 3:
                if not isinstance(b, int) or b:
                    act.wait_ge(at[f"parts_out{i}"], 16 * len(range(i, 8, 3)) * b)
            else:
                act.wait_ge(at[f"parts_out{i % 3}"], 16 * (len(range(i % 3, 8, 3)) * b + i // 3))
            nc.scalar.activation(PT[:, i % 3, 0, :], QC[:, i % 2, :], ACT.Copy).then_inc(at["p1"], 1)

        def low1_dve(dve, b, i):
            dve.wait_ge(at["p1"], 8 * b + i + 1)
            nc.vector.tensor_tensor(QS[:, i % 3, :], QC[:, i % 2, :], PT[:, i % 3, 0, :], ALU.subtract).then_inc(at["low"], 1)

        def part2_act(act, b, i):
            act.wait_ge(at["low"], 2 + 8 * b + i + 1)
            nc.scalar.activation(PT[:, i % 3, 1, :], QS[:, i % 3, :], ACT.Copy).then_inc(at["p2"], 1)

        def part3_pool(pool, b, i):
            pool.wait_ge(at["p2"], 8 * b + i + 1)
            nc.gpsimd.tensor_tensor(PT[:, i % 3, 2, :], QS[:, i % 3, :], PT[:, i % 3, 1, :], ALU.subtract).then_inc(at["p3"], 1)

        def v_pe(b, i, bk):
            for t in range(2):
                ins = project(bk[:, t * D:(t + 1) * D], lambda a, d: XT[a][:, d, (2 * i + t) * P:(2 * i + t + 1) * P],
                              lambda a, d: W[a][:, 2, d, :])
            ins.then_inc(at["v_ps"], 1)

        def v_dve(dve, b, i, bk):
            dve.wait_ge(at["v_ps"], 4 * b + i + 1)
            for t in range(2):
                ins = nc.vector.tensor_tensor(
                    VN[:, 2 * i + t, 0:HEADS * VW].rearrange("p (h d) -> p h d", d=VW)[:, :, 0:HD],
                    bk[:, t * D:(t + 1) * D].rearrange("p (h d) -> p h d", d=HD),
                    BV[:, :].rearrange("p (h d) -> p h d", d=HD), ALU.add)
            ins.then_inc(at["vn"], 1)

        def v_copy_dve(dve, b, prev):
            dve.wait_ge(at["vn"], 4 * b + 4)
            if prev:
                dve.wait_ge(at["pv"], 2 + STEPS * b)
            nc.vector.tensor_copy(V[:, :, :], VN[:, :, :]).then_inc(at["v"], 1)

        def part_sync(sp, b, i):
            m, h, c = QK[i]
            sp.wait_ge(at["p3"], 3 + 8 * b + i + 1)
            sp.dma_start(qkd[bass.ds(b, 1), :, m, h * P:h * P + P, c * C:c * C + C].rearrange("o a p n -> p (o a) n"),
                         PT[:, i % 3, :, :]).then_inc(at[f"parts_out{i % 3}"], 16)

        def parts_sync(sp, b, first, end):
            for i in range(first, end):
                part_sync(sp, b, i)

        STACKED = 16 * 2 * len(Q_PARTS)

        def stack_sync(sp, b, g, half):
            if half == 0 and g in (0, 2):
                for i in range(3):
                    gate(sp, "sp", at[f"parts_out{i}"], 16 * (len(range(i, 8, 3)) * b + len(range(i, 4 if g == 0 else 8, 3))))
            cols = slice(half * C, half * C + C)
            for m, buf, parts in ((0, STQ, Q_PARTS), (1, STK, K_PARTS)):
                for r, part in enumerate(parts):
                    src = qkd[bass.ds(b, 1), part, m, g * GH * HD:(g + 1) * GH * HD, cols]
                    sp.dma_start(buf[g % 2][HD * r:HD * r + HD, :, cols],
                                 src.rearrange("o (h r) n -> r (o h) n", h=GH)).then_inc(at[f"stk_in{g % 2}{half}"], 16)

        def maxrow_sync(sp, b, g):
            u = 4 * b + g
            sp.wait_ge(at["m3"], u + 1)
            sp.dma_start(md.rearrange("a p n -> p a n"), M3[:, :, :]).then_inc(at["m_out"], 16)
            sp.wait_ge(at["m_out"], 16 * u + 16)
            sp.dma_start(STQ[g % 2][STACK:ROWS, :, :], md.rearrange("a (h q) n -> a h (q n)", h=GH)).then_inc(at["m_row"], 16)

        def next_stack_sync(sp, b, g, half, pre):
            if g + 2 >= NG and not pre:
                return
            sp.wait_ge(at["st"], (STEPS * b + NP_ * g + (8 if half == 0 else NP_)) * GH)
            stack_sync(sp, *after(b, g, 2), half)

        def att_sync(sp, b, pre):
            for g in range(NG):
                if pre and g == 0:
                    y_sync(sp, b + 1, 1)
                next_stack_sync(sp, b, g, 0, pre)
                if pre and g == 2:
                    parts_sync(sp, b + 1, 4, 6)
                if g + 1 < NG or pre:
                    maxrow_sync(sp, *after(b, g, 1))
                if pre and g == 1:
                    parts_sync(sp, b + 1, 0, 1)
                if pre and g == 2:
                    parts_sync(sp, b + 1, 6, 7)
                next_stack_sync(sp, b, g, 1, pre)
                if pre and g == 0:
                    y_sync(sp, b + 2, 0)
                if pre and g == 1:
                    parts_sync(sp, b + 1, 1, 4)
                if pre and g == 2:
                    parts_sync(sp, b + 1, 7, 8)

        def after(b, g, n):
            return (b, g + n) if g + n < NG else (b + 1, g + n - NG)

        def max_pieces(b, step, pre):
            g, p = divmod(step, NP_)
            if p > MAX_LAST:
                ahead, p = 2, p - NP_
            else:
                ahead = 1
            if p < MAX_FIRST or g + ahead >= NG and not pre:
                return []
            return [(*after(b, g, ahead), n) for n in range(MAX_UPTO[p - 1], MAX_UPTO[p])]

        def of_head(pieces, h):
            return pieces[len(pieces) * h // GH:len(pieces) * (h + 1) // GH]

        def max_ends(b, step, pre, at_piece):
            g, p = divmod(step, NP_)
            return [after(b, g, 1)] if p == at_piece and (g + 1 < NG or pre) else []

        def max_pe(pe, b, g, n):
            h, q, c, cols = MAXP[n]
            i = (4 * b + g) * MAX_N + n
            if n in (0, MAX_EARLY):
                pe.wait_ge(at[f"stk_in{g % 2}{int(n > 0)}"], (2 * b + g // 2 + 1) * STACKED)
            pe.wait_ge(at["mx_red"], i + 1)
            o = MAXB[n % 3]
            diag = q // 4 == c
            ins = nc.tensor.matmul(o[:, 0:cols], STQ[g % 2][0:STACK, h, q * P:q * P + P], STK[g % 2][0:STACK, h, c * C:c * C + cols],
                                   start=True, stop=not diag)
            if diag:
                ins = nc.tensor.matmul(o[:, cols - P:cols], ID16[:, :], MASK16[:, :], start=False, stop=True)
            ins.then_inc(at["mx_ps"], 1)

        def max_dve(dve, b, g, n):
            h, q, c, cols = MAXP[n]
            i = (4 * b + g) * MAX_N + n
            dve.wait_ge(at["mx_ps"], i + 1)
            if n == 0:
                dve.wait_ge(at["m_done"], 4 * b + g + 1)
            nc.vector.tensor_reduce(MX[:, c, h * TPB + q:h * TPB + q + 1], MAXB[n % 3][:, 0:cols], AX.X, ALU.max).then_inc(at["mx_red"], 1)

        def max_join_dve(dve, b, g):
            u = 4 * b + g
            dve.wait_ge(at["mx_red"], 3 + (u + 1) * MAX_N)
            a, c = (MX[:, i, 0:GH * TPB].rearrange("p (h q) -> p h q", h=GH)[:, :, 4:8] for i in range(2))
            nc.vector.tensor_tensor(a, a, c, ALU.max).then_inc(at["m_link"], 1)

        def b7_use(b, g, what):
            u = NG * b + g
            if what == "m":
                return 0 if isinstance(u, int) and u == 0 else 3 * u - 1
            last = isinstance(u, int) and u == NB * NG - 1
            return 3 * u + 1 + (0 if what == 0 else 1 if last else 2)

        def max_turn_pe(pe, b, g):
            pe.wait_ge(at["m_link"], 4 * b + g + 1)
            pe.wait_ge(at["b7_free"], b7_use(b, g, "m") + 1)
            nc.tensor.transpose(B7[:, 0:P], MX[:, 0, :], ident).then_inc(at["m_done"], 1)

        def max_split_dve(dve, b, g):
            u = 4 * b + g
            dve.wait_ge(at["m_done"], 1 + u + 1)
            if not isinstance(u, int) or u:
                dve.wait_ge(at["m_row"], 16 * u)
            src = B7[0:GH * TPB, 0:P]
            nc.vector.tensor_scalar(M3[:, 0, :], src, -1.0, None, ALU.mult).then_inc(at["m3_link"], 1)
            dve.wait_ge(at["m3_link"], 3 * u + 1)
            nc.vector.scalar_tensor_tensor(MR[:, :], src, -1.0, M3[:, 0, :], ALU.mult, ALU.subtract).then_inc(at["b7_free"], 1)
            dve.wait_ge(at["b7_free"], 1 + b7_use(b, g, "m") + 1)
            nc.vector.tensor_copy(M3[:, 1, :], MR[:, :]).then_inc(at["m3_link"], 1)
            dve.wait_ge(at["m3_link"], 3 * u + 2)
            nc.vector.tensor_tensor(MR[:, :], MR[:, :], M3[:, 1, :], ALU.subtract).then_inc(at["m3_link"], 1)
            dve.wait_ge(at["m3_link"], 3 * u + 3)
            nc.vector.tensor_copy(M3[:, 2, :], MR[:, :]).then_inc(at["m3"], 1)

        def score_pe(pe, b, step, h):
            g, p = divmod(step, NP_)
            c, j, off, cols = PIECES[p]
            if p == 0 and h == 0:
                pe.wait_ge(at["m_row"], 16 * (4 * b + g + 1))
            n = step * GH + h
            pe.wait_ge(at["exp"], STEPS * GH * b + n + 1)
            q0 = c * C + off
            ins = nc.tensor.matmul(STB[n % 2][:, 0:cols], STK[g % 2][0:ROWS, h, j * P:j * P + P],
                                   STQ[g % 2][0:ROWS, h, q0:q0 + cols], start=True, stop=not DIAG[p])
            if DIAG[p]:
                ins = nc.tensor.matmul(STB[n % 2][:, 0:P], MASK16[:, :], ID16[:, :], start=False, stop=True)
            ins.then_inc(at["st"], 1)

        def exp_act(act, b, step, prev):
            g, p = divmod(step, NP_)
            cols = PIECES[p][3]
            act.wait_ge(at["pv"], STEPS * b + step + 1)
            for h in range(GH):
                n = step * GH + h
                act.wait_ge(at["st"], STEPS * GH * b + n + 1)
                nc.scalar.activation(PR[:, n % (2 * GH), 0:cols], STB[n % 2][:, 0:cols], ACT.Exp,
                                     scale=SCORE_SCALE).then_inc(at["exp"], 1)
                if h == 2:
                    for u in outputs(b, step, 1, prev):
                        out_act(act, *u)

        def value_pe(pe, b, step):
            g, p = divmod(step, NP_)
            c, j, off, cols = PIECES[p]
            pe.wait_ge(at["exp"], 2 + STEPS * GH * b + (step + 1) * GH)
            if step == 0:
                pe.wait_ge(at["v"], 1 + b)
            if j == 0:
                pe.wait_ge(at["ot"], 8 * b + 2 * g + c + 2)
            for h in range(GH):
                ins = nc.tensor.matmul(PVB[32 * h:32 * h + 32, off:C], V[:, j, (g * GH + h) * VW:(g * GH + h) * VW + 32],
                                       PR[:, (step * GH + h) % (2 * GH), 0:cols],
                                       start=(j == 0), stop=(j == 4 * c + 3), skip_group_check=True)
            ins.then_inc(at["pv"], 1)

        def outputs(b, step, lag, prev):
            g, p = divmod(step - lag, NP_)
            if g < 0:
                return [(b - 1, NG - 1, 1)] if p == NP_ - 1 and prev else []
            return [(b, g, 0)] if p == 3 and g < NG else [(b, g, 1)] if p == NP_ - 1 and g < NG else []

        def out_act(act, b, g, c):
            u = 8 * b + 2 * g + c
            act.wait_ge(at["pv"], 2 + STEPS * b + NP_ * g + (4 if c == 0 else NP_))
            act.wait_ge(at["b7"], u + 1)
            nc.scalar.activation(OT[:, c, :], PVB[:, :], ACT.Copy).then_inc(at["ot"], 1)

        def out_pe(pe, b, g, c):
            pe.wait_ge(at["ot"], 2 + 8 * b + 2 * g + c + 1)
            pe.wait_ge(at["b7_free"], b7_use(b, g, c) + 1)
            for t in range(4):
                ins = nc.tensor.transpose(B7[:, t * P:t * P + P], OT[:, c, t * P:t * P + P], ident)
            ins.then_inc(at["b7"], 1)

        def out_dve(dve, b, g, c):
            u = 8 * b + 2 * g + c
            dve.wait_ge(at["b7"], 2 + u + 1)
            o = B7[:, :].rearrange("p (t h d) -> p t h d", t=4, h=GH)
            nc.vector.reciprocal(RC[:, :, :], o[:, :, :, HD]).then_inc(at["a_link"], 1)
            dve.wait_ge(at["a_link"], u + 1)
            dst = A[:, 4 * c:4 * c + 4, g * GH * HD:(g + 1) * GH * HD].rearrange("p t (h d) -> p t h d", h=GH)
            nc.vector.tensor_tensor(dst, o[:, :, :, 0:HD], RC[:, :, :].unsqueeze(3).to_broadcast([P, 4, GH, HD]),
                                    ALU.mult).then_inc(at["b7_free"], 1)

        def proj_pe(b, i, bk):
            for t in range(2):
                ins = project(bk[:, t * D:(t + 1) * D], lambda a, d: XT[a][:, d, (2 * i + t) * P:(2 * i + t + 1) * P],
                              lambda a, d: W[a][:, 3, d, :])
            ins.then_inc(pj["out"], 1)

        def proj_dve(dve, b, i, bk):
            dve.wait_ge(pj["out"], 4 * b + i + 1)
            if i == 0:
                dve.wait_ge(at["biased"], b + 1)
            rows = X[:, bass.ds(b * TPB + 2 * i, 2), :]
            nc.vector.tensor_tensor(rows, bk[:, :].rearrange("p (t d) -> p t d", t=2), rows, ALU.add).then_inc(pj["added"], 1)

        def bias_pool(pool, b):
            pool.wait_ge(ln["att"]["xn"], TPB * (b + 1))
            nc.gpsimd.tensor_tensor(xb(b), xb(b), BO[:, :].unsqueeze(1).to_broadcast([P, TPB, D]), ALU.add).then_inc(at["biased"], 1)

        LAST_JOBS = {4 + i: ("turn_out", i) for i in range(4)} | {8 + i: ("proj", i) for i in range(4)} \
            | {33 + i: ("turn_route", i) for i in range(4)} | {37: ("logit", 0), 44: ("rank", 0)}
        NEXT_JOBS = {13 + i: ("turn_qkv", i) for i in range(4)} | {17 + 2 * i: ("qk", i) for i in range(8)} \
            | {18 + 2 * i: ("v", i) for i in range(4)}
        TURNS = {"turn_out": (pj, A), "turn_qkv": (ln["att"], XN), "turn_route": (ln["r1"], XN)}

        def jobs(b, step, prev, pre):
            found = []
            if prev and step in LAST_JOBS:
                found.append((b - 1, *LAST_JOBS[step]))
            if pre and step in NEXT_JOBS:
                found.append((b + 1, *NEXT_JOBS[step]))
            return found

        def released(b, what, i):
            if what in TURNS:
                return TURNS[what][0]["lo"], 2 + 4 * b + i + 1
            return {"proj": (pj["added"], 4 * b + i + 1), "qk": (at["qb"], 8 * b + i + 1), "v": (at["vn"], 4 * b + i + 1),
                    "logit": (rt[1]["lg"], 1 + b), "rank": (rt[1]["rank"], 1 + b)}[what]

        def job_pe(pe, b, what, i, before, bk=AUX):
            if before is not None:
                pe.wait_ge(*released(*before))
            if what in TURNS:
                s, src = TURNS[what]
                if "xn" in s:
                    pe.wait_ge(s["xn"], 2 * i + 2 + TPB * b)
                else:
                    pe.wait_ge(at["b7_free"], 1 + 1 + b7_use(b, NG - 1, 1))
                turn_pe(s, src, i, bk)
            elif what == "proj":
                if i == 0:
                    pe.wait_ge(pj["lo"], 6 + 4 * b)
                proj_pe(b, i, bk)
            elif what == "qk":
                if i == 0:
                    pe.wait_ge(ln["att"]["lo"], 6 + 4 * b)
                qk_pe(b, i, bk)
            elif what == "v":
                v_pe(b, i, bk)
            elif what == "logit":
                pe.wait_ge(ln["r1"]["lo"], 6 + 4 * b)
                logit_pe(rt[1], bk)
            else:
                rank_pe(pe, rt[1], b, bk)

        def job_act(act, b, what, i, bk=AUX):
            if what in TURNS:
                turn_act(act, TURNS[what][0], b, i, bk)
            elif what == "qk":
                qk_act(act, b, i, bk)

        def job_dve(dve, b, what, i, bk=AUX):
            if what in TURNS:
                turn_dve(dve, TURNS[what][0], b, i, bk)
            elif what == "proj":
                proj_dve(dve, b, i, bk)
            elif what == "qk":
                qk_dve(dve, b, i)
            elif what == "v":
                v_dve(dve, b, i, bk)
            elif what == "logit":
                choice_dve(dve, rt[1], b, bk)
            else:
                slot_dve(dve, rt[1], b, bk)

        def side_dve(dve, b, step, prev, pre):
            if pre and step in (0, 1):
                combine_dve(dve, b + 1, step)
            if pre and step in (9, 10):
                combine_dve(dve, b + 1, step - 7)
            if pre and step == 11:
                gate(dve, "dve", cb[0]["link"], 2 * (b + 2))
                stats_dve(dve, ln["att"], b + 1)
            if pre and step == 12:
                if prev:
                    dve.wait_ge(rt[1]["sent"], b)
                norm_dve(dve, ln["att"], b + 1)
            if prev and step == 21:
                gate(dve, "dve", pj["added"], 4 * b)
                stats_dve(dve, ln["r1"], b - 1)
            if prev and step == 24:
                norm_dve(dve, ln["r1"], b - 1, XN, True)
            for n, what, i in jobs(b, step - 4, prev, pre):
                if what == "qk":
                    low1_dve(dve, n, i)

        def groups_pe(pe, b, prev, pre):
            before = None
            for step in range(STEPS):
                pieces = max_pieces(b, step, pre)
                for h in range(GH):
                    score_pe(pe, b, step, h)
                    if h == 0:
                        for u in max_ends(b, step, pre, MAX_LAST + 1):
                            max_turn_pe(pe, *u)
                    if h == 1:
                        if step:
                            value_pe(pe, b, step - 1)
                        elif prev:
                            value_pe(pe, b - 1, STEPS - 1)
                    for piece in of_head(pieces, h):
                        max_pe(pe, *piece)
                for u in outputs(b, step, PE_LAG, prev):
                    out_pe(pe, *u)
                for job in jobs(b, step, prev, pre):
                    job_pe(pe, *job, before)
                    before = job
            if before is not None:
                pe.wait_ge(*released(*before))

        def groups_act(act, b, prev, pre):
            for step in range(STEPS):
                for job in jobs(b, step - 1, prev, pre):
                    job_act(act, *job)
                exp_act(act, b, step, prev)
                for lag, part in ((3, part1_act), (5, part2_act)):
                    for n, what, i in jobs(b, step - lag, prev, pre):
                        if what == "qk":
                            part(act, n, i)
                if prev and step == 39:
                    route_act(act, rt[1], b - 1)

        def groups_dve(dve, b, prev, pre):
            for step in range(STEPS):
                for u in max_ends(b, step, pre, MAX_LAST + 1):
                    max_split_dve(dve, *u)
                pieces = max_pieces(b, step, pre)
                for h in range(GH):
                    for piece in of_head(pieces, h):
                        max_dve(dve, *piece)
                    if h == JOB_AT:
                        for job in jobs(b, step - 1, prev, pre):
                            job_dve(dve, *job)
                    if h == 1 and step == 0:
                        v_copy_dve(dve, b, prev)
                for u in max_ends(b, step, pre, MAX_LAST):
                    max_join_dve(dve, *u)
                for u in outputs(b, step, DVE_LAG, prev):
                    out_dve(dve, *u)
                side_dve(dve, b, step, prev, pre)

        def groups_pool(pool, b, prev, pre):
            for step in range(STEPS):
                for lag, part in ((2, rotate_pool), (6, part3_pool)):
                    for n, what, i in jobs(b, step - lag, prev, pre):
                        if what == "qk":
                            part(pool, n, i)
                if pre and step == 12:
                    norm_pool(pool, ln["att"], b + 1)
                if pre and step == 14:
                    bias_pool(pool, b + 1)
                if prev and step == 22:
                    norm_pool(pool, ln["r1"], b - 1)
                if prev and step == 46:
                    route_pool(pool, rt[1], b - 1)
                if prev and step == STEPS - 1:
                    pool.wait_ge(rt[1]["scattered"], SCATTERED * b)
                    pool.sem_inc(rt[1]["sent"], 1)

        def batches(groups, eng):
            groups(eng, 0, False, True)
            with eng.Fori(1, NB - 1) as b:
                groups(eng, b, True, True)
            groups(eng, NB - 1, True, False)

        PE_LAG, DVE_LAG = 2, 3
        JOB_AT = 0

        def alone(what, n):
            return [(what, i) for i in range(n)]

        BEGIN = [([("turn_qkv", i)], 0) for i in range(4)] + [([("qk", i)], 0) for i in range(4)] \
            + [([("qk", i + 4), ("v", i)], 8 if i == 3 else 0) for i in range(4)]
        BEGIN_ONLY = "turn_qkv", "qk", "v"
        END = alone("turn_out", 4), alone("proj", 4), alone("turn_route", 4), alone("logit", 1), alone("rank", 1)

        def begin(n):
            def qk(n):
                return [i for what, i in BEGIN[n][0] if what == "qk"] if 0 <= n < len(BEGIN) else []
            if n == len(BEGIN):
                return [], range(sum(m for _, m in BEGIN), MAX_N), qk(n - 1)
            done = sum(m for _, m in BEGIN[:n])
            return BEGIN[n][0], range(done, done + BEGIN[n][1]), qk(n - 1)

        ALONE = AUX, PVB

        def place(what, i):
            order = sum([todo for todo, _ in BEGIN], []) if what in BEGIN_ONLY else sum(END, [])
            return ALONE[order.index((what, i)) % 2]

        def run_pe(pe, b, todo, done):
            for job in todo:
                job_pe(pe, b, *job, (b, *done[-2]) if len(done) > 1 else None, place(*job))
                done.append(job)

        def end_pe(pe, b, done):
            for job in done[-2:]:
                pe.wait_ge(*released(b, *job))

        FILLED = 16 * (SLOTS // CAP)
        Y_FILLED = 16 * (SLOTS // SEQ)
        SETUP_DMAS = 16 * 11

        @block.sync
        def _(sp):
            for i, wt in enumerate((wq, wk, wv, wo)):
                sp.dma_start(A[:, 2 * i:2 * i + 2, 0:D], wt.rearrange("(c p) n -> p c n", p=P)).then_inc(su["dma"], 16)
            sp.dma_start(XN[:, 0, 0:DH * NE].rearrange("p (c n) -> p c n", c=DH), router_w.rearrange("(c p) n -> p c n", p=P)).then_inc(su["dma"], 16)
            sp.dma_start(KC[:, :], consts).then_inc(su["dma"], 16)
            for m, v in enumerate((bq, bk)):
                sp.dma_start(BQK[:, m, :], v.rearrange("(c p) -> p c", p=P), allow_slow_non_contiguous=True).then_inc(su["dma"], 16)
            for buf, v in ((BV, bv), (BO, bo), (FB, fbias.rearrange("a b d -> (a b d)"))):
                sp.dma_start(buf[:, :], v.partition_broadcast(P)).then_inc(su["dma"], 16)
            for b in range(NB):
                sp.dma_start(xb(b), batch_tiles[b]).then_inc(x_in[b], 16)
            sp.wait_ge(su["zeros"], 1)
            zeros = G[:, :, :].rearrange("p t d -> p (t d)")
            for i in range(SLOTS // CAP):
                sp.dma_start(xe[i * CAP:(i + 1) * CAP, :].rearrange("(p r) d -> p (r d)", p=P), zeros[:, 0:NS * (D + 1)]).then_inc(su["filled"], 16)
            for i in range(SLOTS // SEQ):
                sp.dma_start(yt[i * SEQ:(i + 1) * SEQ, :].rearrange("(p r) d -> p (r d)", p=P),
                             zeros).then_inc(su["y_filled"], 16)
            sp.wait_ge(su["filled"], FILLED)
            sp.wait_ge(su["y_filled"], Y_FILLED)
            weights_sync(sp, ff[0], 0)
            sp.wait_ge(rt[0]["scattered"], SCATTERED * NB)
            ffn_sync(sp, 0)
            for k in range(TOPK):
                sp.wait_ge(ff[0][f"y_out{k}"], Y_OUT)
            y_sync(sp, 0, 0)
            sp.dma_start(A[:, :, 0:D], y_rows(0, 1)).then_inc(cb[0]["in1"], 16)
            sp.dma_start(ROPE[:, :, :], rope.rearrange("a p n -> p a n")).then_inc(at["rope_in"], 16)
            y_sync(sp, 1, 0)
            for i in range(4):
                part_sync(sp, 0, i)
            for g in range(2):
                for half in range(2):
                    stack_sync(sp, 0, g, half)
                parts_sync(sp, 0, 4 + 2 * g, 6 + 2 * g)
            maxrow_sync(sp, 0, 0)
            att_sync(sp, 0, True)
            with sp.Fori(1, NB - 1) as b:
                att_sync(sp, b, True)
            att_sync(sp, NB - 1, False)
            sp.wait_ge(cb[0]["in0"], 16 * (NB + 1))
            sp.wait_ge(rt[1]["route"], NB)
            weights_sync(sp, ff[1], 0)
            sp.wait_ge(rt[1]["scattered"], SCATTERED * NB)
            ffn_sync(sp, 1)
            for c, rows in enumerate((GF0, GF1)):
                sp.wait_ge(ff[1][f"y_out{c}"], Y_OUT)
                for b in range(NB):
                    sp.dma_start(rows[b][:, :, :], y_rows(b, c)).then_inc(cb[1][f"in{b}"] if c else x_in[b], 16)
            sp.wait_ge(out_done, 16 * NB)

        @block.tensor
        def _(pe):
            pe.wait_ge(su["split"], 6)
            for b in range(NB):
                l = ln["r0"]
                for i in range(4):
                    pe.wait_ge(l["lo"], 1 + i + 4 * b)
                    pe.wait_ge(l["xn"], 2 * i + 2 + TPB * b)
                    turn_pe(l, XNS[b % 2], i, bank[i % 2])
                pe.wait_ge(l["lo"], 6 + 4 * b)
                logit_pe(rt[0], bank[6])
                rank_pe(pe, rt[0], b, bank[7])
            pe.wait_ge(rt[0]["route"], NB)
            ffn_pe(pe, 0)
            pe.wait_ge(at["const"], 1)
            done = []
            for n in range(len(BEGIN) + 1):
                todo, pieces, _ = begin(n)
                run_pe(pe, 0, todo, done)
                for piece in pieces:
                    max_pe(pe, 0, 0, piece)
            end_pe(pe, 0, done)
            max_turn_pe(pe, 0, 0)
            for n in range(MAX_UPTO[-1]):
                max_pe(pe, 0, 1, n)
            batches(groups_pe, pe)
            value_pe(pe, NB - 1, STEPS - 1)
            out_pe(pe, NB - 1, NG - 1, 1)
            done = []
            run_pe(pe, NB - 1, sum(END, []), done)
            end_pe(pe, NB - 1, done)
            pe.wait_ge(rt[1]["route"], NB)
            ffn_pe(pe, 1)

        @block.scalar
        def _(act):
            for s, n in ((ff[0], 4), (ff[1], 4)):
                act.sem_inc(s["gelu"], n)
                act.sem_inc(s["y_evac"], 2)
                act.sem_inc(s["y_free0"], 1)
                act.sem_inc(s["y_free1"], 1)
            act.sem_inc(at["exp"], 2)
            act.sem_inc(at["ot"], 2)
            act.wait_ge(su["dma"], SETUP_DMAS)
            nc.scalar.activation(WH[:, :, :, :].rearrange("p m d n -> p (m d) n"), A[:, :, 0:D], ACT.Copy)
            nc.scalar.activation(RW[:, :, 0:NE], XN[:, 0, 0:DH * NE].rearrange("p (c n) -> p c n", c=DH), ACT.Copy).then_inc(su["act"], 1)
            for b in range(NB):
                for i in range(4):
                    turn_act(act, ln["r0"], b, i, bank[i % 2])
                route_act(act, rt[0], b)
            ffn_act(act, 0)
            for n in range(len(BEGIN) + 1):
                todo, _, last = begin(n)
                for job in todo:
                    job_act(act, 0, *job, place(*job))
                for i in last:
                    part1_act(act, 0, i)
                    part2_act(act, 0, i)
            batches(groups_act, act)
            out_act(act, NB - 1, NG - 1, 1)
            for what, i in sum(END, []):
                job_act(act, NB - 1, what, i, place(what, i))
            route_act(act, rt[1], NB - 1)
            ffn_act(act, 1)
            for b in range(NB):
                act.wait_ge(cb[1]["link"], NB + b + 1)
                act.dma_start(out_tiles[b], xb(b)).then_inc(out_done, 16)

        @block.vector
        def _(dve):
            for l in (*ln.values(), pj):
                dve.sem_inc(l["lo"], 2)
            for s in ff:
                dve.sem_inc(s["xe_lo"], 2)
                dve.sem_inc(s["h_lo"], 2)
            dve.sem_inc(at["mx_red"], 3)
            dve.sem_inc(at["low"], 2)
            dve.sem_inc(at["b7_free"], 1)
            nc.vector.memset(G[:, :, :], 0.0).then_inc(su["zeros"], 1)
            nc.vector.memset(ONES16[:, :], 1.0)
            dve.wait_ge(su["dma"], SETUP_DMAS)
            nc.vector.tensor_scalar(FB[:, :], FB[:, :], 0.5, None, ALU.mult)
            nc.vector.memset(NEGHALF[:, :], -0.5)
            nc.vector.memset(CARRY[:, :, :], 0.0)
            dve.wait_ge(su["act"], 1)
            for i, (dst, col) in enumerate(((ID16, K_ID), (LT16, K_LT), (MASK16, K_MASK))):
                nc.vector.tensor_copy(dst[:, :], KC[:, col:col + P]).then_inc(su["split"], 1)
            nc.vector.tensor_tensor(WL[:, :, :, :].rearrange("p m d n -> p (m d) n"), A[:, :, 0:D],
                                    WH[:, :, :, :].rearrange("p m d n -> p (m d) n").bitcast(F32), ALU.subtract).then_inc(su["split"], 1)
            nc.vector.tensor_tensor(RW[:, :, NE:2 * NE], XN[:, 0, 0:DH * NE].rearrange("p (c n) -> p c n", c=DH),
                                    RW[:, :, 0:NE].bitcast(F32), ALU.subtract).then_inc(su["split"], 2)
            dve.wait_ge(su["split"], 6)
            def route_stats(b):
                dve.wait_ge(x_in[b], 16)
                if b:
                    dve.wait_ge(ln["r0"]["stats"], b)
                stats_dve(dve, ln["r0"], b, b)

            for b in range(2):
                route_stats(b)
                norm_dve(dve, ln["r0"], b, XNS[b], True, b)
            for b in range(NB):
                if b >= 2:
                    dve.wait_ge(rt[0]["sent"], b - 1)
                    norm_dve(dve, ln["r0"], b, XNS[b % 2], True, b)
                for i in range(4):
                    turn_dve(dve, ln["r0"], b, i, bank[i % 2])
                if b + 2 < NB:
                    route_stats(b + 2)
                choice_dve(dve, rt[0], b, bank[6])
                slot_dve(dve, rt[0], b, bank[7], SLTS[b % 2])
            ffn_dve(dve, 0)
            for k in range(TOPK):
                dve.wait_ge(ff[0][f"y_out{k}"], Y_OUT)
            nc.vector.memset(CARRY[:, :, :], 0.0)
            dve.wait_ge(at["rope_in"], 16)
            dve.wait_ge(ff[0]["biased"], NE)
            for part in range(4):
                combine_dve(dve, 0, part, A)
            gate(dve, "dve", cb[0]["link"], 2)
            stats_dve(dve, ln["att"], 0)
            norm_dve(dve, ln["att"], 0)
            dve.wait_ge(at["const"], 4)
            for n in range(len(BEGIN) + 1):
                todo, pieces, last = begin(n)
                for job in todo:
                    job_dve(dve, 0, *job, place(*job))
                    if job[0] == "qk":
                        cos_dve(dve, 0, job[1])
                for i in last:
                    low1_dve(dve, 0, i)
                for piece in pieces:
                    max_dve(dve, 0, 0, piece)
            max_join_dve(dve, 0, 0)
            max_split_dve(dve, 0, 0)
            for n in range(MAX_UPTO[-1]):
                max_dve(dve, 0, 1, n)
            batches(groups_dve, dve)
            out_dve(dve, NB - 1, NG - 1, 1)
            turns, projs, turns2, logit, rank = END
            for what, i in turns + projs:
                job_dve(dve, NB - 1, what, i, place(what, i))
            gate(dve, "dve", pj["added"], 4 * NB)
            stats_dve(dve, ln["r1"], NB - 1)
            dve.wait_ge(rt[1]["sent"], NB)
            norm_dve(dve, ln["r1"], NB - 1, XN, True)
            for what, i in turns2 + logit + rank:
                job_dve(dve, NB - 1, what, i, place(what, i))
            ffn_dve(dve, 1)
            for f in range(NF, 3 + 2 * NB):
                first_rows_dve(dve, f)
            for b in range(NB):
                dve.wait_ge(cb[1][f"in{b}"], 16)
                dve.wait_ge(cb[1]["link"], NB)
                add_rows_dve(GF1[b], cb[1], b, 1, range(TPB))

        @block.gpsimd
        def _(pool):
            pool.sem_inc(at["cos"], 2)
            pool.sem_inc(at["p3"], 3)
            pool.sem_inc(rt[1]["sent"], 1)
            pool.sem_inc(at["pv"], 2)
            pool.sem_inc(at["m_done"], 1)
            pool.sem_inc(at["b7"], 2)
            for s in ff:
                pool.sem_inc(s["down"], 4)
            pool.wait_ge(su["split"], 6)

            def route_norm(b):
                if b:
                    pool.wait_ge(ln["r0"]["rstd"], b)
                norm_pool(pool, ln["r0"], b, b)

            for b in range(3):
                route_norm(b)
            for b in range(NB):
                pool.wait_ge(su["filled"], FILLED)
                route_pool(pool, rt[0], b, XNS[b % 2], SLTS[b % 2])
                if b == 0:
                    route_norm(3)
                if b + 2 < NB:
                    pool.wait_ge(rt[0]["scattered"], SCATTERED * (b + 1))
                    pool.sem_inc(rt[0]["sent"], 1)
            ffn_pool(pool, 0)
            for k in range(TOPK):
                pool.wait_ge(ff[0][f"y_out{k}"], Y_OUT)
            nc.gpsimd.memset(VN[:, :, :], 0.0).then_inc(at["const"], 1)
            pool.wait_ge(at["const"], 1)
            nc.gpsimd.memset(VN[:, :, 0:HEADS * VW].rearrange("p t (h d) -> p t h d", d=VW)[:, :, :, HD:VW], 1.0)
            nc.gpsimd.memset(MX[:, :, :], 0.0).then_inc(at["const"], 1)
            norm_pool(pool, ln["att"], 0)
            pool.wait_ge(ln["att"]["rstd"], 1)
            nc.gpsimd.memset(STK[0][STACK:ROWS, :, :], 1.0).then_inc(at["const"], 1)
            pool.wait_ge(at["const"], 3)
            nc.gpsimd.memset(STK[1][STACK:ROWS, :, :], 1.0).then_inc(at["const"], 1)
            pool.wait_ge(at["const"], 4)
            for n in range(len(BEGIN) + 1):
                todo, _, last = begin(n)
                for what, i in todo:
                    if what == "qk":
                        rotate_pool(pool, 0, i, cos=False)
                for i in last:
                    part3_pool(pool, 0, i)
            bias_pool(pool, 0)
            batches(groups_pool, pool)
            norm_pool(pool, ln["r1"], NB - 1)
            route_pool(pool, rt[1], NB - 1)
            ffn_pool(pool, 1)


_INS = ["L0_attn_x", "L0_attn_wq", "L0_attn_bq", "L0_attn_wk", "L0_attn_bk", "L0_attn_wv", "L0_attn_bv",
        "L0_attn_wo", "L0_attn_bo", "L0_ffn_router_w", "L0_ffn_w1", "L0_ffn_w2", "L0_ffn_bias"]


def kernel(**inputs):
    import numpy as _np
    import concourse.bacc as _bacc
    from concourse import mybir as _mybir
    from concourse.bass_utils import run_bass_kernel_spmd as _run

    nc = _bacc.Bacc("TRN2", target_bir_lowering=False, num_devices=1)
    arrays, args = {}, []
    given = {name: _np.ascontiguousarray(inputs[name]) for name in _INS}
    given["shape_constants"] = shape_constants()
    given["rope_tables"] = rope_tables()
    for name, a in given.items():
        arrays[f"in_{name}_dram"] = a
        args.append(nc.dram_tensor(f"in_{name}_dram", a.shape, _mybir.dt.from_np(a.dtype), kind="ExternalInput").ap())
    args.append(nc.dram_tensor("out_0_dram", (NB, SEQ, D), _mybir.dt.float32, kind="ExternalOutput").ap())
    build(nc, *args)
    r = _run(nc, [arrays], core_ids=[0])
    return r.results[0]["out_0_dram"]
```
